# Optimizing a Trainium2 kernel written in Bass

```python
import numpy as np
import jax
import jax.numpy as jnp

def _softmax(x, axis=-1):
    return jax.nn.softmax(x, axis=axis)

def _gelu(x):
    return jax.nn.gelu(x, approximate=True)

def _silu(x):
    return jax.nn.silu(x)

def _sigmoid(x):
    return jax.nn.sigmoid(x)

def _layernorm(x, axis=-1, eps=1e-05):
    m = jnp.mean(x, axis=axis, keepdims=True)
    v = jnp.var(x, axis=axis, keepdims=True)
    return (x - m) / jnp.sqrt(v + eps)

def _scatter_add(tgt, idx, src, axis=0):
    return tgt.at[idx].add(src)

def _segment_sum(src, seg, n):
    return jax.ops.segment_sum(src, seg, n)
kernel_name = 'mk_gnn_preln_d4_gnn_r64_d4baaf'

def setup_inputs(seed: int=0):
    np.random.seed(seed)
    _w = jnp.asarray

    def _rec_inputs():
        import jax
        import jax.numpy as jnp
        _gk = jax.random.key(seed)
        x = -0.000202 + 1 * jax.random.normal(jax.random.fold_in(_gk, 1), (50000, 128), jnp.float32)
        src = jax.random.randint(jax.random.fold_in(_gk, 2), (12500,), 0, 50000, jnp.int32)
        dst = jnp.minimum((50000 * jax.random.uniform(jax.random.fold_in(_gk, 3), (12500,)) ** 2.0).astype(jnp.int32), 49999)
        _o = jnp.argsort(dst, stable=True)
        src = src[_o]
        dst = dst[_o]
        edge_weight = 6.14103e-05 + 0.0999867 * jax.random.normal(jax.random.fold_in(_gk, 12), (12500,), jnp.float32)
        return (x, src, dst, edge_weight)
    x, src, dst, edge_weight = _rec_inputs()

    def _L0_gnn_setup():
        import jax, jax.numpy as jnp
        import numpy as np
        N = 50000
        E = 12500
        C = 128
        H = 8
        HD = C // H
        key = jax.random.key(seed)
        ks = jax.random.split(key, 8)
        s = 1.0 / np.sqrt(C)
        x = jax.random.normal(ks[0], (N, C), jnp.float32)
        edge_index = jax.random.randint(ks[1], (2, E), 0, N, jnp.int32)
        edge_weight = jax.random.normal(ks[2], (E,), jnp.float32) * 0.1
        Wq = jax.random.normal(ks[3], (C, C), jnp.float32) * s
        Wk = jax.random.normal(ks[4], (C, C), jnp.float32) * s
        Wv = jax.random.normal(ks[5], (C, C), jnp.float32) * s
        Wd = jax.random.normal(ks[6], (H, 1), jnp.float32)
        Wo = jax.random.normal(ks[7], (C, C), jnp.float32) * s
        return {'x': x, 'edge_index': edge_index, 'edge_weight': edge_weight, 'Wq': Wq, 'bq': jnp.zeros((C,), jnp.float32), 'Wk': Wk, 'bk': jnp.zeros((C,), jnp.float32), 'Wv': Wv, 'bv': jnp.zeros((C,), jnp.float32), 'Wd': Wd, 'bd': jnp.zeros((H,), jnp.float32), 'Wo': Wo, 'bo': jnp.zeros((C,), jnp.float32)}
    _L0_gnn_all = _L0_gnn_setup()
    _L0_gnn_in = {k: v for k, v in _L0_gnn_all.items() if k in ('Wq', 'bq', 'Wk', 'bk', 'Wv', 'bv', 'Wd', 'bd', 'Wo', 'bo')}
    del _L0_gnn_all

    def _L1_gnn_setup():
        import jax, jax.numpy as jnp
        import numpy as np
        N_NODES = 50000
        N_EDGES = 12500
        D = 128

        def _mlp(h, W1, b1, W2, b2):
            return jax.nn.relu(h @ W1 + b1) @ W2 + b2
        key = jax.random.key(seed)
        ks = jax.random.split(key, 6)
        s = 0.05
        x = jax.random.normal(ks[0], (N_NODES, D), dtype=jnp.float32)
        edge_index = jax.random.randint(ks[1], (2, N_EDGES), 0, N_NODES, dtype=jnp.int64)
        We1 = jax.random.normal(ks[2], (2 * D, D), dtype=jnp.float32) * s
        be1 = jnp.zeros((D,), dtype=jnp.float32)
        We2 = jax.random.normal(ks[3], (D, D), dtype=jnp.float32) * s
        be2 = jnp.zeros((D,), dtype=jnp.float32)
        Wn1 = jax.random.normal(ks[4], (2 * D, D), dtype=jnp.float32) * s
        bn1 = jnp.zeros((D,), dtype=jnp.float32)
        Wn2 = jax.random.normal(ks[5], (D, D), dtype=jnp.float32) * s
        bn2 = jnp.zeros((D,), dtype=jnp.float32)
        return {'x': x, 'edge_index': edge_index, 'We1': We1, 'be1': be1, 'We2': We2, 'be2': be2, 'Wn1': Wn1, 'bn1': bn1, 'Wn2': Wn2, 'bn2': bn2}
    _L1_gnn_all = _L1_gnn_setup()
    _L1_gnn_in = {k: v for k, v in _L1_gnn_all.items() if k in ('We1', 'be1', 'We2', 'be2', 'Wn1', 'bn1', 'Wn2', 'bn2')}
    del _L1_gnn_all

    def _L2_gnn_setup():
        import jax, jax.numpy as jnp
        import numpy as np
        N = 100000
        E = 25000
        D_IN = 128
        D_OUT = 128
        EPS_GIN = 0.0
        LN_EPS = 1e-05
        PROJ_EPS = 1e-09

        def _aggregate(x, edge_index, edge_weight):
            src = edge_index[0]
            tgt = edge_index[1]
            n = x.shape[0]
            m = jax.ops.segment_max(edge_weight, tgt, num_segments=n)
            ew = jnp.exp(edge_weight - m[tgt])
            denom = jax.ops.segment_sum(ew, tgt, num_segments=n)
            w = ew / denom[tgt]
            msg = w[:, None] * x[src]
            agg = jax.ops.segment_sum(msg, tgt, num_segments=n)
            norm = jnp.linalg.norm(agg, axis=-1, keepdims=True)
            return agg / (norm + PROJ_EPS)

        def _layer_norm(h, gamma, beta):
            mu = jnp.mean(h, axis=-1, keepdims=True)
            var = jnp.var(h, axis=-1, keepdims=True)
            return gamma * (h - mu) * jax.lax.rsqrt(var + LN_EPS) + beta
        key = jax.random.key(seed)
        ks = jax.random.split(key, 9)
        x = jax.random.normal(ks[0], (N, D_IN), dtype=jnp.float32)
        edge_index = jax.random.randint(ks[1], (2, E), 0, N, dtype=jnp.int64)
        edge_weight = jax.random.normal(ks[2], (E,), dtype=jnp.float32)
        s1 = 1.0 / np.sqrt(D_IN)
        s2 = 1.0 / np.sqrt(D_OUT)
        W1 = jax.random.uniform(ks[3], (D_IN, D_OUT), jnp.float32, -s1, s1)
        b1 = jax.random.uniform(ks[4], (D_OUT,), jnp.float32, -s1, s1)
        W2 = jax.random.uniform(ks[5], (D_OUT, D_OUT), jnp.float32, -s2, s2)
        b2 = jax.random.uniform(ks[6], (D_OUT,), jnp.float32, -s2, s2)
        gamma = jnp.ones((D_OUT,), jnp.float32)
        beta = jnp.zeros((D_OUT,), jnp.float32)
        return {'x': x, 'edge_index': edge_index, 'edge_weight': edge_weight, 'W1': W1, 'b1': b1, 'W2': W2, 'b2': b2, 'gamma': gamma, 'beta': beta}
    _L2_gnn_all = _L2_gnn_setup()
    _L2_gnn_in = {k: v for k, v in _L2_gnn_all.items() if k in ('W1', 'b1', 'W2', 'b2', 'gamma', 'beta')}
    del _L2_gnn_all

    def _L3_gnn_setup():
        import jax, jax.numpy as jnp
        import numpy as np
        N_NODES = 10000
        key = jax.random.key(seed)
        k1, k2, k3 = jax.random.split(key, 3)
        N, E, D, D_OUT = (N_NODES, 10000, 128, 128)
        x = jax.random.normal(k1, (N, D), dtype=jnp.float32)
        edge_index = jax.random.randint(k2, (2, E), 0, N, dtype=jnp.int64)
        limit = float(np.sqrt(6.0 / (2 * D + D_OUT)))
        W_out = jax.random.uniform(k3, (D_OUT, 2 * D), dtype=jnp.float32, minval=-limit, maxval=limit)
        b_out = jnp.zeros((D_OUT,), dtype=jnp.float32)
        return {'x': x, 'edge_index': edge_index, 'W_out': W_out, 'b_out': b_out}
    _L3_gnn_all = _L3_gnn_setup()
    _L3_gnn_in = {k: v for k, v in _L3_gnn_all.items() if k in ('W_out', 'b_out')}
    del _L3_gnn_all
    return {'x': x, 'src': src, 'dst': dst, 'edge_weight': edge_weight, 'L0_gnn_Wq': _L0_gnn_in['Wq'], 'L0_gnn_bq': _L0_gnn_in['bq'], 'L0_gnn_Wk': _L0_gnn_in['Wk'], 'L0_gnn_bk': _L0_gnn_in['bk'], 'L0_gnn_Wv': _L0_gnn_in['Wv'], 'L0_gnn_bv': _L0_gnn_in['bv'], 'L0_gnn_Wd': _L0_gnn_in['Wd'], 'L0_gnn_bd': _L0_gnn_in['bd'], 'L0_gnn_Wo': _L0_gnn_in['Wo'], 'L0_gnn_bo': _L0_gnn_in['bo'], 'L1_gnn_We1': _L1_gnn_in['We1'], 'L1_gnn_be1': _L1_gnn_in['be1'], 'L1_gnn_We2': _L1_gnn_in['We2'], 'L1_gnn_be2': _L1_gnn_in['be2'], 'L1_gnn_Wn1': _L1_gnn_in['Wn1'], 'L1_gnn_bn1': _L1_gnn_in['bn1'], 'L1_gnn_Wn2': _L1_gnn_in['Wn2'], 'L1_gnn_bn2': _L1_gnn_in['bn2'], 'L2_gnn_W1': _L2_gnn_in['W1'], 'L2_gnn_b1': _L2_gnn_in['b1'], 'L2_gnn_W2': _L2_gnn_in['W2'], 'L2_gnn_b2': _L2_gnn_in['b2'], 'L2_gnn_gamma': _L2_gnn_in['gamma'], 'L2_gnn_beta': _L2_gnn_in['beta'], 'L3_gnn_W_out': _L3_gnn_in['W_out'], 'L3_gnn_b_out': _L3_gnn_in['b_out']}

def reference(x, src, dst, edge_weight, L0_gnn_Wq, L0_gnn_bq, L0_gnn_Wk, L0_gnn_bk, L0_gnn_Wv, L0_gnn_bv, L0_gnn_Wd, L0_gnn_bd, L0_gnn_Wo, L0_gnn_bo, L1_gnn_We1, L1_gnn_be1, L1_gnn_We2, L1_gnn_be2, L1_gnn_Wn1, L1_gnn_bn1, L1_gnn_Wn2, L1_gnn_bn2, L2_gnn_W1, L2_gnn_b1, L2_gnn_W2, L2_gnn_b2, L2_gnn_gamma, L2_gnn_beta, L3_gnn_W_out, L3_gnn_b_out):
    import jax
    import jax.numpy as jnp

    def _L0_gnn_ref(x, edge_index, edge_weight, Wq, bq, Wk, bk, Wv, bv, Wd, bd, Wo, bo):
        import jax, jax.numpy as jnp
        import numpy as np
        N = 50000
        E = 12500
        C = 128
        H = 8
        HD = C // H
        row, col = (edge_index[0], edge_index[1])
        n = x.shape[0]
        q = (x @ Wq.T + bq).reshape(n, H, HD)
        k = (x @ Wk.T + bk).reshape(n, H, HD)
        v = (x @ Wv.T + bv).reshape(n, H, HD)
        scores = jnp.einsum('ehd,ehd->eh', q[row], k[col]) / np.sqrt(HD)
        scores = scores + edge_weight[:, None]
        dmean = jnp.mean(x[col] - x[row], axis=-1, keepdims=True)
        scores = scores + dmean @ Wd.T + bd
        attn = jax.nn.softmax(scores, axis=0)
        msgs = (v[col] * attn[:, :, None]).reshape(-1, H * HD)
        out = jnp.zeros((n, H * HD), x.dtype).at[row].add(msgs)
        return out @ Wo.T + bo

    def _L1_gnn_ref(x, edge_index, We1, be1, We2, be2, Wn1, bn1, Wn2, bn2):
        import jax, jax.numpy as jnp
        import numpy as np
        N_NODES = 50000
        N_EDGES = 12500
        D = 128

        def _mlp(h, W1, b1, W2, b2):
            return jax.nn.relu(h @ W1 + b1) @ W2 + b2
        src = edge_index[0]
        dst = edge_index[1]
        e_in = jnp.concatenate([x[src], x[dst]], axis=-1)
        edge_new = _mlp(e_in, We1, be1, We2, be2)
        agg = jax.ops.segment_sum(edge_new, dst, num_segments=x.shape[0])
        mesh_new = _mlp(jnp.concatenate([x, agg], axis=-1), Wn1, bn1, Wn2, bn2)
        return x + mesh_new

    def _L2_gnn_ref(x, edge_index, edge_weight, W1, b1, W2, b2, gamma, beta):
        import jax, jax.numpy as jnp
        import numpy as np
        N = 100000
        E = 25000
        D_IN = 128
        D_OUT = 128
        EPS_GIN = 0.0
        LN_EPS = 1e-05
        PROJ_EPS = 1e-09

        def _aggregate(x, edge_index, edge_weight):
            src = edge_index[0]
            tgt = edge_index[1]
            n = x.shape[0]
            m = jax.ops.segment_max(edge_weight, tgt, num_segments=n)
            ew = jnp.exp(edge_weight - m[tgt])
            denom = jax.ops.segment_sum(ew, tgt, num_segments=n)
            w = ew / denom[tgt]
            msg = w[:, None] * x[src]
            agg = jax.ops.segment_sum(msg, tgt, num_segments=n)
            norm = jnp.linalg.norm(agg, axis=-1, keepdims=True)
            return agg / (norm + PROJ_EPS)

        def _layer_norm(h, gamma, beta):
            mu = jnp.mean(h, axis=-1, keepdims=True)
            var = jnp.var(h, axis=-1, keepdims=True)
            return gamma * (h - mu) * jax.lax.rsqrt(var + LN_EPS) + beta
        neigh = _aggregate(x, edge_index, edge_weight)
        combined = (1.0 + EPS_GIN) * x + neigh
        h = jnp.maximum(combined @ W1 + b1, 0.0)
        h = h @ W2 + b2
        h = _layer_norm(h, gamma, beta)
        return h

    def _L3_gnn_ref(x, edge_index, W_out, b_out):
        import jax, jax.numpy as jnp
        import numpy as np
        N_NODES = 10000
        row, col = (edge_index[0], edge_index[1])
        N = x.shape[0]
        neigh_sum = jax.ops.segment_sum(x[row], col, num_segments=N)
        count = jax.ops.segment_sum(jnp.ones_like(col, dtype=x.dtype), col, num_segments=N)
        out = neigh_sum / jnp.clip(count, 1.0)[:, None]
        h = jnp.concatenate([x, out], axis=-1)
        return h @ W_out.T + b_out
    edge_index = jnp.stack([src, dst])
    h = jnp.maximum(_layernorm(x, axis=-1), 0.0)
    x = x + _L0_gnn_ref(h, edge_index, edge_weight, L0_gnn_Wq, L0_gnn_bq, L0_gnn_Wk, L0_gnn_bk, L0_gnn_Wv, L0_gnn_bv, L0_gnn_Wd, L0_gnn_bd, L0_gnn_Wo, L0_gnn_bo)
    h = jnp.maximum(_layernorm(x, axis=-1), 0.0)
    x = x + _L1_gnn_ref(h, edge_index, L1_gnn_We1, L1_gnn_be1, L1_gnn_We2, L1_gnn_be2, L1_gnn_Wn1, L1_gnn_bn1, L1_gnn_Wn2, L1_gnn_bn2)
    h = jnp.maximum(_layernorm(x, axis=-1), 0.0)
    x = x + _L2_gnn_ref(h, edge_index, edge_weight, L2_gnn_W1, L2_gnn_b1, L2_gnn_W2, L2_gnn_b2, L2_gnn_gamma, L2_gnn_beta)
    h = jnp.maximum(_layernorm(x, axis=-1), 0.0)
    x = x + _L3_gnn_ref(h, edge_index, L3_gnn_W_out, L3_gnn_b_out)
    return x

_drawn_inputs = setup_inputs


def setup_inputs(seed=0):
    import zlib

    import numpy as np

    out = dict(_drawn_inputs(seed))
    spreads = {'L0_gnn_bq': (0.0, 2.0),
     'L0_gnn_bk': (0.0, 0.8),
     'L0_gnn_bv': (0.0, 2.0),
     'L0_gnn_bd': (0.0, 0.8),
     'L0_gnn_bo': (0.0, 0.1),
     'L1_gnn_be1': (0.0, 0.8),
     'L1_gnn_be2': (0.0, 0.8),
     'L1_gnn_bn1': (0.0, 0.354),
     'L1_gnn_bn2': (0.0, 0.1),
     'L2_gnn_gamma': (1.0, 0.2),
     'L2_gnn_beta': (0.0, 0.1),
     'L3_gnn_b_out': (0.0, 0.1)}
    factors = {'edge_weight': 64.0,
     'L0_gnn_Wq': 8.0,
     'L0_gnn_Wk': 8.0,
     'L0_gnn_Wv': 8.0,
     'L0_gnn_Wd': 200.0,
     'L0_gnn_Wo': 8.0,
     'L1_gnn_We1': 4.505,
     'L1_gnn_We2': 3.707}
    for name, (base, spread) in spreads.items():
        noise = np.random.default_rng([zlib.crc32(name.encode()), seed]).standard_normal(out[name].shape)
        drawn = base * np.exp(spread * noise) if base else spread * noise
        out[name] = jnp.asarray(drawn.astype(out[name].dtype))
    for name, factor in factors.items():
        out[name] = (out[name] * factor).astype(out[name].dtype)
    return out
```

```python
import concourse.bass as bass
from concourse import mybir
from contextlib import ExitStack

P = 128
U = 4
LN_EPS = 1e-5
PROJ_EPS = 1e-9
FAR = 3.0e38
ABSENT = 2.0 ** 127


class Phase(dict):

    def __init__(self, sems):
        super().__init__(sems)
        self.start = {}

    def due(self, name, n):
        return n + self.start.get(name, 0)


class Chain:

    def __init__(self, engine, sem, per):
        self.engine, self.sem, self.per, self.n, self.base = engine, sem, per, 0, 0

    def step(self, g):
        self.base, self.n = g * self.per, 0

    def __call__(self, ins):
        self.n += 1
        ins.then_inc(self.sem, 1)
        self.engine.wait_ge(self.sem, self.base + self.n)

    def end(self):
        assert self.n == self.per, f"chain of {self.n}, not {self.per}"


def build_gnn(nc, x, src, dst, edge_weight, WqT, bq, WkT, bk, WvT, bv, Wd, bd, WoT, bo,
              We1, be1, We2, be2, Wn1, bn1, Wn2, bn2, W1, b1, W2, b2, gamma, beta, WoutT, b_out, out):
    f32, bf16, i32 = mybir.dt.float32, mybir.dt.bfloat16, mybir.dt.int32
    ALU, ACT, AX = mybir.AluOpType, mybir.ActivationFunctionType, mybir.AxisListType
    ds = bass.ds

    N, C = x.shape
    E = src.shape[0]
    H = bd.shape[0]
    HD = C // H
    EP = max(p for p in range(1, P + 1) if E % p == 0 and (E // p) % U == 0)
    CH = E // EP
    G = CH // U
    TF = (N + P + P - 1) // P
    NT = TF * P
    ROWS = P * U
    NG = 2 * ((N + 2 * ROWS - 1) // (2 * ROWS))
    bases = [min(g * ROWS, N - ROWS) for g in range(NG)]
    assert all(b == g * ROWS for g, b in enumerate(bases[:-2]))
    SCALE = 1.0 / HD ** 0.5
    AW = C + 2
    ZR = next(z for z in (28, 4, 2, 1) if TF % z == 0)
    KV, QW = 2 * C + H, C + H

    ctx = ExitStack()
    with ctx:
        def sb(name, shape, dt=f32):
            return ctx.enter_context(nc.sbuf_tensor(name, shape, dt))

        def sem(name):
            return ctx.enter_context(nc.semaphore(name))

        S0 = nc.dram_tensor("sum_attention", (NT, C), f32, kind="Internal").ap()
        S1 = nc.dram_tensor("sum_edge_mlp", (NT, C), f32, kind="Internal").ap()
        S2 = nc.dram_tensor("sum_weighted", (NT, AW), f32, kind="Internal").ap()
        S3 = nc.dram_tensor("sum_mean", (NT, C), f32, kind="Internal").ap()

        ident = sb("ident", [P, P])
        ones = sb("ones", [P, P])
        ones16 = sb("ones16", [1, P], bf16)
        ltri = sb("ltri", [P, P])
        iota_f = sb("iota_f", [P, max(TF, P)])
        iota_p = sb("iota_p", [P, 1])
        trash = sb("trash", [P, 1])
        not_edge = sb("not_edge", [P, 1])
        eps = sb("eps", [P, 1])
        far_row = sb("far_row", [1, TF], bf16)
        zeros = sb("zeros", [P, AW])

        srcI = sb("srcI", [P, CH + U], i32)
        dstI = sb("dstI", [P, CH + U], i32)
        keyS = sb("keyS", [P, CH])
        keyD = sb("keyD", [P, CH])
        keyp = sb("keyp", [P, CH])
        keyf = sb("keyf", [P, CH])
        ew = sb("ew", [P, CH])
        rankD = sb("rankD", [P, CH])
        idxD = sb("idxD", [P, CH], i32)
        segmax = sb("segmax", [P, CH])
        wexp = sb("wexp", [P, CH])
        tmpc = sb("tmpc", [P, CH])
        keyI = idxD[:, :]
        pI, fI = tmpc[:, :].bitcast(i32), wexp[:, :].bitcast(i32)
        table = sb("table", [P, TF])
        scores = sb("scores", [P, CH, H])
        hmax = sb("hmax", [P, H])
        hall = sb("hall", [P, H])
        hsum = sb("hsum", [P, H])
        hrec = sb("hrec", [P, H])

        wkv = sb("wkv", [P, KV])
        wq = sb("wq", [P, QW])
        wo = sb("wo", [P, C])
        we1 = sb("we1", [P, 2, C])
        we2 = sb("we2", [P, C])
        wn1 = sb("wn1", [P, 2, C])
        wn2 = sb("wn2", [P, C])
        w1 = sb("w1", [P, C])
        w2 = sb("w2", [P, C])
        wout = sb("wout", [P, 2, C])
        wdb = sb("wdb", [P, H])
        kvq_row = sb("kvq_row", [1, KV + QW])
        be2_row = sb("be2_row", [1, C])
        b2_row = sb("b2_row", [1, C])
        bout_row = sb("bout_row", [1, C])
        be1c = sb("be1c", [P, 1])
        bn1c = sb("bn1c", [P, 1])
        b1c = sb("b1c", [P, 1])
        bo_b = sb("bo_b", [P, C])
        bn2_b = sb("bn2_b", [P, C])
        gamma_b = sb("gamma_b", [P, C])
        beta_b = sb("beta_b", [P, C])

        RS = sb("rows_src", [P, CH, C])
        RD = sb("rows_dst", [P, CH, C])
        RV = sb("rows_val", [P, CH, C])

        gA = sb("gA", [P, U, AW])
        gB = sb("gB", [P, U, AW])
        ibS = sb("ibS", [P, U], i32)
        ibD = sb("ibD", [P, U], i32)
        ibO = sb("ibO", [P, U], i32)
        dgA = sb("dgA", [P, U, P])
        dgB = sb("dgB", [P, U, P])
        sel = sb("sel", [P, U, P])
        wA = sb("wA", [P, U, C])
        wB = sb("wB", [P, U, C])
        hTA = sb("hTA", [P, U, P])
        hTB = sb("hTB", [P, U, P])
        y = sb("y", [P, U, AW])
        msg = gB
        qsb = sb("qsb", [P, 2, QW])
        sct = sb("sct", [P, U, H])
        red = sb("red", [P, U, H])
        oh = sb("oh", [P, U, P])
        oh16 = sb("oh16", [P, U, P], bf16)
        ohv = sb("ohv", [P, 2, TF])
        ohb = sb("ohb", [P, 2, TF], bf16)
        st = sb("st", [P, 2 * U, 6])
        mv = sb("mv", [P, 2 * U, 6])
        sd = sb("sd", [P, 2 * U])
        rs = sb("rs", [P, 2 * U])
        st2 = sb("st2", [P, U, 6])
        mv2 = sb("mv2", [P, U, 6])
        sd2 = sb("sd2", [P, U])
        rs2 = sb("rs2", [P, U])
        rk = sb("rk", [P, U])
        fr = sb("fr", [P, U])
        ml = sb("ml", [P, U])
        tk = sb("tk", [P, U])
        sq = sb("sq", [P, U])
        nr = sb("nr", [P, U])
        dn = sb("dn", [P, U])
        rr = sb("rr", [P, U])
        sqB = sb("sqB", [P, U])
        nrB = sb("nrB", [P, U])
        dnB = sb("dnB", [P, U])
        rrB = sb("rrB", [P, U])

        pb = ctx.enter_context(nc.psum_tensor("pb", [P, 8, 512], f32))

        def bank(b):
            return pb[:, b, :].rearrange("p (u c) -> p u c", u=U)

        def over_rows(row):
            return row.unsqueeze(1).broadcast_to([P, U, C])

        def over_cols(col, n=P):
            return col.unsqueeze(2).broadcast_to([P, U, n])

        s_loaded = sem("loaded")
        s_pool_const = sem("pool_const")
        s_vec_const = sem("vec_const")
        s_pool_chain = sem("pool_chain")
        s_zero = [sem(f"zeroed{i}") for i in range(4)]
        s_hold = sem("pool_held")
        s_vhold = sem("vector_held")

        shared = {n: sem(n) for n in ("idx gathered_s gathered_d taken diag bcast sel msgs mT mTs y ysb scat yfree "
                                      "oidx var sd hid hids").split()}
        ended = dict.fromkeys(shared, 0)

        def phase_sems(ph, names, share=""):
            p = Phase({n: sem(f"{ph}_{n}") for n in names.split()})
            for n in share.split():
                p[n], p.start[n] = shared[n], ended[n]
                ended[n] += G + (n in ("idx", "taken", "yfree")) if not n.startswith("gathered") and n != "scat" else 16 * U * G
            return p

        p0 = phase_sems("p0", "idx gathered_s gathered_d taken diag bcast xn xT hT kvq copied prod var sd oh tab tabmax chain")
        sm = phase_sems("sm", "hmax allmax shifted exp hsum allsum done chain")
        l0 = phase_sems("l0", "look looked chain", "diag bcast sel msgs mT mTs y ysb scat yfree oidx")
        wx = phase_sems("wx", "shifted exp chain chain2 chain3")
        l1 = phase_sems("l1", "xn xT hT en ens chain", "idx gathered_s gathered_d taken diag bcast sel hid hids "
                        "mT mTs y ysb scat yfree oidx var sd")
        l2 = phase_sems("l2", "u uT uTs x2 chain", "idx gathered_s taken diag bcast sel var sd msgs y ysb scat yfree "
                        "oidx")
        l3 = phase_sems("l3", "sq norm comb cT cTs h2 var2 sd2 h3 chain", "idx gathered_s taken diag bcast sel "
                        "hid hids var sd mT mTs y ysb scat yfree oidx")
        loads = []

        def load(dst, srcap):
            loads.append((dst, srcap))

        col = lambda v: v.rearrange("(p a) -> p a", a=1)
        row = lambda v: v.rearrange("(a n) -> a n", a=1)
        load(srcI[:EP, 0:CH], src.rearrange("(p c) -> p c", p=EP))
        load(dstI[:EP, 0:CH], dst.rearrange("(p c) -> p c", p=EP))
        load(ew[:EP, :], edge_weight.rearrange("(p c) -> p c", p=EP))
        load(wkv[:, 0:C], WkT)
        load(wkv[:, C:2 * C], WvT)
        load(wq[:, 0:C], WqT)
        load(wo[:, :], WoT)
        for k in range(2):
            load(we1[:, k, :], We1[k * C:(k + 1) * C, :])
            load(wn1[:, k, :], Wn1[k * C:(k + 1) * C, :])
            load(wout[:, k, :], WoutT[k * C:(k + 1) * C, :])
        load(we2[:, :], We2)
        load(wn2[:, :], Wn2)
        load(w1[:, :], W1)
        load(w2[:, :], W2)
        load(kvq_row[:, 0:C], row(bk))
        load(kvq_row[:, C:2 * C], row(bv))
        load(kvq_row[:, 2 * C:KV], row(bd))
        load(kvq_row[:, KV:KV + C], row(bq))
        load(be2_row[:, :], row(be2))
        load(b2_row[:, :], row(b2))
        load(bout_row[:, :], row(b_out))
        load(be1c[:, :], col(be1))
        load(bn1c[:, :], col(bn1))
        load(b1c[:, :], col(b1))
        for t, v in ((bo_b, bo), (bn2_b, bn2), (gamma_b, gamma), (beta_b, beta), (wdb, Wd.rearrange("h a -> (h a)"))):
            load(t[:, :], v.partition_broadcast(P))
        NLOAD = 16 * len(loads)
        T = NG // 2

        flat = [RS[:, :, :].rearrange("p c f -> p (c f)"), RD[:, :, :].rearrange("p c f -> p (c f)"),
                RV[:, :, :].rearrange("p c f -> p (c f)")]
        place = {"at": 0}
        cap = CH * C

        def dense(width):
            n = U * width
            a = place["at"]
            if a // cap != (a + n - 1) // cap:
                a = (a // cap + 1) * cap
            place["at"] = a + n
            return flat[a // cap][:, a % cap:a % cap + n].rearrange("p (u c) -> p u c", u=U)

        if cap >= 512 * 20:
            bufs = {n: [dense(w) for _ in range(2)] for n, w in
                    (("x", C), ("s0", C), ("s1", C), ("s2", AW), ("s3", C), ("x1", C), ("xb", C), ("xn", C),
                     ("hT", C), ("h2", C), ("t", C), ("aa", C), ("o", C))}
        else:
            bufs = {n: [sb(f"d_{n}{k}", [P, U, w])[:, :, :] for k in range(2)] for n, w in
                    (("x", C), ("s0", C), ("s1", C), ("s2", AW), ("s3", C), ("x1", C), ("xb", C), ("xn", C),
                     ("hT", C), ("h2", C), ("t", C), ("aa", C), ("o", C))}
        D_NAMES = ("x1a var1 sd1 xn1 xb xbb t1 h1 hid1 u1 m1 aa sqr norm var2 sd2 comb cT cTs hid2 u2 h2p "
                   "var3 sd3 n3 g3 var4 sd4 xn4 t4 h4 o4 osb")
        dd = phase_sems("d", D_NAMES)
        d_chain = [[sem(f"d{k}_{n}_chain") for n in ("vector", "pool")] for k in range(2)]
        d_in = [[sem(f"d{k}_in_{n}") for n in ("x", "s0", "s1", "s2", "s3")] for k in range(2)]
        d_out = [sem(f"d{k}_stored") for k in range(2)]

        block = ctx.enter_context(nc.Block())

        def rows_of(t, base):
            return t[ds(base, ROWS), :].rearrange("(p u) c -> p u c", u=U)

        @block.sync
        def _(sp):
            sp.wait_ge(s_vec_const, 1)
            for d, s in loads:
                sp.dma_start(d, s, allow_slow_non_contiguous=True).then_inc(s_loaded, 16)
            for k, (t, w) in enumerate(((S0, C), (S1, C), (S2, AW), (S3, C))):
                tv = t.rearrange("(p r) c -> p r c", p=P)
                with sp.Fori(0, TF // ZR) as r:
                    sp.dma_start(tv[:, ds(r * ZR, ZR), :],
                                 zeros[:, 0:w].unsqueeze(1).broadcast_to([P, ZR, w])).then_inc(s_zero[k], 16)
            def fetch(k, base):
                for n, t, s in zip(("x", "s0", "s1", "s2"), (x, S0, S1, S2), d_in[k]):
                    sp.dma_start(bufs[n][k], rows_of(t, base)).then_inc(s, 16)

            def fetch_last(k, base):
                sp.dma_start(bufs["s3"][k], rows_of(S3, base)).then_inc(d_in[k][4], 16)

            def store(k, turn, base):
                sp.wait_ge(dd["osb"], dd.due("osb", 2 * turn + k + 1))
                sp.dma_start(rows_of(out, base), bufs["o"][k]).then_inc(d_out[k], 16)

            sp.wait_ge(l3["yfree"], l3.due("yfree", G + 1))
            for k in range(2):
                fetch(k, bases[k])
                fetch_last(k, bases[k])

            def sp_turn(i, now, after):
                for k in range(2):
                    store(k, i, now[k])
                    fetch(k, after[k])
                for k in range(2):
                    sp.wait_ge(d_out[k], 16 * (i + 1))
                    fetch_last(k, after[k])

            with sp.Fori(0, T - 2) as i:
                sp_turn(i, [(2 * i + k) * ROWS for k in range(2)], [(2 * i + 2 + k) * ROWS for k in range(2)])
            sp_turn(T - 2, bases[NG - 4:NG - 2], bases[NG - 2:])
            store(0, T - 1, bases[NG - 2])
            sp.wait_ge(d_out[0], 16 * T)
            store(1, T - 1, bases[NG - 1])
            sp.wait_ge(d_out[1], 16 * T)

        def at(c):
            return bass.IndirectOffsetOnAxis(ap=c, axis=0)

        @block.gpsimd
        def _(pool):
            def hold(s, v):
                pool.wait_ge(s, v)
                pool.sem_inc(s_hold, 1)

            pool.memset(ident[:, :], 1.0)
            pool.memset(ltri[:, :], 1.0)
            pool.memset(ones[:, :], 1.0).then_inc(s_pool_chain, 1)
            pool.wait_ge(s_pool_chain, 1)
            pool.affine_select(out=ident[:, :], in_=ident[:, :], compare_op=ALU.is_equal, fill=0.0, base=0,
                               pattern=[[-1, P]], channel_multiplier=1)
            pool.affine_select(out=ltri[:, :], in_=ltri[:, :], compare_op=ALU.is_gt, fill=0.0, base=0,
                               pattern=[[-1, P]], channel_multiplier=1)
            pool.iota(iota_f[:, :], pattern=[[1, max(TF, P)]], base=0, channel_multiplier=0,
                      allow_small_or_imprecise_dtypes=True)
            pool.iota(iota_p[:, :], pattern=[[0, 1]], base=0, channel_multiplier=1,
                      allow_small_or_imprecise_dtypes=True)
            pool.iota(trash[:, :], pattern=[[0, 1]], base=N, channel_multiplier=1,
                      allow_small_or_imprecise_dtypes=True).then_inc(s_pool_const, 1)

            def gather(s, buf, width, table_ap, idx):
                for u in range(U):
                    pool.indirect_dma_start(out=buf[:, u, 0:width], out_offset=None, in_=table_ap,
                                            in_offset=at(idx[:, u:u + 1])).then_inc(s, 16)

            def scatter(ph, g, table_ap, width, idx):
                hold(ph["ysb"], ph.due("ysb", g + 1))
                hold(ph["oidx"], ph.due("oidx", g + 1))
                for u in range(U):
                    pool.indirect_dma_start(out=table_ap, out_offset=at(idx[:, u:u + 1]), in_=y[:, u, 0:width],
                                            in_offset=None, compute_op=ALU.add).then_inc(ph["scat"], 16)
                    hold(ph["scat"], ph.due("scat", 16 * U * g + 16 * (u + 1)))
                pool.sem_inc(ph["yfree"], 1)

            with pool.Fori(0, G) as g:
                hold(p0["taken"], p0.due("taken", g + 1))
                hold(p0["idx"], p0.due("idx", g + 1))
                gather(p0["gathered_s"], gA, C, x, ibS)
                gather(p0["gathered_d"], gB, C, x, ibD)
            pool.wait_ge(sm["hmax"], sm.due("hmax", 1))
            pool.partition_all_reduce(hall[:, :], hmax[:, :], P, bass.bass_isa.ReduceOp.max).then_inc(sm["allmax"], 1)
            pool.wait_ge(sm["hsum"], sm.due("hsum", 1))
            pool.partition_all_reduce(hall[:, :], hsum[:, :], P, bass.bass_isa.ReduceOp.add).then_inc(sm["allsum"], 1)
            pool.sem_inc(l0["yfree"], 1)
            hold(s_zero[0], 16 * (TF // ZR))
            with pool.Fori(0, G) as g:
                scatter(l0, g, S0, C, ibO)
            def gather1(g):
                hold(l1["taken"], l1.due("taken", g + 1))
                hold(l1["idx"], l1.due("idx", g + 1))
                gather(l1["gathered_s"], gA, C, S0, ibS)
                gather(l1["gathered_d"], gB, C, S0, ibD)

            pool.sem_inc(l1["yfree"], 1)
            hold(s_zero[1], 16 * (TF // ZR))
            gather1(0)
            with pool.Fori(0, G - 1) as g:
                gather1(g + 1)
                scatter(l1, g, S1, C, ibO)
            scatter(l1, G - 1, S1, C, ibO)

            def gather_one(ph, g, width, table_ap):
                hold(ph["taken"], ph.due("taken", g + 1))
                hold(ph["idx"], ph.due("idx", g + 1))
                gather(ph["gathered_s"], gA, width, table_ap, ibS)

            for ph, zero, source, w_in, target, w_out in ((l2, s_zero[2], S1, C, S2, AW), (l3, s_zero[3], S2, AW, S3, C)):
                pool.sem_inc(ph["yfree"], 1)
                hold(zero, 16 * (TF // ZR))
                gather_one(ph, 0, w_in, source)
                with pool.Fori(0, G - 1) as g:
                    gather_one(ph, g + 1, w_in, source)
                    scatter(ph, g, target, w_out, ibO)
                scatter(ph, G - 1, target, w_out, ibO)

            ch = [Chain(pool, d_chain[k][1], 2) for k in range(2)]

            def stage(f):
                for k in range(2):
                    f(k, {n: b[k] for n, b in bufs.items()}, dd)

            with pool.Fori(0, T) as i:
                def x1a(k, B, d):
                    ch[k].step(i)
                    pool.wait_ge(d_in[k][0], 16 * i + 16)
                    pool.wait_ge(d_in[k][1], 16 * i + 16)
                    ch[k](pool.tensor_tensor(B["x1"], B["x"], B["s0"], ALU.add))
                    pool.tensor_tensor(B["x1"], B["x1"], over_rows(bo_b[:, :]), ALU.add).then_inc(d["x1a"], 1)

                def aa(k, B, d):
                    pool.wait_ge(d_in[k][3], 16 * i + 16)
                    pool.tensor_tensor(B["aa"], B["s2"][:, :, 0:C], B["s2"][:, :, 0:C], ALU.mult).then_inc(d["aa"], 1)

                def xbb(k, B, d):
                    pool.wait_ge(d["xb"], d.due("xb", 2 * i + k + 1))
                    pool.tensor_tensor(B["xb"], B["xb"], over_rows(bn2_b[:, :]), ALU.add).then_inc(d["xbb"], 1)

                def g3(k, B, d):
                    pool.wait_ge(d["n3"], d.due("n3", 2 * i + k + 1))
                    ch[k](pool.tensor_tensor(B["xn"], B["xn"], over_rows(gamma_b[:, :]), ALU.mult))
                    pool.tensor_tensor(B["xn"], B["xn"], over_rows(beta_b[:, :]), ALU.add).then_inc(d["g3"], 1)
                    ch[k].end()

                for f in (x1a, aa, xbb, g3):
                    stage(f)

        @block.scalar
        def _(act):
            def relu(o, i, bias=0.0):
                return act.activation(o, i, ACT.Relu, bias=bias)

            def cp(o, i):
                return act.activation(o, i, ACT.Copy)

            def root(o, i):
                return act.activation(o, i, ACT.Sqrt, bias=eps[:, 0:1])

            def sd_step(ph, want, done, g, o, i):
                act.wait_ge(ph[want], ph.due(want, g + 1))
                root(o, i).then_inc(ph[done], 1)

            act.wait_ge(s_loaded, NLOAD)
            act.wait_ge(s_vec_const, 2)
            with act.Fori(0, G) as g:
                sd_step(p0, "var", "sd", g, sd[:, :], mv[:, :, 1])
                act.wait_ge(p0["xT"], p0.due("xT", g + 1))
                relu(hTA[:, :, :], bank(0))
                relu(hTB[:, :, :], bank(1)).then_inc(p0["hT"], 1)
                for u in range(U):
                    act.wait_ge(p0["kvq"], p0.due("kvq", U * g + u + 1))
                    cp(RV[:, ds(U * g + u, 1), :].rearrange("p a c -> p (a c)"), pb[:, 2 + u % 2, C:2 * C])
                    if u >= 2:
                        act.wait_ge(p0["prod"], p0.due("prod", U * g + u - 1))
                    cp(qsb[:, u % 2, :], pb[:, 2 + u % 2, KV:KV + QW]).then_inc(p0["copied"], 1)
            act.wait_ge(sm["shifted"], sm.due("shifted", 1))
            act.activation(scores[:, :, :], scores[:, :, :], ACT.Exp).then_inc(sm["exp"], 1)

            def copy_sums(ph, g, mid, src_bank, dst):
                act.wait_ge(ph[mid], ph.due(mid, g + 1))
                cp(dst, bank(src_bank)).then_inc(ph[mid + "s"], 1)

            def put_y(ph, g, b):
                act.wait_ge(ph["y"], ph.due("y", g + 1))
                act.wait_ge(ph["yfree"], ph.due("yfree", g + 1))
                cp(y[:, :, 0:C], bank(b)).then_inc(ph["ysb"], 1)

            with act.Fori(0, G) as g:
                copy_sums(l0, g, "mT", 0, hTA[:, :, :])
                put_y(l0, g, 1)
            act.wait_ge(wx["shifted"], wx.due("shifted", 1))
            act.activation(wexp[:, :], segmax[:, :], ACT.Exp).then_inc(wx["exp"], 1)
            with act.Fori(0, G) as g:
                sd_step(l1, "var", "sd", g, sd[:, :], mv[:, :, 1])
                act.wait_ge(l1["xT"], l1.due("xT", g + 1))
                relu(hTA[:, :, :], bank(0))
                relu(hTB[:, :, :], bank(1)).then_inc(l1["hT"], 1)
                act.wait_ge(l1["hid"], l1.due("hid", g + 1))
                cp(RV[:, ds(U * g, U), :], bank(3))
                relu(hTB[:, :, :], bank(2), be1c[:, 0:1]).then_inc(l1["hids"], 1)
                copy_sums(l1, g, "en", 6, oh[:, :, :])
                copy_sums(l1, g, "mT", 7, hTA[:, :, :])
                put_y(l1, g, 6)
            with act.Fori(0, G) as g:
                act.wait_ge(l2["uT"], l2.due("uT", g + 1))
                relu(hTA[:, :, :], bank(0), bn1c[:, 0:1]).then_inc(l2["uTs"], 1)
                sd_step(l2, "var", "sd", g, sd[:, 0:U], mv[:, 0:U, 1])
                act.wait_ge(l2["y"], l2.due("y", g + 1))
                act.wait_ge(l2["yfree"], l2.due("yfree", g + 1))
                for b in range(2):
                    last = cp(y[:, 2 * b:2 * b + 2, :], pb[:, 2 + b, 0:2 * AW].rearrange("p (u c) -> p u c", u=2))
                last.then_inc(l2["ysb"], 1)
            with act.Fori(0, G) as g:
                act.wait_ge(l3["sq"], l3.due("sq", g + 1))
                act.activation(nr[:, :], sq[:, :], ACT.Sqrt).then_inc(l3["norm"], 1)
                copy_sums(l3, g, "cT", 0, hTA[:, :, :])
                act.wait_ge(l3["hid"], l3.due("hid", g + 1))
                relu(hTB[:, :, :], bank(1), b1c[:, 0:1]).then_inc(l3["hids"], 1)
                sd_step(l3, "var", "sd", g, sd[:, 0:U], mv[:, 0:U, 1])
                sd_step(l3, "var2", "sd2", g, sd2[:, :], mv2[:, :, 1])
                copy_sums(l3, g, "mT", 0, hTA[:, :, :])
                put_y(l3, g, 1)

            def both(i, want, done, f):
                for k in range(2):
                    act.wait_ge(dd[want], dd.due(want, 2 * i + k + 1))
                    f(k, {n: b[k] for n, b in bufs.items()}).then_inc(dd[done], 1)

            smalls = [(st, mv, sd, rs), (st2, mv2, sd2, rs2)]

            with act.Fori(0, T) as i:
                rt = lambda k, B: root(smalls[k][2][:, 0:U], smalls[k][1][:, 0:U, 1])
                both(i, "var1", "sd1", rt)
                both(i, "t1", "h1", lambda k, B: relu(B["hT"], bank(4 * k)))
                both(i, "hid1", "u1", lambda k, B: relu(B["t"], bank(4 * k + 1), bn1c[:, 0:1]))
                both(i, "sqr", "norm", lambda k, B: act.activation((nr, nrB)[k][:, :], (sq, sqB)[k][:, :], ACT.Sqrt))
                both(i, "var2", "sd2", rt)
                both(i, "cT", "cTs", lambda k, B: cp(B["hT"], bank(4 * k)))
                both(i, "hid2", "u2", lambda k, B: relu(B["t"], bank(4 * k + 1), b1c[:, 0:1]))
                both(i, "var3", "sd3", rt)
                both(i, "var4", "sd4", rt)
                both(i, "t4", "h4", lambda k, B: relu(B["hT"], bank(4 * k)))

        @block.tensor
        def _(pe):
            def transposes(b, tiles, done):
                for u in range(U):
                    last = pe.transpose(bank(b)[:, u, :], tiles[:, u, 0:P], ident[:, :])
                last.then_inc(done, 1)

            def bcast(b, dg):
                return pe.matmul(pb[:, b, :], ones[:, :], dg[:, :, :], start=True, stop=True)

            def stationary(b, w, rhs):
                return pe.matmul(pb[:, b, :], w, rhs, start=True, stop=True)

            def per_tile(b, lhs, rhs, bias=None):
                if bias is not None:
                    pe.matmul(pb[:, b, :], ones[0:1, :], bias[0:1, :].unsqueeze(1).broadcast_to([1, U, C]), start=True, stop=False, skip_group_check=True)
                for u in range(U):
                    last = pe.matmul(bank(b)[:, u, :], lhs[:, u, 0:P], rhs[:, u, :] if len(rhs.shape) == 3 else rhs,
                                     start=bias is None, stop=True, skip_group_check=True)
                return last

            pe.wait_ge(s_loaded, NLOAD)
            pe.wait_ge(s_pool_const, 1)
            pe.wait_ge(s_vec_const, 2)

            with pe.Fori(0, G) as g:
                def kvq(u):
                    b = 2 + u % 2
                    if u >= 2:
                        pe.wait_ge(p0["copied"], p0.due("copied", U * g + u - 1))
                        pe.wait_ge(p0["prod"], p0.due("prod", U * g + u - 1))
                    pe.matmul(pb[:, b, 0:KV + QW], ones[0:1, :], kvq_row[0:1, :], start=True, stop=False,
                              skip_group_check=True)
                    pe.matmul(pb[:, b, 0:KV], hTB[:, u, :], wkv[:, :], start=False, stop=True, skip_group_check=True)
                    pe.matmul(pb[:, b, KV:KV + QW], hTA[:, u, :], wq[:, :], start=False, stop=True,
                              skip_group_check=True).then_inc(p0["kvq"], 1)

                def tab(u):
                    b = 6 + u % 2
                    pe.wait_ge(p0["oh"], p0.due("oh", U * g + u + 1))
                    if u >= 2:
                        pe.wait_ge(p0["tabmax"], p0.due("tabmax", U * g + u - 1))
                    o = pb[:, b, 0:TF]
                    pe.matmul(o, ones16[0:1, :], far_row[0:1, :], start=True, stop=False)
                    pe.matmul(o, oh16[:, u, :], ohb[:, u % 2, :], start=False, stop=False)
                    pe.matmul(o, oh[:, u, :], ohv[:, u % 2, :], start=False, stop=True).then_inc(p0["tab"], 1)

                pe.wait_ge(p0["diag"], p0.due("diag", g + 1))
                bcast(4, dgA)
                bcast(5, dgB).then_inc(p0["bcast"], 1)
                pe.wait_ge(p0["xn"], p0.due("xn", g + 1))
                for b, t in ((0, wA), (1, wB)):
                    for u in range(U):
                        last = pe.transpose(bank(b)[:, u, :], t[:, u, :], ident[:, :])
                last.then_inc(p0["xT"], 1)
                pe.wait_ge(p0["hT"], p0.due("hT", g + 1))
                kvq(0)
                kvq(1)
                for u in range(U):
                    tab(u)
                kvq(2)
                kvq(3)

            def sums(ph, g, out_bank, rhs):
                pe.wait_ge(ph["mTs"], ph.due("mTs", g + 1))
                per_tile(out_bank, hTA, rhs).then_inc(ph["y"], 1)

            with pe.Fori(0, G) as g:
                pe.wait_ge(l0["diag"], l0.due("diag", g + 1))
                bcast(4, dgA)
                bcast(5, dgB).then_inc(l0["bcast"], 1)
                pe.wait_ge(l0["sel"], l0.due("sel", g + 1))
                for u in range(U):
                    if u >= 2:
                        pe.wait_ge(l0["looked"], l0.due("looked", U * g + u - 1))
                    pe.matmul(pb[:, 6 + u % 2, 0:TF], oh[:, u, :], table[:, :], start=True, stop=True)\
                      .then_inc(l0["look"], 1)
                pe.wait_ge(l0["msgs"], l0.due("msgs", g + 1))
                per_tile(0, wA, sel).then_inc(l0["mT"], 1)
                sums(l0, g, 1, wo[:, :])

            def select(ph, g, b):
                pe.wait_ge(ph["diag"], ph.due("diag", g + 1))
                bcast(b, dgA).then_inc(ph["bcast"], 1)

            with pe.Fori(0, G) as g:
                select(l1, g, 4)
                pe.wait_ge(l1["xn"], l1.due("xn", g + 1))
                for b, t in ((0, wA), (1, wB)):
                    for u in range(U):
                        last = pe.transpose(bank(b)[:, u, :], t[:, u, :], ident[:, :])
                last.then_inc(l1["xT"], 1)
                pe.wait_ge(l1["hT"], l1.due("hT", g + 1))
                pe.matmul(pb[:, 2, :], we1[:, 0, :], hTA[:, :, :], start=True, stop=False)
                pe.matmul(pb[:, 2, :], we1[:, 1, :], hTB[:, :, :], start=False, stop=True)
                per_tile(3, hTA, wn1[:, 0, :]).then_inc(l1["hid"], 1)
                pe.wait_ge(l1["hids"], l1.due("hids", g + 1))
                per_tile(6, hTB, we2[:, :], be2_row).then_inc(l1["en"], 1)
                pe.wait_ge(l1["ens"], l1.due("ens", g + 1))
                pe.wait_ge(l1["sel"], l1.due("sel", g + 1))
                per_tile(7, oh, sel).then_inc(l1["mT"], 1)
                sums(l1, g, 6, wn1[:, 1, :])
            with pe.Fori(0, G) as g:
                select(l2, g, 4)
                pe.wait_ge(l2["u"], l2.due("u", g + 1))
                transposes(0, wA, l2["uT"])
                pe.wait_ge(l2["uTs"], l2.due("uTs", g + 1))
                per_tile(1, hTA, wn2[:, :]).then_inc(l2["x2"], 1)
                pe.wait_ge(l2["sel"], l2.due("sel", g + 1))
                pe.wait_ge(l2["msgs"], l2.due("msgs", g + 1))
                for u in range(U):
                    last = pe.matmul(pb[:, 2 + u // 2, AW * (u % 2):AW * (u % 2) + AW], sel[:, u, :], msg[:, u, :],
                                     start=True, stop=True, skip_group_check=True)
                last.then_inc(l2["y"], 1)
            with pe.Fori(0, G) as g:
                select(l3, g, 4)
                pe.wait_ge(l3["comb"], l3.due("comb", g + 1))
                transposes(0, wA, l3["cT"])
                pe.wait_ge(l3["cTs"], l3.due("cTs", g + 1))
                stationary(1, w1[:, :], hTA[:, :, :]).then_inc(l3["hid"], 1)
                pe.wait_ge(l3["hids"], l3.due("hids", g + 1))
                per_tile(2, hTB, w2[:, :], b2_row).then_inc(l3["h2"], 1)
                pe.wait_ge(l3["sel"], l3.due("sel", g + 1))
                pe.wait_ge(l3["h3"], l3.due("h3", g + 1))
                per_tile(0, wB, sel).then_inc(l3["mT"], 1)
                sums(l3, g, 1, wout[:, 1, :])

            def both(i, wants, done, f):
                for k in range(2):
                    for wname in wants:
                        pe.wait_ge(dd[wname], dd.due(wname, 2 * i + k + 1))
                    f(k, {n: b[k] for n, b in bufs.items()}).then_inc(dd[done], 1)

            def tr(b, tiles):
                for u in range(U):
                    last = pe.transpose(bank(b)[:, u, :], tiles[:, u, :], ident[:, :])
                return last

            with pe.Fori(0, T) as i:
                def hid1(k, B):
                    pe.wait_ge(d_in[k][2], 16 * i + 16)
                    pe.matmul(pb[:, 4 * k + 1, :], wn1[:, 0, :], B["hT"], start=True, stop=False,
                              skip_group_check=True)
                    for u in range(U):
                        last = pe.matmul(bank(4 * k + 1)[:, u, :], B["s1"][:, u, :], ident[:, :], start=False,
                                         stop=True, skip_group_check=True)
                    return last

                both(i, ["xn1"], "t1", lambda k, B: tr(4 * k, B["xn"]))
                both(i, ["h1"], "hid1", hid1)
                both(i, ["u1"], "m1", lambda k, B: per_tile(4 * k + 2, B["t"], wn2[:, :]))
                both(i, ["comb"], "cT", lambda k, B: tr(4 * k, B["h2"]))
                both(i, ["cTs"], "hid2", lambda k, B: stationary(4 * k + 1, w1[:, :], B["hT"]))
                both(i, ["u2"], "h2p", lambda k, B: per_tile(4 * k + 2, B["t"], w2[:, :], b2_row))
                both(i, ["xn4"], "t4", lambda k, B: tr(4 * k, B["xn"]))
                both(i, ["h4"], "o4", lambda k, B: per_tile(4 * k + 2, B["hT"], wout[:, 0, :], bout_row))

        @block.vector
        def _(v):
            tt, ts, stt = v.tensor_tensor, v.tensor_scalar, v.scalar_tensor_tensor

            def stats(chain, tiles, st_, mv_, ph, want, n):
                for t in range(n):
                    ins = v.bn_stats(st_[:, t, :], tiles[t])
                chain(ins)
                f = lambda j: st_[:, 0:n, j]
                tt(mv_[:, 0:n, 2], f(1), f(4), ALU.add)
                tt(mv_[:, 0:n, 3], f(1), f(4), ALU.subtract)
                chain(tt(mv_[:, 0:n, 4], f(2), f(5), ALU.add))
                ts(mv_[:, 0:n, 0], mv_[:, 0:n, 2], 0.5, None, ALU.mult)
                chain(stt(out=mv_[:, 0:n, 5], in0=mv_[:, 0:n, 3], scalar=0.25, in1=mv_[:, 0:n, 3],
                          op0=ALU.mult, op1=ALU.mult))
                stt(out=mv_[:, 0:n, 1], in0=mv_[:, 0:n, 4], scalar=1.0 / C, in1=mv_[:, 0:n, 5],
                    op0=ALU.mult, op1=ALU.add).then_inc(ph[want], 1)

            def normalize(chain, ph, done, g, outs, tiles, mv_, sd_, rs_, n):
                v.wait_ge(ph[done], ph.due(done, g + 1))
                chain(v.reciprocal(rs_[:, 0:n], sd_[:, 0:n]))
                for t in range(n):
                    ins = v.tensor_scalar(outs[t], tiles[t], mv_[:, t, 0:1], rs_[:, t:t + 1], ALU.subtract, ALU.mult)
                return ins


            v.memset(srcI[:, :], 0)
            v.memset(dstI[:, :], 0)
            v.memset(ew[:, :], 0.0)
            v.memset(kvq_row[:, :], 0.0)
            v.memset(zeros[:, :], 0.0).then_inc(s_vec_const, 1)
            v.memset(ones16[:, :], 1.0)
            v.memset(far_row[:, :], -ABSENT)
            v.memset(table[:, :], -ABSENT)
            v.memset(eps[:, :], LN_EPS)
            setup = Chain(v, sem("vec_setup"), 12)
            setup.step(0)
            v.wait_ge(s_loaded, NLOAD)
            v.wait_ge(s_pool_const, 1)
            setup(ts(not_edge[:, :], iota_p[:, :], float(EP), None, ALU.is_ge))
            setup(tt(rr[:, 0:1], not_edge[:, :], trash[:, :], ALU.mult))
            setup(ts(keyS[:, :], srcI[:, 0:CH], rr[:, 0:1], None, ALU.add))
            setup(ts(keyD[:, :], dstI[:, 0:CH], rr[:, 0:1], None, ALU.add))
            setup(v.tensor_copy(keyI, keyD[:, :]))
            setup(ts(pI, keyI, P - 1, None, ALU.bitwise_and))
            setup(ts(fI, keyI, 7, None, ALU.arith_shift_right))
            setup(v.tensor_copy(keyp[:, :], pI))
            setup(v.tensor_copy(keyf[:, :], fI))
            setup(ts(wkv[:, 2 * C:KV], wdb[:, :], 1.0 / C, None, ALU.mult))
            setup(ts(wq[:, C:QW], wdb[:, :], -1.0 / C, None, ALU.mult))
            v.tensor_copy(ibS[:, :], srcI[:, 0:U])
            setup(v.tensor_copy(ibD[:, :], dstI[:, 0:U]))
            setup.end()
            v.sem_inc(s_vec_const, 1)
            v.sem_inc(p0["taken"], 1)
            v.sem_inc(p0["idx"], 1)

            def cols(t, g):
                return t[:, ds(U * g, U)]

            def diag(dg, keys):
                return tt(dg[:, :, :], ident[:, :].unsqueeze(1).broadcast_to([P, U, P]), over_cols(keys), ALU.mult)

            def next_idx(ph, g, both_ends):
                ins = v.tensor_copy(ibS[:, :], srcI[:, ds(U * g + U, U)])
                if both_ends:
                    ins = v.tensor_copy(ibD[:, :], dstI[:, ds(U * g + U, U)])
                ins.then_inc(ph["idx"], 1)

            c = Chain(v, p0["chain"], 13 + 3 * U)
            with v.Fori(0, G) as g:
                c.step(g)
                diag(dgA, cols(keyD, g))
                diag(dgB, cols(ew, g)).then_inc(p0["diag"], 1)
                v.wait_ge(p0["gathered_s"], p0.due("gathered_s", 16 * U * g + 16 * U))
                v.wait_ge(p0["gathered_d"], p0.due("gathered_d", 16 * U * g + 16 * U))
                next_idx(p0, g, True)
                v.tensor_copy(RS[:, ds(U * g, U), :], gA[:, :, 0:C])
                ins = v.tensor_copy(RD[:, ds(U * g, U), :], gB[:, :, 0:C])
                c(ins)
                v.sem_inc(p0["taken"], 1)
                tiles = [RS[:, ds(U * g + u, 1), :].rearrange("p a c -> p (a c)") for u in range(U)] + \
                        [RD[:, ds(U * g + u, 1), :].rearrange("p a c -> p (a c)") for u in range(U)]
                stats(c, tiles, st, mv, p0, "var", 2 * U)
                normalize(c, p0, "sd", g, [wA[:, u, :] for u in range(U)] + [wB[:, u, :] for u in range(U)],
                          tiles, mv, sd, rs, 2 * U).then_inc(p0["xn"], 1)
                v.wait_ge(p0["bcast"], p0.due("bcast", g + 1))
                c(tt(sel[:, :, :], bank(4), over_cols(cols(keyD, g)), ALU.not_equal))
                c(stt(out=dgB[:, :, 0:C], in0=sel[:, :, :], scalar=-FAR, in1=bank(5), op0=ALU.mult, op1=ALU.add))
                c(v.tensor_reduce(out=ml[:, :], in_=dgB[:, :, 0:C], axis=AX.X, op=ALU.max))
                c(stt(out=dgA[:, :, :], in0=sel[:, :, :], scalar=0.0, in1=ltri[:, :].unsqueeze(1).broadcast_to([P, U, P]),
                      op0=ALU.is_equal, op1=ALU.mult))
                c(v.tensor_reduce(out=rk[:, :], in_=dgA[:, :, :], axis=AX.X, op=ALU.add))
                v.tensor_copy(cols(rankD, g), rk[:, :])
                c(ts(fr[:, :], rk[:, :], 0.0, None, ALU.is_equal))
                for u in range(U):
                    cc = ds(U * g + u, 1)
                    ins = ts(oh[:, u, :], iota_f[:, 0:P], keyp[:, cc], fr[:, u:u + 1], ALU.is_equal, ALU.mult)
                c(ins)
                v.tensor_copy(oh16[:, :, :], oh[:, :, :])

                def table_max(u):
                    v.wait_ge(p0["tab"], p0.due("tab", U * g + u + 1))
                    c(tt(table[:, :], pb[:, 6 + u % 2, 0:TF], table[:, :], ALU.max))
                    v.sem_inc(p0["tabmax"], 1)

                for u in range(U):
                    cc = ds(U * g + u, 1)
                    if u >= 2:
                        table_max(u - 2)
                    ts(ohv[:, u % 2, :], iota_f[:, 0:TF], keyf[:, cc], ml[:, u:u + 1], ALU.is_equal, ALU.mult)
                    ts(ohb[:, u % 2, :], iota_f[:, 0:TF], keyf[:, cc], ABSENT, ALU.is_equal, ALU.mult)\
                        .then_inc(p0["oh"], 1)
                table_max(2)
                table_max(3)
                for u in range(U):
                    b = 2 + u % 2
                    cc = ds(U * g + u, 1)
                    v.wait_ge(p0["copied"], p0.due("copied", U * g + u + 1))
                    c(tt(dgA[:, u, :], pb[:, b, 0:C], qsb[:, u % 2, 0:C], ALU.mult))
                    c(stt(out=sct[:, u, :], in0=pb[:, b, 2 * C:KV], scalar=ew[:, cc], in1=qsb[:, u % 2, C:QW],
                          op0=ALU.add, op1=ALU.add))
                    v.sem_inc(p0["prod"], 1)
                c(v.tensor_reduce(out=red[:, :, :].rearrange("p u h -> p (u h)"),
                                  in_=dgA[:, :, :].rearrange("p u (h d) -> p (u h) d", d=HD), axis=AX.X, op=ALU.add))
                stt(out=scores[:, ds(U * g, U), :], in0=red[:, :, :], scalar=SCALE, in1=sct[:, :, :],
                    op0=ALU.mult, op1=ALU.add)
                c.end()
            c = Chain(v, sm["chain"], 12)
            c.step(0)

            def indices(rank, key, t):
                c(ts(rank, rank, 1.0, None, ALU.min))
                c(ts(t, key, -1.0, trash[:, 0:1], ALU.mult, ALU.add))
                c(tt(t, t, rank, ALU.mult))
                c(tt(t, t, key, ALU.add))

            indices(rankD[:, :], keyD[:, :], tmpc[:, :])
            c(v.tensor_copy(idxD[:, :], tmpc[:, :]))
            c(ts(rr[:, 0:1], not_edge[:, :], -FAR, None, ALU.mult))
            c(ts(scores[:, :, :], scores[:, :, :], rr[:, 0:1], None, ALU.add))
            v.tensor_reduce(out=hmax[:, :], in_=scores[:, :, :].rearrange("p c h -> p h c"), axis=AX.X, op=ALU.max)\
                .then_inc(sm["hmax"], 1)
            over_edges = lambda t: t[:, :].unsqueeze(1).broadcast_to([P, CH, H])
            v.wait_ge(sm["allmax"], sm.due("allmax", 1))
            tt(scores[:, :, :], scores[:, :, :], over_edges(hall), ALU.subtract).then_inc(sm["shifted"], 1)
            v.wait_ge(sm["exp"], sm.due("exp", 1))
            v.tensor_reduce(out=hsum[:, :], in_=scores[:, :, :].rearrange("p c h -> p h c"), axis=AX.X, op=ALU.add)\
                .then_inc(sm["hsum"], 1)
            v.wait_ge(sm["allsum"], sm.due("allsum", 1))
            c(v.reciprocal(hrec[:, :], hall[:, :]))
            c(tt(scores[:, :, :], scores[:, :, :], over_edges(hrec), ALU.mult))

            sc_end = c
            c = Chain(v, l0["chain"], 6)
            with v.Fori(0, G) as g:
                c.step(g)
                diag(dgA, cols(keyS, g))
                diag(dgB, cols(keyp, g)).then_inc(l0["diag"], 1)
                v.wait_ge(l0["bcast"], l0.due("bcast", g + 1))
                tt(wA[:, :, :].rearrange("p u (h d) -> p (u h) d", d=HD),
                   RV[:, ds(U * g, U), :].rearrange("p u (h d) -> p (u h) d", d=HD),
                   scores[:, ds(U * g, U), :].rearrange("p u h -> p (u h)").unsqueeze(2).broadcast_to([P, U * H, HD]),
                   ALU.mult).then_inc(l0["msgs"], 1)
                ts(oh[:, :, :], bank(5), iota_p[:, 0:1], None, ALU.is_equal)
                ins = tt(sel[:, :, :], bank(4), over_cols(cols(keyS, g)), ALU.is_equal)
                ins.then_inc(l0["sel"], 1)
                v.wait_ge(l0["sel"], l0.due("sel", g + 1))
                c(tt(dgA[:, :, :], sel[:, :, :], ltri[:, :].unsqueeze(1).broadcast_to([P, U, P]), ALU.mult))
                c(v.tensor_reduce(out=rk[:, :], in_=dgA[:, :, :], axis=AX.X, op=ALU.add))
                for u in range(U):
                    v.wait_ge(l0["look"], l0.due("look", U * g + u + 1))
                    stt(out=ohv[:, u % 2, :], in0=iota_f[:, 0:TF], scalar=keyf[:, ds(U * g + u, 1)],
                        in1=pb[:, 6 + u % 2, 0:TF], op0=ALU.is_equal, op1=ALU.mult, accum_out=ml[:, u:u + 1])\
                        .then_inc(l0["looked"], 1)
                v.wait_ge(l0["looked"], l0.due("looked", U * g + U))
                v.tensor_copy(cols(segmax, g), ml[:, :])
                indices(rk[:, :], cols(keyS, g), fr[:, :])
                v.wait_ge(l0["yfree"], l0.due("yfree", g + 1))
                v.tensor_copy(ibO[:, :], fr[:, :]).then_inc(l0["oidx"], 1)
                c.end()
            c = Chain(v, wx["chain"], 1)
            c.step(0)
            tt(segmax[:, :], ew[:, :], segmax[:, :], ALU.subtract).then_inc(wx["shifted"], 1)
            v.wait_ge(wx["exp"], wx.due("exp", 1))

            def first_idx(before, ph, both_ends):
                v.wait_ge(before["yfree"], before.due("yfree", G + 1))
                ins = v.tensor_copy(ibS[:, :], srcI[:, 0:U])
                if both_ends:
                    ins = v.tensor_copy(ibD[:, :], dstI[:, 0:U])
                c(ins)
                v.sem_inc(ph["taken"], 1)
                v.sem_inc(ph["idx"], 1)

            def out_idx(ph, g):
                v.wait_ge(ph["yfree"], ph.due("yfree", g + 1))
                v.tensor_copy(ibO[:, :], cols(idxD, g)).then_inc(ph["oidx"], 1)

            def select(ph, g):
                v.wait_ge(ph["bcast"], ph.due("bcast", g + 1))
                tt(sel[:, :, :], bank(4), over_cols(cols(keyD, g)), ALU.is_equal).then_inc(ph["sel"], 1)

            def each(t, g):
                return [t[:, ds(U * g + u, 1), :].rearrange("p a c -> p (a c)") for u in range(U)]

            def part(t):
                return [t[:, u, 0:C] for u in range(U)]

            first_idx(l0, l1, True)
            c = Chain(v, l1["chain"], 8)
            with v.Fori(0, G) as g:
                c.step(g)
                S, D = RS[:, ds(U * g, U), :], RD[:, ds(U * g, U), :]
                diag(dgA, cols(keyD, g)).then_inc(l1["diag"], 1)
                v.wait_ge(l1["gathered_s"], l1.due("gathered_s", 16 * U * g + 16 * U))
                v.wait_ge(l1["gathered_d"], l1.due("gathered_d", 16 * U * g + 16 * U))
                next_idx(l1, g, True)
                tt(S, S, gA[:, :, 0:C], ALU.add)
                c(tt(D, D, gB[:, :, 0:C], ALU.add))
                v.sem_inc(l1["taken"], 1)
                tt(S, S, over_rows(bo_b[:, :]), ALU.add)
                c(tt(D, D, over_rows(bo_b[:, :]), ALU.add))
                tiles = each(RS, g) + each(RD, g)
                v.sem_inc(s_vhold, 1)
                stats(c, tiles, st, mv, l1, "var", 2 * U)
                normalize(c, l1, "sd", g, part(wA) + part(wB), tiles, mv, sd, rs, 2 * U).then_inc(l1["xn"], 1)
                v.wait_ge(l1["xn"], l1.due("xn", g + 1))
                c(stt(out=S, in0=wA[:, :, :], scalar=0.0, in1=S, op0=ALU.max, op1=ALU.add))
                c(tt(S, S, over_rows(bn2_b[:, :]), ALU.add))
                select(l1, g)
                out_idx(l1, g)
                c.end()
            c = Chain(v, wx["chain2"], 1)
            c.step(0)
            first_idx(l1, l2, False)
            v.memset(msg[:, :, :], 1.0)
            c = Chain(v, l2["chain"], 7)
            with v.Fori(0, G) as g:
                c.step(g)
                S = RS[:, ds(U * g, U), :]
                diag(dgA, cols(keyD, g)).then_inc(l2["diag"], 1)
                v.wait_ge(l2["gathered_s"], l2.due("gathered_s", 16 * U * g + 16 * U))
                next_idx(l2, g, False)
                tt(wA[:, :, :], RV[:, ds(U * g, U), :], gA[:, :, 0:C], ALU.add).then_inc(l2["u"], 1)
                v.wait_ge(l2["u"], l2.due("u", g + 1))
                v.sem_inc(l2["taken"], 1)
                select(l2, g)
                v.wait_ge(l2["x2"], l2.due("x2", g + 1))
                c(tt(S, bank(1), S, ALU.add))
                v.sem_inc(s_vhold, 1)
                stats(c, each(RS, g), st, mv, l2, "var", U)
                c(normalize(c, l2, "sd", g, part(wB), each(RS, g), mv, sd, rs, U))
                c(ts(RD[:, ds(U * g, U), :], wB[:, :, :], 0.0, None, ALU.max))
                tt(msg[:, :, 0:C], RD[:, ds(U * g, U), :], over_cols(cols(wexp, g), C), ALU.mult)
                v.tensor_copy(msg[:, :, C:C + 1].rearrange("p u a -> p (u a)"), cols(wexp, g)).then_inc(l2["msgs"], 1)
                out_idx(l2, g)
                c.end()
            c = Chain(v, wx["chain3"], 1)
            c.step(0)
            first_idx(l2, l3, False)
            c = Chain(v, l3["chain"], 17)

            def scale_of_sum(c, table_rows, dn_, nr_, rr_, ph, g):
                den = table_rows[:, :, C:C + 1].rearrange("p u a -> p (u a)")
                c(ts(dn_[:, :], den, 0.5, PROJ_EPS, ALU.max, ALU.mult))
                v.wait_ge(ph["norm"], ph.due("norm", g + 1))
                c(tt(dn_[:, :], nr_[:, :], dn_[:, :], ALU.add))
                c(v.reciprocal(rr_[:, :], dn_[:, :]))

            with v.Fori(0, G) as g:
                c.step(g)
                S = RS[:, ds(U * g, U), :]
                diag(dgA, cols(keyD, g)).then_inc(l3["diag"], 1)
                v.wait_ge(l3["gathered_s"], l3.due("gathered_s", 16 * U * g + 16 * U))
                next_idx(l3, g, False)
                c(tt(dgB[:, :, 0:C], gA[:, :, 0:C], gA[:, :, 0:C], ALU.mult))
                v.tensor_reduce(out=sq[:, :], in_=dgB[:, :, 0:C], axis=AX.X, op=ALU.add).then_inc(l3["sq"], 1)
                scale_of_sum(c, gA, dn, nr, rr, l3, g)
                h2 = each(RD, g)
                for u in range(U):
                    ins = stt(out=wA[:, u, :], in0=gA[:, u, 0:C], scalar=rr[:, u:u + 1], in1=h2[u],
                              op0=ALU.mult, op1=ALU.add)
                ins.then_inc(l3["comb"], 1)
                v.wait_ge(l3["comb"], l3.due("comb", g + 1))
                v.sem_inc(l3["taken"], 1)
                select(l3, g)
                v.wait_ge(l3["h2"], l3.due("h2", g + 1))
                stats(c, part(bank(2)), st, mv, l3, "var", U)
                c(normalize(c, l3, "sd", g, part(wB), part(bank(2)), mv, sd, rs, U))
                c(tt(wB[:, :, :], wB[:, :, :], over_rows(gamma_b[:, :]), ALU.mult))
                c(tt(wB[:, :, :], wB[:, :, :], over_rows(beta_b[:, :]), ALU.add))
                c(tt(S, S, wB[:, :, :], ALU.add))
                v.sem_inc(s_vhold, 1)
                stats(c, each(RS, g), st2, mv2, l3, "var2", U)
                c(normalize(c, l3, "sd2", g, part(wB), each(RS, g), mv2, sd2, rs2, U))
                ts(wB[:, :, :], wB[:, :, :], 0.0, None, ALU.max).then_inc(l3["h3"], 1)
                out_idx(l3, g)
                c.end()

            v.wait_ge(l3["yfree"], l3.due("yfree", G + 1))
            ch = [Chain(v, d_chain[k][0], 26) for k in range(2)]
            SM = [(st, mv, sd, rs, sq, nr, dn, rr), (st2, mv2, sd2, rs2, sqB, nrB, dnB, rrB)]

            def stage(f):
                for k in range(2):
                    f(k, {n: b[k] for n, b in bufs.items()}, dd, ch[k], *SM[k])

            with v.Fori(0, T) as i:
                def s1(k, B, d, c, st, mv, sd, rs, sq, nr, dn, rr):
                    c.step(i)
                    v.wait_ge(d["x1a"], d.due("x1a", 2 * i + k + 1))
                    stats(c, part(B["x1"]), st, mv, d, "var1", U)

                def s2(k, B, d, c, st, mv, sd, rs, sq, nr, dn, rr):
                    normalize(c, d, "sd1", 2 * i + k, part(B["xn"]), part(B["x1"]), mv, sd, rs, U).then_inc(d["xn1"], 1)
                    v.wait_ge(d["xn1"], d.due("xn1", 2 * i + k + 1))
                    stt(out=B["xb"], in0=B["xn"], scalar=0.0, in1=B["x1"], op0=ALU.max, op1=ALU.add)\
                        .then_inc(d["xb"], 1)

                def s3(k, B, d, c, st, mv, sd, rs, sq, nr, dn, rr):
                    v.wait_ge(d["aa"], d.due("aa", 2 * i + k + 1))
                    v.tensor_reduce(out=sq[:, :], in_=B["aa"], axis=AX.X, op=ALU.add).then_inc(d["sqr"], 1)

                def s4(k, B, d, c, st, mv, sd, rs, sq, nr, dn, rr):
                    v.wait_ge(d["m1"], d.due("m1", 2 * i + k + 1))
                    v.wait_ge(d["xbb"], d.due("xbb", 2 * i + k + 1))
                    c(tt(B["x1"], bank(4 * k + 2), B["xb"], ALU.add))
                    stats(c, part(B["x1"]), st, mv, d, "var2", U)

                def s5(k, B, d, c, st, mv, sd, rs, sq, nr, dn, rr):
                    c(normalize(c, d, "sd2", 2 * i + k, part(B["xn"]), part(B["x1"]), mv, sd, rs, U))
                    c(ts(B["h2"], B["xn"], 0.0, None, ALU.max))
                    scale_of_sum(c, B["s2"], dn, nr, rr, d, 2 * i + k)
                    for u in range(U):
                        ins = stt(out=B["h2"][:, u, :], in0=B["s2"][:, u, 0:C], scalar=rr[:, u:u + 1],
                                  in1=B["h2"][:, u, :], op0=ALU.mult, op1=ALU.add)
                    ins.then_inc(d["comb"], 1)

                def s6(k, B, d, c, st, mv, sd, rs, sq, nr, dn, rr):
                    v.wait_ge(d["h2p"], d.due("h2p", 2 * i + k + 1))
                    stats(c, part(bank(4 * k + 2)), st, mv, d, "var3", U)

                def s7(k, B, d, c, st, mv, sd, rs, sq, nr, dn, rr):
                    normalize(c, d, "sd3", 2 * i + k, part(B["xn"]), part(bank(4 * k + 2)), mv, sd, rs, U).then_inc(d["n3"], 1)

                def s8(k, B, d, c, st, mv, sd, rs, sq, nr, dn, rr):
                    v.wait_ge(d["g3"], d.due("g3", 2 * i + k + 1))
                    c(tt(B["x1"], B["x1"], B["xn"], ALU.add))
                    stats(c, part(B["x1"]), st, mv, d, "var4", U)

                def s9(k, B, d, c, st, mv, sd, rs, sq, nr, dn, rr):
                    normalize(c, d, "sd4", 2 * i + k, part(B["xn"]), part(B["x1"]), mv, sd, rs, U).then_inc(d["xn4"], 1)
                    v.wait_ge(d_in[k][4], 16 * i + 16)
                    cnt = B["s2"][:, :, C + 1:C + 2].rearrange("p u a -> p (u a)")
                    c(ts(dn[:, :], cnt, 1.0, None, ALU.max))
                    c(v.reciprocal(rr[:, :], dn[:, :]))
                    for u in range(U):
                        ins = stt(out=B["o"][:, u, :], in0=B["s3"][:, u, :], scalar=rr[:, u:u + 1],
                                  in1=B["x1"][:, u, :], op0=ALU.mult, op1=ALU.add)
                    c(ins)

                def s10(k, B, d, c, st, mv, sd, rs, sq, nr, dn, rr):
                    v.wait_ge(d["o4"], d.due("o4", 2 * i + k + 1))
                    tt(B["o"], bank(4 * k + 2), B["o"], ALU.add).then_inc(d["osb"], 1)
                    c.end()

                for f in (s1, s2, s3, s4, s5, s6, s7, s8, s9, s10):
                    stage(f)


_ORDER = ['x', 'src', 'dst', 'edge_weight', 'WqT', 'bq', 'WkT', 'bk', 'WvT', 'bv', 'Wd', 'bd', 'WoT', 'bo',
          'We1', 'be1', 'We2', 'be2', 'Wn1', 'bn1', 'Wn2', 'bn2', 'W1', 'b1', 'W2', 'b2', 'gamma', 'beta',
          'WoutT', 'b_out']
_FROM = {'WqT': ('L0_gnn_Wq', True), 'bq': ('L0_gnn_bq', False), 'WkT': ('L0_gnn_Wk', True),
         'bk': ('L0_gnn_bk', False), 'WvT': ('L0_gnn_Wv', True), 'bv': ('L0_gnn_bv', False),
         'Wd': ('L0_gnn_Wd', False), 'bd': ('L0_gnn_bd', False), 'WoT': ('L0_gnn_Wo', True),
         'bo': ('L0_gnn_bo', False), 'WoutT': ('L3_gnn_W_out', True), 'b_out': ('L3_gnn_b_out', False)}
_FROM.update({n: (f'L1_gnn_{n}', False) for n in ('We1', 'be1', 'We2', 'be2', 'Wn1', 'bn1', 'Wn2', 'bn2')})
_FROM.update({n: (f'L2_gnn_{n}', False) for n in ('W1', 'b1', 'W2', 'b2', 'gamma', 'beta')})


def kernel(**inputs):
    import numpy as _np
    import concourse.bacc as _bacc
    from concourse import mybir as _mybir
    from concourse.bass_utils import run_bass_kernel_spmd as _run

    nc = _bacc.Bacc("TRN2", target_bir_lowering=False, num_devices=1)
    arrays, args = {}, []
    for name in _ORDER:
        key, transposed = _FROM.get(name, (name, False))
        a = _np.asarray(inputs[key])
        a = _np.ascontiguousarray(a.T if transposed else a)
        arrays[f"in_{name}"] = a
        args.append(nc.dram_tensor(f"in_{name}", a.shape, _mybir.dt.from_np(a.dtype), kind="ExternalInput").ap())
    shape = tuple(arrays["in_x"].shape)
    out = nc.dram_tensor("out_x", shape, _mybir.dt.float32, kind="ExternalOutput").ap()
    build_gnn(nc, *args, out)
    r = _run(nc, [arrays], core_ids=[0])
    return r.results[0]["out_x"]
```

```python
import concourse.bass as bass
from concourse import mybir
from contextlib import ExitStack

P = 128
U = 4
LN_EPS = 1e-5
PROJ_EPS = 1e-9
FAR = 3.0e38
ABSENT = 2.0 ** 127


class Phase(dict):

    def __init__(self, sems):
        super().__init__(sems)
        self.start = {}

    def due(self, name, n):
        return n + self.start.get(name, 0)


class Chain:

    def __init__(self, engine, sem, per):
        self.engine, self.sem, self.per, self.n, self.base = engine, sem, per, 0, 0

    def step(self, g):
        self.base, self.n = g * self.per, 0

    def __call__(self, ins):
        self.n += 1
        ins.then_inc(self.sem, 1)
        self.engine.wait_ge(self.sem, self.base + self.n)

    def end(self):
        assert self.n == self.per, f"chain of {self.n}, not {self.per}"


def build_gnn(nc, x, src, dst, edge_weight, WqT, bq, WkT, bk, WvT, bv, Wd, bd, WoT, bo,
              We1, be1, We2, be2, Wn1, bn1, Wn2, bn2, W1, b1, W2, b2, gamma, beta, WoutT, b_out, out):
    f32, bf16, i32 = mybir.dt.float32, mybir.dt.bfloat16, mybir.dt.int32
    ALU, ACT, AX = mybir.AluOpType, mybir.ActivationFunctionType, mybir.AxisListType
    ds = bass.ds

    N, C = x.shape
    E = src.shape[0]
    H = bd.shape[0]
    HD = C // H
    EP = max(p for p in range(1, P + 1) if E % p == 0 and (E // p) % U == 0)
    CH = E // EP
    G = CH // U
    TF = (N + P + P - 1) // P
    NT = TF * P
    ROWS = P * U
    NG = 2 * ((N + 2 * ROWS - 1) // (2 * ROWS))
    bases = [min(g * ROWS, N - ROWS) for g in range(NG)]
    assert all(b == g * ROWS for g, b in enumerate(bases[:-1]))
    SCALE = 1.0 / HD ** 0.5
    AW = C + 2
    ZR = next(z for z in (28, 4, 2, 1) if TF % z == 0)
    KV, QW = 2 * C + H, C + H

    ctx = ExitStack()
    with ctx:
        def sb(name, shape, dt=f32):
            return ctx.enter_context(nc.sbuf_tensor(name, shape, dt))

        def sem(name):
            return ctx.enter_context(nc.semaphore(name))

        S0 = nc.dram_tensor("sum_attention", (NT, C), f32, kind="Internal").ap()
        S1 = nc.dram_tensor("sum_edge_mlp", (NT, C), f32, kind="Internal").ap()
        S2 = nc.dram_tensor("sum_weighted", (NT, AW), f32, kind="Internal").ap()
        S3 = nc.dram_tensor("sum_mean", (NT, C), f32, kind="Internal").ap()

        ident = sb("ident", [P, P])
        ones = sb("ones", [P, P])
        ones16 = sb("ones16", [1, P], bf16)
        ltri = sb("ltri", [P, P])
        iota_f = sb("iota_f", [P, max(TF, P)])
        iota_p = sb("iota_p", [P, 1])
        trash = sb("trash", [P, 1])
        not_edge = sb("not_edge", [P, 1])
        eps = sb("eps", [P, 1])
        far_row = sb("far_row", [1, TF], bf16)
        zeros = sb("zeros", [P, AW])

        srcI = sb("srcI", [P, CH + U], i32)
        dstI = sb("dstI", [P, CH + U], i32)
        keyS = sb("keyS", [P, CH])
        keyD = sb("keyD", [P, CH])
        keyp = sb("keyp", [P, CH])
        keyf = sb("keyf", [P, CH])
        ew = sb("ew", [P, CH])
        rankD = sb("rankD", [P, CH])
        idxD = sb("idxD", [P, CH], i32)
        segmax = sb("segmax", [P, CH])
        wexp = sb("wexp", [P, CH])
        tmpc = sb("tmpc", [P, CH])
        keyI = idxD[:, :]
        pI, fI = tmpc[:, :].bitcast(i32), wexp[:, :].bitcast(i32)
        table = sb("table", [P, TF])
        scores = sb("scores", [P, CH, H])
        hmax = sb("hmax", [P, H])
        hall = sb("hall", [P, H])
        hsum = sb("hsum", [P, H])
        hrec = sb("hrec", [P, H])

        wkv = sb("wkv", [P, KV])
        wq = sb("wq", [P, QW])
        wo = sb("wo", [P, C])
        we1 = sb("we1", [P, 2, C])
        we2 = sb("we2", [P, C])
        wn1 = sb("wn1", [P, 2, C])
        wn2 = sb("wn2", [P, C])
        w1 = sb("w1", [P, C])
        w2 = sb("w2", [P, C])
        wout = sb("wout", [P, 2, C])
        wdb = sb("wdb", [P, H])
        kvq_row = sb("kvq_row", [1, KV + QW])
        be2_row = sb("be2_row", [1, C])
        b2_row = sb("b2_row", [1, C])
        bout_row = sb("bout_row", [1, C])
        be1c = sb("be1c", [P, 1])
        bn1c = sb("bn1c", [P, 1])
        b1c = sb("b1c", [P, 1])
        bo_b = sb("bo_b", [P, C])
        bn2_b = sb("bn2_b", [P, C])
        gamma_b = sb("gamma_b", [P, C])
        beta_b = sb("beta_b", [P, C])

        RS = sb("rows_src", [P, CH, C])
        RD = sb("rows_dst", [P, CH, C])
        RV = sb("rows_val", [P, CH, C])

        gA = sb("gA", [P, U, AW])
        gB = sb("gB", [P, U, AW])
        ibS = sb("ibS", [P, U], i32)
        ibD = sb("ibD", [P, U], i32)
        ibO = sb("ibO", [P, U], i32)
        dgA = sb("dgA", [P, U, P])
        dgB = sb("dgB", [P, U, P])
        sel = sb("sel", [P, U, P])
        wA = sb("wA", [P, U, C])
        wB = sb("wB", [P, U, C])
        hTA = sb("hTA", [P, U, P])
        hTB = sb("hTB", [P, U, P])
        y = sb("y", [P, U, AW])
        msg = gB
        qsb = sb("qsb", [P, 2, QW])
        sct = sb("sct", [P, U, H])
        red = sb("red", [P, U, H])
        oh = sb("oh", [P, U, P])
        oh16 = sb("oh16", [P, U, P], bf16)
        ohv = sb("ohv", [P, 2, TF])
        ohb = sb("ohb", [P, 2, TF], bf16)
        st = sb("st", [P, 2 * U, 6])
        mv = sb("mv", [P, 2 * U, 6])
        sd = sb("sd", [P, 2 * U])
        rs = sb("rs", [P, 2 * U])
        st2 = sb("st2", [P, U, 6])
        mv2 = sb("mv2", [P, U, 6])
        sd2 = sb("sd2", [P, U])
        rs2 = sb("rs2", [P, U])
        rk = sb("rk", [P, U])
        fr = sb("fr", [P, U])
        ml = sb("ml", [P, U])
        tk = sb("tk", [P, U])
        sq = sb("sq", [P, U])
        nr = sb("nr", [P, U])
        dn = sb("dn", [P, U])
        rr = sb("rr", [P, U])
        sqB = sb("sqB", [P, U])
        nrB = sb("nrB", [P, U])
        dnB = sb("dnB", [P, U])
        rrB = sb("rrB", [P, U])

        pb = ctx.enter_context(nc.psum_tensor("pb", [P, 8, 512], f32))

        def bank(b):
            return pb[:, b, :].rearrange("p (u c) -> p u c", u=U)

        def over_rows(row):
            return row.unsqueeze(1).broadcast_to([P, U, C])

        def over_cols(col, n=P):
            return col.unsqueeze(2).broadcast_to([P, U, n])

        s_loaded = sem("loaded")
        s_pool_const = sem("pool_const")
        s_vec_const = sem("vec_const")
        s_pool_chain = sem("pool_chain")
        s_zero = [sem(f"zeroed{i}") for i in range(4)]
        s_hold = sem("pool_held")
        s_vhold = sem("vector_held")
        s_sphold = sem("sync_held")

        shared = {n: sem(n) for n in ("idx gathered_s gathered_d taken diag bcast sel msgs mT mTs y ysb scat yfree "
                                      "oidx var sd hid hids").split()}
        ended = dict.fromkeys(shared, 0)

        def phase_sems(ph, names, share=""):
            p = Phase({n: sem(f"{ph}_{n}") for n in names.split()})
            for n in share.split():
                p[n], p.start[n] = shared[n], ended[n]
                ended[n] += G + (n in ("idx", "taken", "yfree")) if not n.startswith("gathered") and n != "scat" else 16 * U * G
            return p

        p0 = phase_sems("p0", "idx gathered_s gathered_d taken diag bcast xn xT hT kvq copied prod var sd oh tab tabmax chain")
        sm = phase_sems("sm", "hmax allmax shifted exp hsum allsum done chain")
        l0 = phase_sems("l0", "look looked chain", "diag bcast sel msgs mT mTs y ysb scat yfree oidx")
        wx = phase_sems("wx", "shifted exp chain chain2 chain3")
        l1 = phase_sems("l1", "xn xT hT en ens chain", "idx gathered_s gathered_d taken diag bcast sel hid hids "
                        "mT mTs y ysb scat yfree oidx var sd")
        l2 = phase_sems("l2", "u uT uTs x2 chain", "idx gathered_s taken diag bcast sel var sd msgs y ysb scat yfree "
                        "oidx")
        l3 = phase_sems("l3", "sq norm comb cT cTs h2 var2 sd2 h3 chain", "idx gathered_s taken diag bcast sel "
                        "hid hids var sd mT mTs y ysb scat yfree oidx")
        loads = []

        def load(dst, srcap):
            loads.append((dst, srcap))

        col = lambda v: v.rearrange("(p a) -> p a", a=1)
        row = lambda v: v.rearrange("(a n) -> a n", a=1)
        load(srcI[:EP, 0:CH], src.rearrange("(p c) -> p c", p=EP))
        load(dstI[:EP, 0:CH], dst.rearrange("(p c) -> p c", p=EP))
        load(ew[:EP, :], edge_weight.rearrange("(p c) -> p c", p=EP))
        load(wkv[:, 0:C], WkT)
        load(wkv[:, C:2 * C], WvT)
        load(wq[:, 0:C], WqT)
        load(wo[:, :], WoT)
        for k in range(2):
            load(we1[:, k, :], We1[k * C:(k + 1) * C, :])
            load(wn1[:, k, :], Wn1[k * C:(k + 1) * C, :])
            load(wout[:, k, :], WoutT[k * C:(k + 1) * C, :])
        load(we2[:, :], We2)
        load(wn2[:, :], Wn2)
        load(w1[:, :], W1)
        load(w2[:, :], W2)
        load(kvq_row[:, 0:C], row(bk))
        load(kvq_row[:, C:2 * C], row(bv))
        load(kvq_row[:, 2 * C:KV], row(bd))
        load(kvq_row[:, KV:KV + C], row(bq))
        load(be2_row[:, :], row(be2))
        load(b2_row[:, :], row(b2))
        load(bout_row[:, :], row(b_out))
        load(be1c[:, :], col(be1))
        load(bn1c[:, :], col(bn1))
        load(b1c[:, :], col(b1))
        for t, v in ((bo_b, bo), (bn2_b, bn2), (gamma_b, gamma), (beta_b, beta), (wdb, Wd.rearrange("h a -> (h a)"))):
            load(t[:, :], v.partition_broadcast(P))
        NLOAD = 16 * len(loads)
        T = NG // 2

        LB, LC, LD, LF = 2, 4, 6, 7
        R = 8
        TURNS = NG // R
        assert TURNS > 2
        D_COUNTS = dict(s2=8, x1=8, s3=8, xb=4, xn1=2, n3=4, xn4=2, h2=2, hT1=2, hT2=2, hT4=2, u1=2, u2=2,
                        o=4, x=4, s0=4, s1=4, squares=1)
        rows = [t[:, :, :].rearrange("p c f -> p (c f)") for t in (RS, RD, RV)]
        cap = CH * C
        spot = 0

        def place(name, *shape):
            nonlocal spot
            w = 1
            for n in shape:
                w *= n
            if cap < 24 * U * C:
                t = sb(f"d_{name}", [P, *shape])
                return t[tuple([slice(None)] * (len(shape) + 1))]
            if spot // cap != (spot + w - 1) // cap:
                spot = (spot // cap + 1) * cap
            t = rows[spot // cap][:, spot % cap:spot % cap + w]
            spot += w
            return t if len(shape) == 1 else t.rearrange("p (a b) -> p a b", b=shape[1])

        bufs = {name: [place(f"{name}{k}", U, AW if name == "s2" else C) for k in range(count)]
                for name, count in D_COUNTS.items()}
        st16 = [place(f"st16_{k}", 4 * U, 6) for k in range(2)]
        mv16 = [place(f"mv16_{k}", 7, 4 * U) for k in range(2)]
        sd16 = [place(f"sd16_{k}", 4 * U) for k in range(2)]
        sq4 = [place(f"sq4_{k}", U) for k in range(2)]
        nr4 = [place(f"nr4_{k}", U) for k in range(2)]
        dn4 = place("dn4", 2, U)
        rr8 = place("rr8", 2 * R, U)
        dd = phase_sems("d", "x1a var sd rs xn1 xb xbb t1 h1 hid1 u1 m1 x2 sq norm h2 comb cT cTs hid2 u2 h2p n3 x3 "
                        "xn4 t4 h4 o4 osb chain pchain pchain2 pchain3 comb4 set")
        d_in = [sem(f"d_in{k}") for k in range(4)]
        d_in3 = [sem(f"d_in3{k}") for k in range(2)]
        d_out = [sem(f"d_out{k}") for k in range(4)]

        class Group:

            def __init__(self, number, residue, quarter, half):
                self.number, self.residue, self.quarter, self.half = number, residue, quarter, half

            def from_number(self, least):
                return not isinstance(self.number, int) or self.number >= least

        def B(name, n):
            return bufs[name][n.residue % D_COUNTS[name]]

        def slots(engine, slot, last, first=1):
            def straight(s):
                def g(lag):
                    n = s - lag
                    return Group(n, n % R, n // 4, n // 2) if 0 <= n < NG else None
                return g

            for s in range(first * R):
                slot(straight(s), Group(s, s % R, s // 4, s // 2))
            with engine.Fori(first, TURNS) as i:
                for j in range(R):
                    def g(lag, j=j):
                        return Group(i * R + (j - lag), (j - lag) % R, i * (R // 4) + (j - lag) // 4,
                                     i * (R // 2) + (j - lag) // 2)
                    slot(g, g(0))
            for s in range(TURNS * R, last + 1):
                slot(straight(s), Group(s, s % R, s // 4, s // 2))

        def loads_due(n):
            return n.quarter * 64 + 64

        block = ctx.enter_context(nc.Block())

        def rows_of(t, base):
            return t[ds(base, ROWS), :].rearrange("(p u) c -> p u c", u=U)

        @block.sync
        def _(sp):
            sp.wait_ge(s_vec_const, 1)
            for d, s in loads:
                sp.dma_start(d, s, allow_slow_non_contiguous=True).then_inc(s_loaded, 16)
            for k, (t, w) in enumerate(((S0, C), (S1, C), (S2, AW), (S3, C))):
                tv = t.rearrange("(p r) c -> p r c", p=P)
                with sp.Fori(0, TF // ZR) as r:
                    sp.dma_start(tv[:, ds(r * ZR, ZR), :],
                                 zeros[:, 0:w].unsqueeze(1).broadcast_to([P, ZR, w])).then_inc(s_zero[k], 16)
            sp.wait_ge(l3["yfree"], l3.due("yfree", G + 1))

            def base_of(n):
                return bases[n.number] if isinstance(n.number, int) else n.number * ROWS

            def hold(s, v):
                sp.wait_ge(s, v)
                sp.sem_inc(s_sphold, 1)

            def fetch(n):
                for name, t in (("x", x), ("s0", S0), ("s1", S1), ("s2", S2)):
                    sp.dma_start(B(name, n), rows_of(t, base_of(n))).then_inc(d_in[n.residue % 4], 16)

            def store(n):
                hold(dd["osb"], n.number + 1)
                if isinstance(n.number, int) and n.number == NG - 1:
                    for k in range(4):
                        sp.wait_ge(d_out[k], 16 * len(range(k, NG - 1, 4)))
                sp.dma_start(rows_of(out, base_of(n)), B("o", n)).then_inc(d_out[n.residue % 4], 16)

            def sp_slot(g, now):
                if (n := g(0)) is not None:
                    if n.from_number(4):
                        hold(dd["x1a"], n.number - 3)
                        hold(dd["hid1"], n.number - 3)
                    if n.from_number(8):
                        hold(dd["comb"], n.number - 7)
                    fetch(n)
                if (n := g(LD - 2)) is not None:
                    if n.from_number(8):
                        hold(dd["comb4"], n.number - 7)
                    sp.dma_start(B("s3", n), rows_of(S3, base_of(n))).then_inc(d_in3[n.residue % 2], 16)
                if (n := g(SL)) is not None:
                    store(n)

            SL = LF + 3
            slots(sp, sp_slot, NG - 1 + SL, 2)
            for k in range(4):
                sp.wait_ge(d_out[k], 16 * len(range(k, NG, 4)))

        def at(c):
            return bass.IndirectOffsetOnAxis(ap=c, axis=0)

        @block.gpsimd
        def _(pool):
            def hold(s, v):
                pool.wait_ge(s, v)
                pool.sem_inc(s_hold, 1)

            pool.memset(ident[:, :], 1.0)
            pool.memset(ltri[:, :], 1.0)
            pool.memset(ones[:, :], 1.0).then_inc(s_pool_chain, 1)
            pool.wait_ge(s_pool_chain, 1)
            pool.affine_select(out=ident[:, :], in_=ident[:, :], compare_op=ALU.is_equal, fill=0.0, base=0,
                               pattern=[[-1, P]], channel_multiplier=1)
            pool.affine_select(out=ltri[:, :], in_=ltri[:, :], compare_op=ALU.is_gt, fill=0.0, base=0,
                               pattern=[[-1, P]], channel_multiplier=1)
            pool.iota(iota_f[:, :], pattern=[[1, max(TF, P)]], base=0, channel_multiplier=0,
                      allow_small_or_imprecise_dtypes=True)
            pool.iota(iota_p[:, :], pattern=[[0, 1]], base=0, channel_multiplier=1,
                      allow_small_or_imprecise_dtypes=True)
            pool.iota(trash[:, :], pattern=[[0, 1]], base=N, channel_multiplier=1,
                      allow_small_or_imprecise_dtypes=True).then_inc(s_pool_const, 1)

            def gather(s, buf, width, table_ap, idx):
                for u in range(U):
                    pool.indirect_dma_start(out=buf[:, u, 0:width], out_offset=None, in_=table_ap,
                                            in_offset=at(idx[:, u:u + 1])).then_inc(s, 16)

            def scatter(ph, g, table_ap, width, idx):
                hold(ph["ysb"], ph.due("ysb", g + 1))
                hold(ph["oidx"], ph.due("oidx", g + 1))
                for u in range(U):
                    pool.indirect_dma_start(out=table_ap, out_offset=at(idx[:, u:u + 1]), in_=y[:, u, 0:width],
                                            in_offset=None, compute_op=ALU.add).then_inc(ph["scat"], 16)
                    hold(ph["scat"], ph.due("scat", 16 * U * g + 16 * (u + 1)))
                pool.sem_inc(ph["yfree"], 1)

            with pool.Fori(0, G) as g:
                hold(p0["taken"], p0.due("taken", g + 1))
                hold(p0["idx"], p0.due("idx", g + 1))
                gather(p0["gathered_s"], gA, C, x, ibS)
                gather(p0["gathered_d"], gB, C, x, ibD)
            pool.wait_ge(sm["hmax"], sm.due("hmax", 1))
            pool.partition_all_reduce(hall[:, :], hmax[:, :], P, bass.bass_isa.ReduceOp.max).then_inc(sm["allmax"], 1)
            pool.wait_ge(sm["hsum"], sm.due("hsum", 1))
            pool.partition_all_reduce(hall[:, :], hsum[:, :], P, bass.bass_isa.ReduceOp.add).then_inc(sm["allsum"], 1)
            pool.sem_inc(l0["yfree"], 1)
            hold(s_zero[0], 16 * (TF // ZR))
            with pool.Fori(0, G) as g:
                scatter(l0, g, S0, C, ibO)
            def gather1(g):
                hold(l1["taken"], l1.due("taken", g + 1))
                hold(l1["idx"], l1.due("idx", g + 1))
                gather(l1["gathered_s"], gA, C, S0, ibS)
                gather(l1["gathered_d"], gB, C, S0, ibD)

            pool.sem_inc(l1["yfree"], 1)
            hold(s_zero[1], 16 * (TF // ZR))
            gather1(0)
            with pool.Fori(0, G - 1) as g:
                gather1(g + 1)
                scatter(l1, g, S1, C, ibO)
            scatter(l1, G - 1, S1, C, ibO)

            def gather_one(ph, g, width, table_ap):
                hold(ph["taken"], ph.due("taken", g + 1))
                hold(ph["idx"], ph.due("idx", g + 1))
                gather(ph["gathered_s"], gA, width, table_ap, ibS)

            for ph, zero, source, w_in, target, w_out in ((l2, s_zero[2], S1, C, S2, AW), (l3, s_zero[3], S2, AW, S3, C)):
                pool.sem_inc(ph["yfree"], 1)
                hold(zero, 16 * (TF // ZR))
                gather_one(ph, 0, w_in, source)
                with pool.Fori(0, G - 1) as g:
                    gather_one(ph, g + 1, w_in, source)
                    scatter(ph, g, target, w_out, ibO)
                scatter(ph, G - 1, target, w_out, ibO)

            def attend(n):
                pool.wait_ge(d_in[n.residue % 4], loads_due(n))
                pool.tensor_tensor(B("x1", n), B("x", n), B("s0", n), ALU.add).then_inc(dd["pchain"], 1)
                pool.wait_ge(dd["pchain"], n.number + 1)
                pool.tensor_tensor(B("x1", n), B("x1", n), over_rows(bo_b[:, :]), ALU.add).then_inc(dd["x1a"], 1)

            def pool_slot(g, now):
                if (n := g(-1)) is not None:
                    if n.from_number(8):
                        pool.wait_ge(dd["comb4"], n.number - 7)
                        pool.sem_inc(s_hold, 1)
                    attend(n)
                if (n := g(0)) is not None:
                    pool.wait_ge(dd["xb"], n.number + 1)
                    pool.tensor_tensor(B("xb", n), B("xb", n), over_rows(bn2_b[:, :]), ALU.add).then_inc(dd["xbb"], 1)
                if (n := g(LC)) is not None:
                    pool.wait_ge(dd["n3"], n.number + 1)
                    pool.tensor_tensor(B("n3", n), B("n3", n), over_rows(gamma_b[:, :]), ALU.mult)\
                        .then_inc(dd["pchain2"], 1)
                    pool.wait_ge(dd["pchain2"], n.number + 1)
                    pool.tensor_tensor(B("n3", n), B("n3", n), over_rows(beta_b[:, :]), ALU.add)\
                        .then_inc(dd["pchain3"], 1)
                    pool.wait_ge(dd["pchain3"], n.number + 1)
                    pool.tensor_tensor(B("x1", n), B("x1", n), B("n3", n), ALU.add).then_inc(dd["x3"], 1)

            attend(Group(0, 0, 0, 0))
            slots(pool, pool_slot, NG - 1 + LC)

        @block.scalar
        def _(act):
            def relu(o, i, bias=0.0):
                return act.activation(o, i, ACT.Relu, bias=bias)

            def cp(o, i):
                return act.activation(o, i, ACT.Copy)

            def root(o, i):
                return act.activation(o, i, ACT.Sqrt, bias=eps[:, 0:1])

            def sd_step(ph, want, done, g, o, i):
                act.wait_ge(ph[want], ph.due(want, g + 1))
                root(o, i).then_inc(ph[done], 1)

            act.wait_ge(s_loaded, NLOAD)
            act.wait_ge(s_vec_const, 2)
            with act.Fori(0, G) as g:
                sd_step(p0, "var", "sd", g, sd[:, :], mv[:, :, 1])
                act.wait_ge(p0["xT"], p0.due("xT", g + 1))
                relu(hTA[:, :, :], bank(0))
                relu(hTB[:, :, :], bank(1)).then_inc(p0["hT"], 1)
                for u in range(U):
                    act.wait_ge(p0["kvq"], p0.due("kvq", U * g + u + 1))
                    cp(RV[:, ds(U * g + u, 1), :].rearrange("p a c -> p (a c)"), pb[:, 2 + u % 2, C:2 * C])
                    if u >= 2:
                        act.wait_ge(p0["prod"], p0.due("prod", U * g + u - 1))
                    cp(qsb[:, u % 2, :], pb[:, 2 + u % 2, KV:KV + QW]).then_inc(p0["copied"], 1)
            act.wait_ge(sm["shifted"], sm.due("shifted", 1))
            act.activation(scores[:, :, :], scores[:, :, :], ACT.Exp).then_inc(sm["exp"], 1)

            def copy_sums(ph, g, mid, src_bank, dst):
                act.wait_ge(ph[mid], ph.due(mid, g + 1))
                cp(dst, bank(src_bank)).then_inc(ph[mid + "s"], 1)

            def put_y(ph, g, b):
                act.wait_ge(ph["y"], ph.due("y", g + 1))
                act.wait_ge(ph["yfree"], ph.due("yfree", g + 1))
                cp(y[:, :, 0:C], bank(b)).then_inc(ph["ysb"], 1)

            with act.Fori(0, G) as g:
                copy_sums(l0, g, "mT", 0, hTA[:, :, :])
                put_y(l0, g, 1)
            act.wait_ge(wx["shifted"], wx.due("shifted", 1))
            act.activation(wexp[:, :], segmax[:, :], ACT.Exp).then_inc(wx["exp"], 1)
            with act.Fori(0, G) as g:
                sd_step(l1, "var", "sd", g, sd[:, :], mv[:, :, 1])
                act.wait_ge(l1["xT"], l1.due("xT", g + 1))
                relu(hTA[:, :, :], bank(0))
                relu(hTB[:, :, :], bank(1)).then_inc(l1["hT"], 1)
                act.wait_ge(l1["hid"], l1.due("hid", g + 1))
                cp(RV[:, ds(U * g, U), :], bank(3))
                relu(hTB[:, :, :], bank(2), be1c[:, 0:1]).then_inc(l1["hids"], 1)
                copy_sums(l1, g, "en", 6, oh[:, :, :])
                copy_sums(l1, g, "mT", 7, hTA[:, :, :])
                put_y(l1, g, 6)
            with act.Fori(0, G) as g:
                act.wait_ge(l2["uT"], l2.due("uT", g + 1))
                relu(hTA[:, :, :], bank(0), bn1c[:, 0:1]).then_inc(l2["uTs"], 1)
                sd_step(l2, "var", "sd", g, sd[:, 0:U], mv[:, 0:U, 1])
                act.wait_ge(l2["y"], l2.due("y", g + 1))
                act.wait_ge(l2["yfree"], l2.due("yfree", g + 1))
                for b in range(2):
                    last = cp(y[:, 2 * b:2 * b + 2, :], pb[:, 2 + b, 0:2 * AW].rearrange("p (u c) -> p u c", u=2))
                last.then_inc(l2["ysb"], 1)
            with act.Fori(0, G) as g:
                act.wait_ge(l3["sq"], l3.due("sq", g + 1))
                act.activation(nr[:, :], sq[:, :], ACT.Sqrt).then_inc(l3["norm"], 1)
                copy_sums(l3, g, "cT", 0, hTA[:, :, :])
                act.wait_ge(l3["hid"], l3.due("hid", g + 1))
                relu(hTB[:, :, :], bank(1), b1c[:, 0:1]).then_inc(l3["hids"], 1)
                sd_step(l3, "var", "sd", g, sd[:, 0:U], mv[:, 0:U, 1])
                sd_step(l3, "var2", "sd2", g, sd2[:, :], mv2[:, :, 1])
                copy_sums(l3, g, "mT", 0, hTA[:, :, :])
                put_y(l3, g, 1)

            def act_slot(g, now):
                if (n := g(LB)) is not None:
                    act.wait_ge(d_in[n.residue % 4], loads_due(n))
                    for u in range(U):
                        ins = act.activation(B("squares", n)[:, u, :], B("s2", n)[:, u, 0:C], ACT.Square,
                                             accum_out=sq4[n.residue % 2][:, u:u + 1])
                    ins.then_inc(dd["sq"], 1)
                    act.wait_ge(dd["sq"], n.number + 1)
                    act.activation(nr4[n.residue % 2][:, :], sq4[n.residue % 2][:, :], ACT.Sqrt).then_inc(dd["norm"], 1)
                par = now.residue % 2
                m = mv16[par]
                act.wait_ge(dd["var"], now.number + 1)
                root(sd16[par][:, :], m[:, 1, :]).then_inc(dd["sd"], 1)
                act.wait_ge(dd["rs"], now.number + 1)
                if (n := g(LB)) is not None:
                    for u in range(U):
                        t = U + u
                        ins = act.activation(B("h2", n)[:, u, :], B("x1", n)[:, u, :], ACT.Relu,
                                             scale=m[:, 2, t:t + 1], bias=m[:, 3, t:t + 1])
                    ins.then_inc(dd["h2"], 1)
                if (n := g(0)) is not None:
                    act.wait_ge(dd["t1"], n.number + 1)
                    relu(B("hT1", n), bank(0)).then_inc(dd["h1"], 1)
                if (n := g(LD)) is not None:
                    act.wait_ge(dd["t4"], n.number + 1)
                    relu(B("hT4", n), bank(6)).then_inc(dd["h4"], 1)
                if (n := g(LB + 1)) is not None:
                    act.wait_ge(dd["hid2"], n.number + 1)
                    relu(B("u2", n), bank(4), b1c[:, 0:1]).then_inc(dd["u2"], 1)
                if (n := g(LC)) is not None:
                    for u in range(U):
                        t = 2 * U + u
                        ins = act.activation(B("n3", n)[:, u, :], bank(5)[:, u, :], ACT.Identity,
                                             scale=m[:, 2, t:t + 1], bias=m[:, 3, t:t + 1])
                    ins.then_inc(dd["n3"], 1)
                if (n := g(0)) is not None:
                    act.wait_ge(dd["hid1"], n.number + 1)
                    relu(B("u1", n), bank(1), bn1c[:, 0:1]).then_inc(dd["u1"], 1)
                if (n := g(LB)) is not None:
                    act.wait_ge(dd["cT"], n.number + 1)
                    cp(B("hT2", n), bank(3)).then_inc(dd["cTs"], 1)

            slots(act, act_slot, NG - 1 + LF)

        @block.tensor
        def _(pe):
            def transposes(b, tiles, done):
                for u in range(U):
                    last = pe.transpose(bank(b)[:, u, :], tiles[:, u, 0:P], ident[:, :])
                last.then_inc(done, 1)

            def bcast(b, dg):
                return pe.matmul(pb[:, b, :], ones[:, :], dg[:, :, :], start=True, stop=True)

            def stationary(b, w, rhs):
                return pe.matmul(pb[:, b, :], w, rhs, start=True, stop=True)

            def per_tile(b, lhs, rhs, bias=None):
                if bias is not None:
                    pe.matmul(pb[:, b, :], ones[0:1, :], bias[0:1, :].unsqueeze(1).broadcast_to([1, U, C]), start=True, stop=False, skip_group_check=True)
                for u in range(U):
                    last = pe.matmul(bank(b)[:, u, :], lhs[:, u, 0:P], rhs[:, u, :] if len(rhs.shape) == 3 else rhs,
                                     start=bias is None, stop=True, skip_group_check=True)
                return last

            pe.wait_ge(s_loaded, NLOAD)
            pe.wait_ge(s_pool_const, 1)
            pe.wait_ge(s_vec_const, 2)

            with pe.Fori(0, G) as g:
                def kvq(u):
                    b = 2 + u % 2
                    if u >= 2:
                        pe.wait_ge(p0["copied"], p0.due("copied", U * g + u - 1))
                        pe.wait_ge(p0["prod"], p0.due("prod", U * g + u - 1))
                    pe.matmul(pb[:, b, 0:KV + QW], ones[0:1, :], kvq_row[0:1, :], start=True, stop=False,
                              skip_group_check=True)
                    pe.matmul(pb[:, b, 0:KV], hTB[:, u, :], wkv[:, :], start=False, stop=True, skip_group_check=True)
                    pe.matmul(pb[:, b, KV:KV + QW], hTA[:, u, :], wq[:, :], start=False, stop=True,
                              skip_group_check=True).then_inc(p0["kvq"], 1)

                def tab(u):
                    b = 6 + u % 2
                    pe.wait_ge(p0["oh"], p0.due("oh", U * g + u + 1))
                    if u >= 2:
                        pe.wait_ge(p0["tabmax"], p0.due("tabmax", U * g + u - 1))
                    o = pb[:, b, 0:TF]
                    pe.matmul(o, ones16[0:1, :], far_row[0:1, :], start=True, stop=False)
                    pe.matmul(o, oh16[:, u, :], ohb[:, u % 2, :], start=False, stop=False)
                    pe.matmul(o, oh[:, u, :], ohv[:, u % 2, :], start=False, stop=True).then_inc(p0["tab"], 1)

                pe.wait_ge(p0["diag"], p0.due("diag", g + 1))
                bcast(4, dgA)
                bcast(5, dgB).then_inc(p0["bcast"], 1)
                pe.wait_ge(p0["xn"], p0.due("xn", g + 1))
                for b, t in ((0, wA), (1, wB)):
                    for u in range(U):
                        last = pe.transpose(bank(b)[:, u, :], t[:, u, :], ident[:, :])
                last.then_inc(p0["xT"], 1)
                pe.wait_ge(p0["hT"], p0.due("hT", g + 1))
                kvq(0)
                kvq(1)
                for u in range(U):
                    tab(u)
                kvq(2)
                kvq(3)

            def sums(ph, g, out_bank, rhs):
                pe.wait_ge(ph["mTs"], ph.due("mTs", g + 1))
                per_tile(out_bank, hTA, rhs).then_inc(ph["y"], 1)

            with pe.Fori(0, G) as g:
                pe.wait_ge(l0["diag"], l0.due("diag", g + 1))
                bcast(4, dgA)
                bcast(5, dgB).then_inc(l0["bcast"], 1)
                pe.wait_ge(l0["sel"], l0.due("sel", g + 1))
                for u in range(U):
                    if u >= 2:
                        pe.wait_ge(l0["looked"], l0.due("looked", U * g + u - 1))
                    pe.matmul(pb[:, 6 + u % 2, 0:TF], oh[:, u, :], table[:, :], start=True, stop=True)\
                      .then_inc(l0["look"], 1)
                pe.wait_ge(l0["msgs"], l0.due("msgs", g + 1))
                per_tile(0, wA, sel).then_inc(l0["mT"], 1)
                sums(l0, g, 1, wo[:, :])

            def select(ph, g, b):
                pe.wait_ge(ph["diag"], ph.due("diag", g + 1))
                bcast(b, dgA).then_inc(ph["bcast"], 1)

            with pe.Fori(0, G) as g:
                select(l1, g, 4)
                pe.wait_ge(l1["xn"], l1.due("xn", g + 1))
                for b, t in ((0, wA), (1, wB)):
                    for u in range(U):
                        last = pe.transpose(bank(b)[:, u, :], t[:, u, :], ident[:, :])
                last.then_inc(l1["xT"], 1)
                pe.wait_ge(l1["hT"], l1.due("hT", g + 1))
                pe.matmul(pb[:, 2, :], we1[:, 0, :], hTA[:, :, :], start=True, stop=False)
                pe.matmul(pb[:, 2, :], we1[:, 1, :], hTB[:, :, :], start=False, stop=True)
                per_tile(3, hTA, wn1[:, 0, :]).then_inc(l1["hid"], 1)
                pe.wait_ge(l1["hids"], l1.due("hids", g + 1))
                per_tile(6, hTB, we2[:, :], be2_row).then_inc(l1["en"], 1)
                pe.wait_ge(l1["ens"], l1.due("ens", g + 1))
                pe.wait_ge(l1["sel"], l1.due("sel", g + 1))
                per_tile(7, oh, sel).then_inc(l1["mT"], 1)
                sums(l1, g, 6, wn1[:, 1, :])
            with pe.Fori(0, G) as g:
                select(l2, g, 4)
                pe.wait_ge(l2["u"], l2.due("u", g + 1))
                transposes(0, wA, l2["uT"])
                pe.wait_ge(l2["uTs"], l2.due("uTs", g + 1))
                per_tile(1, hTA, wn2[:, :]).then_inc(l2["x2"], 1)
                pe.wait_ge(l2["sel"], l2.due("sel", g + 1))
                pe.wait_ge(l2["msgs"], l2.due("msgs", g + 1))
                for u in range(U):
                    last = pe.matmul(pb[:, 2 + u // 2, AW * (u % 2):AW * (u % 2) + AW], sel[:, u, :], msg[:, u, :],
                                     start=True, stop=True, skip_group_check=True)
                last.then_inc(l2["y"], 1)
            with pe.Fori(0, G) as g:
                select(l3, g, 4)
                pe.wait_ge(l3["comb"], l3.due("comb", g + 1))
                transposes(0, wA, l3["cT"])
                pe.wait_ge(l3["cTs"], l3.due("cTs", g + 1))
                stationary(1, w1[:, :], hTA[:, :, :]).then_inc(l3["hid"], 1)
                pe.wait_ge(l3["hids"], l3.due("hids", g + 1))
                per_tile(2, hTB, w2[:, :], b2_row).then_inc(l3["h2"], 1)
                pe.wait_ge(l3["sel"], l3.due("sel", g + 1))
                pe.wait_ge(l3["h3"], l3.due("h3", g + 1))
                per_tile(0, wB, sel).then_inc(l3["mT"], 1)
                sums(l3, g, 1, wout[:, 1, :])

            def tr(b, tiles):
                for u in range(U):
                    last = pe.transpose(bank(b)[:, u, :], tiles[:, u, :], ident[:, :])
                return last

            def pe_slot(g, now):
                if (n := g(LD + 1)) is not None:
                    pe.wait_ge(dd["h4"], n.number + 1)
                    if n.from_number(1):
                        pe.wait_ge(dd["osb"], n.number)
                    per_tile(7, B("hT4", n), wout[:, 0, :], bout_row).then_inc(dd["o4"], 1)
                if (n := g(LB + 1)) is not None:
                    pe.wait_ge(dd["cTs"], n.number + 1)
                    stationary(4, w1[:, :], B("hT2", n)).then_inc(dd["hid2"], 1)
                if (n := g(0)) is not None:
                    pe.wait_ge(dd["xn1"], n.number + 1)
                    tr(0, B("xn1", n)).then_inc(dd["t1"], 1)
                if (n := g(LD)) is not None:
                    pe.wait_ge(dd["xn4"], n.number + 1)
                    tr(6, B("xn4", n)).then_inc(dd["t4"], 1)
                if (n := g(1)) is not None:
                    pe.wait_ge(dd["u1"], n.number + 1)
                    if n.from_number(1):
                        pe.wait_ge(dd["x2"], n.number)
                    per_tile(2, B("u1", n), wn2[:, :]).then_inc(dd["m1"], 1)
                if (n := g(0)) is not None:
                    pe.wait_ge(dd["h1"], n.number + 1)
                    pe.wait_ge(d_in[n.residue % 4], loads_due(n))
                    pe.matmul(pb[:, 1, :], wn1[:, 0, :], B("hT1", n), start=True, stop=False, skip_group_check=True)
                    for u in range(U):
                        last = pe.matmul(bank(1)[:, u, :], B("s1", n)[:, u, :], ident[:, :], start=False,
                                         stop=True, skip_group_check=True)
                    last.then_inc(dd["hid1"], 1)
                if (n := g(LB + 1)) is not None:
                    pe.wait_ge(dd["u2"], n.number + 1)
                    if n.from_number(1):
                        pe.wait_ge(dd["n3"], n.number)
                    per_tile(5, B("u2", n), w2[:, :], b2_row).then_inc(dd["h2p"], 1)
                if (n := g(LB)) is not None:
                    pe.wait_ge(dd["comb"], n.number + 1)
                    tr(3, B("h2", n)).then_inc(dd["cT"], 1)

            slots(pe, pe_slot, NG + LD)

        @block.vector
        def _(v):
            tt, ts, stt = v.tensor_tensor, v.tensor_scalar, v.scalar_tensor_tensor

            def stats(chain, tiles, st_, mv_, ph, want, n):
                for t in range(n):
                    ins = v.bn_stats(st_[:, t, :], tiles[t])
                chain(ins)
                f = lambda j: st_[:, 0:n, j]
                tt(mv_[:, 0:n, 2], f(1), f(4), ALU.add)
                tt(mv_[:, 0:n, 3], f(1), f(4), ALU.subtract)
                chain(tt(mv_[:, 0:n, 4], f(2), f(5), ALU.add))
                ts(mv_[:, 0:n, 0], mv_[:, 0:n, 2], 0.5, None, ALU.mult)
                chain(stt(out=mv_[:, 0:n, 5], in0=mv_[:, 0:n, 3], scalar=0.25, in1=mv_[:, 0:n, 3],
                          op0=ALU.mult, op1=ALU.mult))
                stt(out=mv_[:, 0:n, 1], in0=mv_[:, 0:n, 4], scalar=1.0 / C, in1=mv_[:, 0:n, 5],
                    op0=ALU.mult, op1=ALU.add).then_inc(ph[want], 1)

            def normalize(chain, ph, done, g, outs, tiles, mv_, sd_, rs_, n):
                v.wait_ge(ph[done], ph.due(done, g + 1))
                chain(v.reciprocal(rs_[:, 0:n], sd_[:, 0:n]))
                for t in range(n):
                    ins = v.tensor_scalar(outs[t], tiles[t], mv_[:, t, 0:1], rs_[:, t:t + 1], ALU.subtract, ALU.mult)
                return ins


            v.memset(srcI[:, :], 0)
            v.memset(dstI[:, :], 0)
            v.memset(ew[:, :], 0.0)
            v.memset(kvq_row[:, :], 0.0)
            v.memset(zeros[:, :], 0.0).then_inc(s_vec_const, 1)
            v.memset(ones16[:, :], 1.0)
            v.memset(far_row[:, :], -ABSENT)
            v.memset(table[:, :], -ABSENT)
            v.memset(eps[:, :], LN_EPS)
            setup = Chain(v, sem("vec_setup"), 12)
            setup.step(0)
            v.wait_ge(s_loaded, NLOAD)
            v.wait_ge(s_pool_const, 1)
            setup(ts(not_edge[:, :], iota_p[:, :], float(EP), None, ALU.is_ge))
            setup(tt(rr[:, 0:1], not_edge[:, :], trash[:, :], ALU.mult))
            setup(ts(keyS[:, :], srcI[:, 0:CH], rr[:, 0:1], None, ALU.add))
            setup(ts(keyD[:, :], dstI[:, 0:CH], rr[:, 0:1], None, ALU.add))
            setup(v.tensor_copy(keyI, keyD[:, :]))
            setup(ts(pI, keyI, P - 1, None, ALU.bitwise_and))
            setup(ts(fI, keyI, 7, None, ALU.arith_shift_right))
            setup(v.tensor_copy(keyp[:, :], pI))
            setup(v.tensor_copy(keyf[:, :], fI))
            setup(ts(wkv[:, 2 * C:KV], wdb[:, :], 1.0 / C, None, ALU.mult))
            setup(ts(wq[:, C:QW], wdb[:, :], -1.0 / C, None, ALU.mult))
            v.tensor_copy(ibS[:, :], srcI[:, 0:U])
            setup(v.tensor_copy(ibD[:, :], dstI[:, 0:U]))
            setup.end()
            v.sem_inc(s_vec_const, 1)
            v.sem_inc(p0["taken"], 1)
            v.sem_inc(p0["idx"], 1)

            def cols(t, g):
                return t[:, ds(U * g, U)]

            def diag(dg, keys):
                return tt(dg[:, :, :], ident[:, :].unsqueeze(1).broadcast_to([P, U, P]), over_cols(keys), ALU.mult)

            def next_idx(ph, g, both_ends):
                ins = v.tensor_copy(ibS[:, :], srcI[:, ds(U * g + U, U)])
                if both_ends:
                    ins = v.tensor_copy(ibD[:, :], dstI[:, ds(U * g + U, U)])
                ins.then_inc(ph["idx"], 1)

            c = Chain(v, p0["chain"], 13 + 3 * U)
            with v.Fori(0, G) as g:
                c.step(g)
                diag(dgA, cols(keyD, g))
                diag(dgB, cols(ew, g)).then_inc(p0["diag"], 1)
                v.wait_ge(p0["gathered_s"], p0.due("gathered_s", 16 * U * g + 16 * U))
                v.wait_ge(p0["gathered_d"], p0.due("gathered_d", 16 * U * g + 16 * U))
                next_idx(p0, g, True)
                v.tensor_copy(RS[:, ds(U * g, U), :], gA[:, :, 0:C])
                ins = v.tensor_copy(RD[:, ds(U * g, U), :], gB[:, :, 0:C])
                c(ins)
                v.sem_inc(p0["taken"], 1)
                tiles = [RS[:, ds(U * g + u, 1), :].rearrange("p a c -> p (a c)") for u in range(U)] + \
                        [RD[:, ds(U * g + u, 1), :].rearrange("p a c -> p (a c)") for u in range(U)]
                stats(c, tiles, st, mv, p0, "var", 2 * U)
                normalize(c, p0, "sd", g, [wA[:, u, :] for u in range(U)] + [wB[:, u, :] for u in range(U)],
                          tiles, mv, sd, rs, 2 * U).then_inc(p0["xn"], 1)
                v.wait_ge(p0["bcast"], p0.due("bcast", g + 1))
                c(tt(sel[:, :, :], bank(4), over_cols(cols(keyD, g)), ALU.not_equal))
                c(stt(out=dgB[:, :, 0:C], in0=sel[:, :, :], scalar=-FAR, in1=bank(5), op0=ALU.mult, op1=ALU.add))
                c(v.tensor_reduce(out=ml[:, :], in_=dgB[:, :, 0:C], axis=AX.X, op=ALU.max))
                c(stt(out=dgA[:, :, :], in0=sel[:, :, :], scalar=0.0, in1=ltri[:, :].unsqueeze(1).broadcast_to([P, U, P]),
                      op0=ALU.is_equal, op1=ALU.mult))
                c(v.tensor_reduce(out=rk[:, :], in_=dgA[:, :, :], axis=AX.X, op=ALU.add))
                v.tensor_copy(cols(rankD, g), rk[:, :])
                c(ts(fr[:, :], rk[:, :], 0.0, None, ALU.is_equal))
                for u in range(U):
                    cc = ds(U * g + u, 1)
                    ins = ts(oh[:, u, :], iota_f[:, 0:P], keyp[:, cc], fr[:, u:u + 1], ALU.is_equal, ALU.mult)
                c(ins)
                v.tensor_copy(oh16[:, :, :], oh[:, :, :])

                def table_max(u):
                    v.wait_ge(p0["tab"], p0.due("tab", U * g + u + 1))
                    c(tt(table[:, :], pb[:, 6 + u % 2, 0:TF], table[:, :], ALU.max))
                    v.sem_inc(p0["tabmax"], 1)

                for u in range(U):
                    cc = ds(U * g + u, 1)
                    if u >= 2:
                        table_max(u - 2)
                    ts(ohv[:, u % 2, :], iota_f[:, 0:TF], keyf[:, cc], ml[:, u:u + 1], ALU.is_equal, ALU.mult)
                    ts(ohb[:, u % 2, :], iota_f[:, 0:TF], keyf[:, cc], ABSENT, ALU.is_equal, ALU.mult)\
                        .then_inc(p0["oh"], 1)
                table_max(2)
                table_max(3)
                for u in range(U):
                    b = 2 + u % 2
                    cc = ds(U * g + u, 1)
                    v.wait_ge(p0["copied"], p0.due("copied", U * g + u + 1))
                    c(tt(dgA[:, u, :], pb[:, b, 0:C], qsb[:, u % 2, 0:C], ALU.mult))
                    c(stt(out=sct[:, u, :], in0=pb[:, b, 2 * C:KV], scalar=ew[:, cc], in1=qsb[:, u % 2, C:QW],
                          op0=ALU.add, op1=ALU.add))
                    v.sem_inc(p0["prod"], 1)
                c(v.tensor_reduce(out=red[:, :, :].rearrange("p u h -> p (u h)"),
                                  in_=dgA[:, :, :].rearrange("p u (h d) -> p (u h) d", d=HD), axis=AX.X, op=ALU.add))
                stt(out=scores[:, ds(U * g, U), :], in0=red[:, :, :], scalar=SCALE, in1=sct[:, :, :],
                    op0=ALU.mult, op1=ALU.add)
                c.end()
            c = Chain(v, sm["chain"], 12)
            c.step(0)

            def indices(rank, key, t):
                c(ts(rank, rank, 1.0, None, ALU.min))
                c(ts(t, key, -1.0, trash[:, 0:1], ALU.mult, ALU.add))
                c(tt(t, t, rank, ALU.mult))
                c(tt(t, t, key, ALU.add))

            indices(rankD[:, :], keyD[:, :], tmpc[:, :])
            c(v.tensor_copy(idxD[:, :], tmpc[:, :]))
            c(ts(rr[:, 0:1], not_edge[:, :], -FAR, None, ALU.mult))
            c(ts(scores[:, :, :], scores[:, :, :], rr[:, 0:1], None, ALU.add))
            v.tensor_reduce(out=hmax[:, :], in_=scores[:, :, :].rearrange("p c h -> p h c"), axis=AX.X, op=ALU.max)\
                .then_inc(sm["hmax"], 1)
            over_edges = lambda t: t[:, :].unsqueeze(1).broadcast_to([P, CH, H])
            v.wait_ge(sm["allmax"], sm.due("allmax", 1))
            tt(scores[:, :, :], scores[:, :, :], over_edges(hall), ALU.subtract).then_inc(sm["shifted"], 1)
            v.wait_ge(sm["exp"], sm.due("exp", 1))
            v.tensor_reduce(out=hsum[:, :], in_=scores[:, :, :].rearrange("p c h -> p h c"), axis=AX.X, op=ALU.add)\
                .then_inc(sm["hsum"], 1)
            v.wait_ge(sm["allsum"], sm.due("allsum", 1))
            c(v.reciprocal(hrec[:, :], hall[:, :]))
            c(tt(scores[:, :, :], scores[:, :, :], over_edges(hrec), ALU.mult))

            sc_end = c
            c = Chain(v, l0["chain"], 6)
            with v.Fori(0, G) as g:
                c.step(g)
                diag(dgA, cols(keyS, g))
                diag(dgB, cols(keyp, g)).then_inc(l0["diag"], 1)
                v.wait_ge(l0["bcast"], l0.due("bcast", g + 1))
                tt(wA[:, :, :].rearrange("p u (h d) -> p (u h) d", d=HD),
                   RV[:, ds(U * g, U), :].rearrange("p u (h d) -> p (u h) d", d=HD),
                   scores[:, ds(U * g, U), :].rearrange("p u h -> p (u h)").unsqueeze(2).broadcast_to([P, U * H, HD]),
                   ALU.mult).then_inc(l0["msgs"], 1)
                ts(oh[:, :, :], bank(5), iota_p[:, 0:1], None, ALU.is_equal)
                ins = tt(sel[:, :, :], bank(4), over_cols(cols(keyS, g)), ALU.is_equal)
                ins.then_inc(l0["sel"], 1)
                v.wait_ge(l0["sel"], l0.due("sel", g + 1))
                c(tt(dgA[:, :, :], sel[:, :, :], ltri[:, :].unsqueeze(1).broadcast_to([P, U, P]), ALU.mult))
                c(v.tensor_reduce(out=rk[:, :], in_=dgA[:, :, :], axis=AX.X, op=ALU.add))
                for u in range(U):
                    v.wait_ge(l0["look"], l0.due("look", U * g + u + 1))
                    stt(out=ohv[:, u % 2, :], in0=iota_f[:, 0:TF], scalar=keyf[:, ds(U * g + u, 1)],
                        in1=pb[:, 6 + u % 2, 0:TF], op0=ALU.is_equal, op1=ALU.mult, accum_out=ml[:, u:u + 1])\
                        .then_inc(l0["looked"], 1)
                v.wait_ge(l0["looked"], l0.due("looked", U * g + U))
                v.tensor_copy(cols(segmax, g), ml[:, :])
                indices(rk[:, :], cols(keyS, g), fr[:, :])
                v.wait_ge(l0["yfree"], l0.due("yfree", g + 1))
                v.tensor_copy(ibO[:, :], fr[:, :]).then_inc(l0["oidx"], 1)
                c.end()
            c = Chain(v, wx["chain"], 1)
            c.step(0)
            tt(segmax[:, :], ew[:, :], segmax[:, :], ALU.subtract).then_inc(wx["shifted"], 1)
            v.wait_ge(wx["exp"], wx.due("exp", 1))

            def first_idx(before, ph, both_ends):
                v.wait_ge(before["yfree"], before.due("yfree", G + 1))
                ins = v.tensor_copy(ibS[:, :], srcI[:, 0:U])
                if both_ends:
                    ins = v.tensor_copy(ibD[:, :], dstI[:, 0:U])
                c(ins)
                v.sem_inc(ph["taken"], 1)
                v.sem_inc(ph["idx"], 1)

            def out_idx(ph, g):
                v.wait_ge(ph["yfree"], ph.due("yfree", g + 1))
                v.tensor_copy(ibO[:, :], cols(idxD, g)).then_inc(ph["oidx"], 1)

            def select(ph, g):
                v.wait_ge(ph["bcast"], ph.due("bcast", g + 1))
                tt(sel[:, :, :], bank(4), over_cols(cols(keyD, g)), ALU.is_equal).then_inc(ph["sel"], 1)

            def each(t, g):
                return [t[:, ds(U * g + u, 1), :].rearrange("p a c -> p (a c)") for u in range(U)]

            def part(t):
                return [t[:, u, 0:C] for u in range(U)]

            first_idx(l0, l1, True)
            c = Chain(v, l1["chain"], 8)
            with v.Fori(0, G) as g:
                c.step(g)
                S, D = RS[:, ds(U * g, U), :], RD[:, ds(U * g, U), :]
                diag(dgA, cols(keyD, g)).then_inc(l1["diag"], 1)
                v.wait_ge(l1["gathered_s"], l1.due("gathered_s", 16 * U * g + 16 * U))
                v.wait_ge(l1["gathered_d"], l1.due("gathered_d", 16 * U * g + 16 * U))
                next_idx(l1, g, True)
                tt(S, S, gA[:, :, 0:C], ALU.add)
                c(tt(D, D, gB[:, :, 0:C], ALU.add))
                v.sem_inc(l1["taken"], 1)
                tt(S, S, over_rows(bo_b[:, :]), ALU.add)
                c(tt(D, D, over_rows(bo_b[:, :]), ALU.add))
                tiles = each(RS, g) + each(RD, g)
                v.sem_inc(s_vhold, 1)
                stats(c, tiles, st, mv, l1, "var", 2 * U)
                normalize(c, l1, "sd", g, part(wA) + part(wB), tiles, mv, sd, rs, 2 * U).then_inc(l1["xn"], 1)
                v.wait_ge(l1["xn"], l1.due("xn", g + 1))
                c(stt(out=S, in0=wA[:, :, :], scalar=0.0, in1=S, op0=ALU.max, op1=ALU.add))
                c(tt(S, S, over_rows(bn2_b[:, :]), ALU.add))
                select(l1, g)
                out_idx(l1, g)
                c.end()
            c = Chain(v, wx["chain2"], 1)
            c.step(0)
            first_idx(l1, l2, False)
            v.memset(msg[:, :, :], 1.0)
            c = Chain(v, l2["chain"], 7)
            with v.Fori(0, G) as g:
                c.step(g)
                S = RS[:, ds(U * g, U), :]
                diag(dgA, cols(keyD, g)).then_inc(l2["diag"], 1)
                v.wait_ge(l2["gathered_s"], l2.due("gathered_s", 16 * U * g + 16 * U))
                next_idx(l2, g, False)
                tt(wA[:, :, :], RV[:, ds(U * g, U), :], gA[:, :, 0:C], ALU.add).then_inc(l2["u"], 1)
                v.wait_ge(l2["u"], l2.due("u", g + 1))
                v.sem_inc(l2["taken"], 1)
                select(l2, g)
                v.wait_ge(l2["x2"], l2.due("x2", g + 1))
                c(tt(S, bank(1), S, ALU.add))
                v.sem_inc(s_vhold, 1)
                stats(c, each(RS, g), st, mv, l2, "var", U)
                c(normalize(c, l2, "sd", g, part(wB), each(RS, g), mv, sd, rs, U))
                c(ts(RD[:, ds(U * g, U), :], wB[:, :, :], 0.0, None, ALU.max))
                tt(msg[:, :, 0:C], RD[:, ds(U * g, U), :], over_cols(cols(wexp, g), C), ALU.mult)
                v.tensor_copy(msg[:, :, C:C + 1].rearrange("p u a -> p (u a)"), cols(wexp, g)).then_inc(l2["msgs"], 1)
                out_idx(l2, g)
                c.end()
            c = Chain(v, wx["chain3"], 1)
            c.step(0)
            first_idx(l2, l3, False)
            c = Chain(v, l3["chain"], 17)

            def scale_of_sum(c, table_rows, dn_, nr_, rr_, ph, g):
                den = table_rows[:, :, C:C + 1].rearrange("p u a -> p (u a)")
                c(ts(dn_[:, :], den, 0.5, PROJ_EPS, ALU.max, ALU.mult))
                v.wait_ge(ph["norm"], ph.due("norm", g + 1))
                c(tt(dn_[:, :], nr_[:, :], dn_[:, :], ALU.add))
                c(v.reciprocal(rr_[:, :], dn_[:, :]))

            with v.Fori(0, G) as g:
                c.step(g)
                S = RS[:, ds(U * g, U), :]
                diag(dgA, cols(keyD, g)).then_inc(l3["diag"], 1)
                v.wait_ge(l3["gathered_s"], l3.due("gathered_s", 16 * U * g + 16 * U))
                next_idx(l3, g, False)
                c(tt(dgB[:, :, 0:C], gA[:, :, 0:C], gA[:, :, 0:C], ALU.mult))
                v.tensor_reduce(out=sq[:, :], in_=dgB[:, :, 0:C], axis=AX.X, op=ALU.add).then_inc(l3["sq"], 1)
                scale_of_sum(c, gA, dn, nr, rr, l3, g)
                h2 = each(RD, g)
                for u in range(U):
                    ins = stt(out=wA[:, u, :], in0=gA[:, u, 0:C], scalar=rr[:, u:u + 1], in1=h2[u],
                              op0=ALU.mult, op1=ALU.add)
                ins.then_inc(l3["comb"], 1)
                v.wait_ge(l3["comb"], l3.due("comb", g + 1))
                v.sem_inc(l3["taken"], 1)
                select(l3, g)
                v.wait_ge(l3["h2"], l3.due("h2", g + 1))
                stats(c, part(bank(2)), st, mv, l3, "var", U)
                c(normalize(c, l3, "sd", g, part(wB), part(bank(2)), mv, sd, rs, U))
                c(tt(wB[:, :, :], wB[:, :, :], over_rows(gamma_b[:, :]), ALU.mult))
                c(tt(wB[:, :, :], wB[:, :, :], over_rows(beta_b[:, :]), ALU.add))
                c(tt(S, S, wB[:, :, :], ALU.add))
                v.sem_inc(s_vhold, 1)
                stats(c, each(RS, g), st2, mv2, l3, "var2", U)
                c(normalize(c, l3, "sd2", g, part(wB), each(RS, g), mv2, sd2, rs2, U))
                ts(wB[:, :, :], wB[:, :, :], 0.0, None, ALU.max).then_inc(l3["h3"], 1)
                out_idx(l3, g)
                c.end()

            v.wait_ge(l3["yfree"], l3.due("yfree", G + 1))
            for k in range(2):
                v.memset(st16[k], 1.0)
            v.memset(dn4, 1.0).then_inc(dd["set"], 1)
            v.wait_ge(dd["set"], 1)

            def bn(g, tile0, tiles):
                for u in range(U):
                    ins = v.bn_stats(st16[g][:, tile0 + u, :], tiles[:, u, 0:C])
                return ins

            def dve_slot(g, now):
                par = now.residue % 2
                count = 0

                def c(ins=None):
                    nonlocal count
                    if ins is None:
                        v.sem_inc(dd["chain"], 1)
                    else:
                        ins.then_inc(dd["chain"], 1)
                        v.wait_ge(dd["chain"], now.number * 6 + (count + 1))
                    count += 1

                n0, nb, nc_, nd, nf = g(0), g(LB), g(LC), g(LD), g(LF)
                ins = None
                if n0 is not None:
                    v.wait_ge(dd["x1a"], n0.number + 1)
                    ins = bn(par, 0, B("x1", n0))
                if nb is not None:
                    v.wait_ge(dd["m1"], nb.number + 1)
                    v.wait_ge(dd["xbb"], nb.number + 1)
                    tt(B("x1", nb), bank(2), B("xb", nb), ALU.add).then_inc(dd["x2"], 1)
                    v.wait_ge(dd["x2"], nb.number + 1)
                    ins = bn(par, U, B("x1", nb))
                if nd is not None:
                    v.wait_ge(dd["x3"], nd.number + 1)
                    ins = bn(par, 3 * U, B("x1", nd))
                if nc_ is not None:
                    v.wait_ge(dd["h2p"], nc_.number + 1)
                    ins = bn(par, 2 * U, bank(5))
                c(ins)
                m, f = mv16[par], lambda j: st16[par][:, :, j]
                tt(m[:, 4, :], f(1), f(4), ALU.add)
                tt(m[:, 5, :], f(1), f(4), ALU.subtract)
                c(tt(m[:, 6, :], f(2), f(5), ALU.add))
                ts(m[:, 0, :], m[:, 4, :], 0.5, None, ALU.mult)
                c(stt(out=m[:, 5, :], in0=m[:, 5, :], scalar=0.25, in1=m[:, 5, :], op0=ALU.mult, op1=ALU.mult))
                stt(out=m[:, 1, :], in0=m[:, 6, :], scalar=1.0 / C, in1=m[:, 5, :], op0=ALU.mult, op1=ALU.add)\
                    .then_inc(dd["var"], 1)
                if nb is not None:
                    den = B("s2", nb)[:, :, C:C + 1].rearrange("p u a -> p (u a)")
                    ts(dn4[:, 0, :], den, 0.5, PROJ_EPS, ALU.max, ALU.mult)
                    cnt = B("s2", nb)[:, :, C + 1:C + 2].rearrange("p u a -> p (u a)")
                    ts(dn4[:, 1, :], cnt, 1.0, None, ALU.max)
                if nf is not None:
                    v.wait_ge(dd["o4"], nf.number + 1)
                    tt(B("o", nf), bank(7), B("o", nf), ALU.add).then_inc(dd["osb"], 1)
                v.wait_ge(dd["sd"], now.number + 1)
                c(v.reciprocal(m[:, 2, :], sd16[par][:, :]))
                if nb is not None:
                    v.wait_ge(dd["norm"], nb.number + 1)
                    tt(dn4[:, 0, :], nr4[nb.residue % 2][:, :], dn4[:, 0, :], ALU.add)
                c(stt(out=m[:, 3, :], in0=m[:, 0, :], scalar=-1.0, in1=m[:, 2, :], op0=ALU.mult, op1=ALU.mult))
                v.sem_inc(dd["rs"], 1)
                if nb is not None:
                    k = nb.residue
                    c(v.reciprocal(rr8[:, 2 * k:2 * k + 2, :], dn4[:, :, :]))
                else:
                    c()

                def norm(o, i, tile0):
                    for u in range(U):
                        t = tile0 + u
                        ins = ts(o[:, u, :], i[:, u, :], m[:, 0, t:t + 1], m[:, 2, t:t + 1], ALU.subtract, ALU.mult)
                    return ins

                if n0 is not None:
                    norm(B("xn1", n0), B("x1", n0), 0).then_inc(dd["xn1"], 1)
                if nd is not None:
                    norm(B("xn4", nd), B("x1", nd), 3 * U).then_inc(dd["xn4"], 1)
                if n0 is not None:
                    v.wait_ge(dd["xn1"], n0.number + 1)
                    stt(out=B("xb", n0), in0=B("xn1", n0), scalar=0.0, in1=B("x1", n0), op0=ALU.max, op1=ALU.add)\
                        .then_inc(dd["xb"], 1)
                if nd is not None:
                    if nd.from_number(4):
                        v.wait_ge(d_out[nd.residue % 4], nd.quarter * 16)
                    v.wait_ge(d_in3[nd.residue % 2], nd.half * 16 + 16)
                    for u in range(U):
                        ins = stt(out=B("o", nd)[:, u, :], in0=B("s3", nd)[:, u, :], scalar=rr8[:, 2 * nd.residue + 1, u:u + 1],
                                  in1=B("x1", nd)[:, u, :], op0=ALU.mult, op1=ALU.add)
                    ins.then_inc(dd["comb4"], 1)
                    v.wait_ge(dd["comb4"], nd.number + 1)
                if nb is not None:
                    v.wait_ge(dd["h2"], nb.number + 1)
                    for u in range(U):
                        ins = stt(out=B("h2", nb)[:, u, :], in0=B("s2", nb)[:, u, 0:C], scalar=rr8[:, 2 * k, u:u + 1],
                                  in1=B("h2", nb)[:, u, :], op0=ALU.mult, op1=ALU.add)
                    ins.then_inc(dd["comb"], 1)
                assert count == 6

            slots(v, dve_slot, NG - 1 + LF, 2)


_ORDER = ['x', 'src', 'dst', 'edge_weight', 'WqT', 'bq', 'WkT', 'bk', 'WvT', 'bv', 'Wd', 'bd', 'WoT', 'bo',
          'We1', 'be1', 'We2', 'be2', 'Wn1', 'bn1', 'Wn2', 'bn2', 'W1', 'b1', 'W2', 'b2', 'gamma', 'beta',
          'WoutT', 'b_out']
_FROM = {'WqT': ('L0_gnn_Wq', True), 'bq': ('L0_gnn_bq', False), 'WkT': ('L0_gnn_Wk', True),
         'bk': ('L0_gnn_bk', False), 'WvT': ('L0_gnn_Wv', True), 'bv': ('L0_gnn_bv', False),
         'Wd': ('L0_gnn_Wd', False), 'bd': ('L0_gnn_bd', False), 'WoT': ('L0_gnn_Wo', True),
         'bo': ('L0_gnn_bo', False), 'WoutT': ('L3_gnn_W_out', True), 'b_out': ('L3_gnn_b_out', False)}
_FROM.update({n: (f'L1_gnn_{n}', False) for n in ('We1', 'be1', 'We2', 'be2', 'Wn1', 'bn1', 'Wn2', 'bn2')})
_FROM.update({n: (f'L2_gnn_{n}', False) for n in ('W1', 'b1', 'W2', 'b2', 'gamma', 'beta')})


def kernel(**inputs):
    import numpy as _np
    import concourse.bacc as _bacc
    from concourse import mybir as _mybir
    from concourse.bass_utils import run_bass_kernel_spmd as _run

    nc = _bacc.Bacc("TRN2", target_bir_lowering=False, num_devices=1)
    arrays, args = {}, []
    for name in _ORDER:
        key, transposed = _FROM.get(name, (name, False))
        a = _np.asarray(inputs[key])
        a = _np.ascontiguousarray(a.T if transposed else a)
        arrays[f"in_{name}"] = a
        args.append(nc.dram_tensor(f"in_{name}", a.shape, _mybir.dt.from_np(a.dtype), kind="ExternalInput").ap())
    shape = tuple(arrays["in_x"].shape)
    out = nc.dram_tensor("out_x", shape, _mybir.dt.float32, kind="ExternalOutput").ap()
    build_gnn(nc, *args, out)
    r = _run(nc, [arrays], core_ids=[0])
    return r.results[0]["out_x"]
```

```python
import concourse.bass as bass
from concourse import mybir
from contextlib import ExitStack

P = 128
U = 4
LN_EPS = 1e-5
PROJ_EPS = 1e-9
FAR = 3.0e38
ABSENT = 2.0 ** 127


class Phase(dict):

    def __init__(self, sems):
        super().__init__(sems)
        self.start = {}

    def due(self, name, n):
        return n + self.start.get(name, 0)


class Chain:

    def __init__(self, engine, sem, per):
        self.engine, self.sem, self.per, self.n, self.base = engine, sem, per, 0, 0

    def step(self, g):
        self.base, self.n = g * self.per, 0

    def __call__(self, ins):
        self.n += 1
        ins.then_inc(self.sem, 1)
        self.engine.wait_ge(self.sem, self.base + self.n)

    def end(self):
        assert self.n == self.per, f"chain of {self.n}, not {self.per}"


def build_gnn(nc, x, src, dst, edge_weight, WqT, bq, WkT, bk, WvT, bv, Wd, bd, WoT, bo,
              We1, be1, We2, be2, Wn1, bn1, Wn2, bn2, W1, b1, W2, b2, gamma, beta, WoutT, b_out, out):
    f32, bf16, i32 = mybir.dt.float32, mybir.dt.bfloat16, mybir.dt.int32
    ALU, ACT, AX = mybir.AluOpType, mybir.ActivationFunctionType, mybir.AxisListType
    ds = bass.ds

    N, C = x.shape
    E = src.shape[0]
    H = bd.shape[0]
    HD = C // H
    EP = max(p for p in range(1, P + 1) if E % p == 0 and (E // p) % U == 0)
    CH = E // EP
    G = CH // U
    TF = (N + P + P - 1) // P
    NT = TF * P
    ROWS = P * U
    NG = 2 * ((N + 2 * ROWS - 1) // (2 * ROWS))
    bases = [min(g * ROWS, N - ROWS) for g in range(NG)]
    assert all(b == g * ROWS for g, b in enumerate(bases[:-1]))
    SCALE = 1.0 / HD ** 0.5
    AW = C + 2
    ZR = next(z for z in range(1, TF + 1) if TF % z == 0 and TF // z <= CH // U)
    KV, QW = 2 * C + H, C + H

    ctx = ExitStack()
    with ctx:
        def sb(name, shape, dt=f32):
            return ctx.enter_context(nc.sbuf_tensor(name, shape, dt))

        def sem(name):
            return ctx.enter_context(nc.semaphore(name))

        S0 = nc.dram_tensor("sum_attention", (NT, C), f32, kind="Internal").ap()
        S1 = nc.dram_tensor("sum_edge_mlp", (NT, C), f32, kind="Internal").ap()
        S2 = nc.dram_tensor("sum_weighted", (NT, AW), f32, kind="Internal").ap()
        S3 = nc.dram_tensor("sum_mean", (NT, C), f32, kind="Internal").ap()

        ident = sb("ident", [P, P])
        ones = sb("ones", [P, P])
        ones16 = sb("ones16", [3, P], bf16)
        ltri = sb("ltri", [P, P])
        iota_f = sb("iota_f", [P, max(TF, P)])
        iota_p = sb("iota_p", [P, 1])
        trash = sb("trash", [P, 1])
        not_edge = sb("not_edge", [P, 1])
        eps = sb("eps", [P, 1])
        far_row = sb("far_row", [1, TF], bf16)
        zeros = sb("zeros", [P, AW])

        srcI = sb("srcI", [P, CH + U], i32)
        dstI = sb("dstI", [P, CH + U], i32)
        keyS = sb("keyS", [P, CH])
        keyD = sb("keyD", [P, CH])
        keyp = sb("keyp", [P, CH])
        keyf = sb("keyf", [P, CH])
        ew = sb("ew", [P, CH])
        rankD = sb("rankD", [P, CH])
        idxD = sb("idxD", [P, CH], i32)
        segmax = sb("segmax", [P, CH])
        wexp = sb("wexp", [P, CH])
        tmpc = sb("tmpc", [P, CH])
        keyI = idxD[:, :]
        pI, fI = tmpc[:, :].bitcast(i32), wexp[:, :].bitcast(i32)
        table = sb("table", [P, TF])
        scores = sb("scores", [P, CH, H])
        hmax = sb("hmax", [P, H])
        hall = sb("hall", [P, H])
        hsum = sb("hsum", [P, H])
        hrec = sb("hrec", [P, H])

        wkv = sb("wkv", [P, KV])
        wq = sb("wq", [P, QW])
        wo = sb("wo", [P, C])
        we1 = sb("we1", [P, 2, C])
        we2 = sb("we2", [P, C])
        wn1 = sb("wn1", [P, 2, C])
        wn2 = sb("wn2", [P, C])
        w1 = sb("w1", [P, C])
        w2 = sb("w2", [P, C])
        wout = sb("wout", [P, 2, C])
        wdb = sb("wdb", [P, H])
        b_e2, b_2, b_out3, b_n2 = [KV + QW + k * C for k in range(4)]
        ROWS_W = KV + QW + 4 * C
        parts3 = sb("bias_parts", [3, ROWS_W], bf16)
        part_of = sb("part_of", [P, 3])
        be1c = sb("be1c", [P, 1])
        bn1c = sb("bn1c", [P, 1])
        b1c = sb("b1c", [P, 1])
        bo_b = sb("bo_b", [P, C])
        gamma_b = sb("gamma_b", [P, C])
        beta_b = sb("beta_b", [P, C])

        RS = sb("rows_src", [P, CH, C])
        RD = sb("rows_dst", [P, CH, C])
        RV = sb("rows_val", [P, CH, C])

        gA = sb("gA", [P, U, AW])
        gB = sb("gB", [P, U, AW])
        ibS = sb("ibS", [P, U], i32)
        ibD = sb("ibD", [P, U], i32)
        ibO = sb("ibO", [P, U], i32)
        dgA = sb("dgA", [P, U, P])
        dgB = sb("dgB", [P, U, P])
        sel = sb("sel", [P, U, P])
        wA = sb("wA", [P, U, C])
        wB = sb("wB", [P, U, C])
        hTA = sb("hTA", [P, U, P])
        hTB = sb("hTB", [P, U, P])
        y = sb("y", [P, U, AW])
        msg = gB
        qsb = sb("qsb", [P, 2, QW])
        sct = sb("sct", [P, U, H])
        red = sb("red", [P, U, H])
        oh = sb("oh", [P, U, P])
        oh16 = sb("oh16", [P, U, P], bf16)
        ohv = sb("ohv", [P, 2, TF])
        ohb = sb("ohb", [P, 2, TF], bf16)
        st = sb("st", [P, 2 * U, 6])
        mv = sb("mv", [P, 2 * U, 6])
        sd = sb("sd", [P, 2 * U])
        rs = sb("rs", [P, 2 * U])
        st2 = sb("st2", [P, U, 6])
        mv2 = sb("mv2", [P, U, 6])
        sd2 = sb("sd2", [P, U])
        rs2 = sb("rs2", [P, U])
        rk = sb("rk", [P, U])
        fr = sb("fr", [P, U])
        ml = sb("ml", [P, U])
        sq = sb("sq", [P, U])
        nr = sb("nr", [P, U])
        dn = sb("dn", [P, U])
        rr = sb("rr", [P, U])

        pb = ctx.enter_context(nc.psum_tensor("pb", [P, 8, 512], f32))

        def bank(b):
            return pb[:, b, :].rearrange("p (u c) -> p u c", u=U)

        def over_rows(row):
            return row.unsqueeze(1).broadcast_to([P, U, C])

        def over_cols(col, n=P):
            return col.unsqueeze(2).broadcast_to([P, U, n])

        s_loaded = sem("loaded")
        s_pool_const = sem("pool_const")
        s_vec_const = sem("vec_const")
        s_pool_chain = sem("pool_chain")
        s_zero = [sem(f"zeroed{i}") for i in range(4)]
        s_hold = sem("pool_held")
        s_vhold = sem("vector_held")
        s_sphold = sem("sync_held")

        shared = {n: sem(n) for n in ("idx gathered_s gathered_d taken diag bcast sel msgs mT mTs y ysb scat yfree "
                                      "oidx var sd hid hids").split()}
        ended = dict.fromkeys(shared, 0)

        def phase_sems(ph, names, share=""):
            p = Phase({n: sem(f"{ph}_{n}") for n in names.split()})
            for n in share.split():
                p[n], p.start[n] = shared[n], ended[n]
                ended[n] += G + (n in ("idx", "taken", "yfree")) if not n.startswith("gathered") and n != "scat" else 16 * U * G
            return p

        p0 = phase_sems("p0", "idx gathered_s gathered_d taken diag bcast xn xT hT kvq copied prod var sd oh tab tabmax chain chain_a")
        sm = phase_sems("sm", "hmax allmax shifted exp hsum allsum chain")
        l0 = phase_sems("l0", "look looked chain", "diag bcast sel msgs mT mTs y ysb scat yfree oidx")
        wx = phase_sems("wx", "shifted exp chain chain2 chain3")
        l1 = phase_sems("l1", "xn xT hT en ens chain", "idx gathered_s gathered_d taken diag bcast sel hid hids "
                        "mT mTs y ysb scat yfree oidx var sd")
        l2 = phase_sems("l2", "u uT uTs x2 chain", "idx gathered_s taken diag bcast sel var sd msgs y ysb scat yfree "
                        "oidx")
        l3 = phase_sems("l3", "sq norm comb cT cTs h2 var2 sd2 h3 chain chain_a", "idx gathered_s taken diag bcast sel "
                        "hid hids var sd mT mTs y ysb scat yfree oidx")
        loads = []

        def load(dst, srcap):
            loads.append((dst, srcap))

        col = lambda v: v.rearrange("(p a) -> p a", a=1)
        load(srcI[:EP, 0:CH], src.rearrange("(p c) -> p c", p=EP))
        load(dstI[:EP, 0:CH], dst.rearrange("(p c) -> p c", p=EP))
        load(ew[:EP, :], edge_weight.rearrange("(p c) -> p c", p=EP))
        load(wkv[:, 0:C], WkT)
        load(wkv[:, C:2 * C], WvT)
        load(wq[:, 0:C], WqT)
        load(wo[:, :], WoT)
        for k in range(2):
            load(we1[:, k, :], We1[k * C:(k + 1) * C, :])
            load(wn1[:, k, :], Wn1[k * C:(k + 1) * C, :])
            load(wout[:, k, :], WoutT[k * C:(k + 1) * C, :])
        load(we2[:, :], We2)
        load(wn2[:, :], Wn2)
        load(w1[:, :], W1)
        load(w2[:, :], W2)
        rest = [t[0:3, :, :].rearrange("p c f -> p (c f)")[:, 0:ROWS_W] for t in (RS, RD, RV)]
        for at_, n, vec in ((0, C, bk), (C, C, bv), (2 * C, H, bd), (KV, C, bq), (b_e2, C, be2), (b_2, C, b2),
                            (b_out3, C, b_out), (b_n2, C, bn2)):
            load(rest[0][:, at_:at_ + n], vec.partition_broadcast(3))
        load(be1c[:, :], col(be1))
        load(bn1c[:, :], col(bn1))
        load(b1c[:, :], col(b1))
        for t, v in ((bo_b, bo), (gamma_b, gamma), (beta_b, beta), (wdb, Wd.rearrange("h a -> (h a)"))):
            load(t[:, :], v.partition_broadcast(P))
        NLOAD = 16 * len(loads)

        LB, LC, LD, LF = 2, 4, 6, 7
        R = 8
        TURNS = NG // R
        assert TURNS > 2
        D_COUNTS = dict(s2=8, x1=8, s3=8, xn1=2, n3=4, xn4=2, h2=2, hT1=2, hT2=2, hT4=2, u1=2, u2=2,
                        o=4, x=4, s0=4, s1=4, squares=1)
        rows = [t[:, :, :].rearrange("p c f -> p (c f)") for t in (RS, RD, RV)]
        cap = CH * C
        spot = 0

        def place(name, *shape):
            nonlocal spot
            w = 1
            for n in shape:
                w *= n
            if cap < 24 * U * C:
                t = sb(f"d_{name}", [P, *shape])
                return t[tuple([slice(None)] * (len(shape) + 1))]
            if spot // cap != (spot + w - 1) // cap:
                spot = (spot // cap + 1) * cap
            t = rows[spot // cap][:, spot % cap:spot % cap + w]
            spot += w
            return t if len(shape) == 1 else t.rearrange("p (a b) -> p a b", b=shape[1])

        bufs = {name: [place(f"{name}{k}", U, AW if name == "s2" else C) for k in range(count)]
                for name, count in D_COUNTS.items()}
        st16 = [place(f"st16_{k}", 4 * U, 6) for k in range(2)]
        mv16 = [place(f"mv16_{k}", 7, 4 * U) for k in range(2)]
        sd16 = [place(f"sd16_{k}", 4 * U) for k in range(2)]
        sq4 = [place(f"sq4_{k}", U) for k in range(2)]
        nr4 = [place(f"nr4_{k}", U) for k in range(2)]
        dn4 = place("dn4", 2, U)
        rr8 = place("rr8", 2 * R, U)
        dd = phase_sems("d", "x1a var sd rs xn1 t1 h1 hid1 u1 m1 x2 sq norm h2 comb cT cTs hid2 u2 h2p n3 x3 "
                        "xn4 t4 h4 o4 osb chain pchain pchain2 pchain3 pchain4 comb4 set")
        d_in = [sem(f"d_in{k}") for k in range(4)]
        d_in3 = [sem(f"d_in3{k}") for k in range(R)]
        d_out = [sem(f"d_out{k}") for k in range(4)]

        class Group:

            def __init__(self, number, residue, quarter, turn):
                self.number, self.residue, self.quarter, self.turn = number, residue, quarter, turn

            def from_number(self, least):
                return not isinstance(self.number, int) or self.number >= least

        def B(name, n):
            return bufs[name][n.residue % D_COUNTS[name]]

        def slots(engine, slot, last, first=1):
            def straight(s):
                def g(lag):
                    n = s - lag
                    return Group(n, n % R, n // 4, n // R) if 0 <= n < NG else None
                return g

            for s in range(first * R):
                slot(straight(s), Group(s, s % R, s // 4, s // R))
            with engine.Fori(first, TURNS) as i:
                for j in range(R):
                    def g(lag, j=j):
                        return Group(i * R + (j - lag), (j - lag) % R, i * (R // 4) + (j - lag) // 4,
                                     i + (j - lag) // R)
                    slot(g, g(0))
            for s in range(TURNS * R, last + 1):
                slot(straight(s), Group(s, s % R, s // 4, s // R))

        def loads_due(n):
            return n.quarter * 64 + 64

        def skewed(engine, step):
            step(None, 0)
            with engine.Fori(0, G - 1) as g:
                step(g, g + 1)
            step(G - 1, None)

        block = ctx.enter_context(nc.Block())

        def rows_of(t, base):
            return t[ds(base, ROWS), :].rearrange("(p u) c -> p u c", u=U)

        @block.sync
        def _(sp):
            def hold(s, v):
                sp.wait_ge(s, v)
                sp.sem_inc(s_sphold, 1)

            sp.wait_ge(s_vec_const, 1)
            for d, s in loads:
                sp.dma_start(d, s, allow_slow_non_contiguous=True).then_inc(s_loaded, 16)
            for first, pair in ((1, ((0, S0, C), (1, S1, C))), (G - TF // ZR + 1, ((2, S2, AW), (3, S3, C)))):
                with sp.Fori(0, TF // ZR) as r:
                    hold(p0["diag"], p0.due("diag", r + first))
                    for k, t, w in pair:
                        sp.dma_start(t.rearrange("(p r) c -> p r c", p=P)[:, ds(r * ZR, ZR), :],
                                     zeros[:, 0:w].unsqueeze(1).broadcast_to([P, ZR, w])).then_inc(s_zero[k], 16)
            sp.wait_ge(l3["yfree"], l3.due("yfree", G + 1))

            def base_of(n):
                return bases[n.number] if isinstance(n.number, int) else n.number * ROWS

            def fetch(n):
                for name, t in (("x", x), ("s0", S0), ("s1", S1), ("s2", S2)):
                    sp.dma_start(B(name, n), rows_of(t, base_of(n))).then_inc(d_in[n.residue % 4], 16)

            def store(n):
                hold(dd["osb"], n.number + 1)
                if isinstance(n.number, int) and n.number == NG - 1:
                    for k in range(4):
                        sp.wait_ge(d_out[k], 16 * len(range(k, NG - 1, 4)))
                sp.dma_start(rows_of(out, base_of(n)), B("o", n)).then_inc(d_out[n.residue % 4], 16)

            def sp_slot(g, now):
                if (n := g(0)) is not None:
                    if n.from_number(4):
                        hold(dd["x1a"], n.number - 3)
                        hold(dd["hid1"], n.number - 3)
                    if n.from_number(8):
                        hold(dd["comb"], n.number - 7)
                    fetch(n)
                if (n := g(LD - 2)) is not None:
                    if n.from_number(8):
                        hold(dd["comb4"], n.number - 7)
                    sp.dma_start(B("s3", n), rows_of(S3, base_of(n))).then_inc(d_in3[n.residue], 16)
                if (n := g(SL)) is not None:
                    store(n)

            SL = LF + 3
            slots(sp, sp_slot, NG - 1 + SL, 2)
            for k in range(4):
                sp.wait_ge(d_out[k], 16 * len(range(k, NG, 4)))

        def at(c):
            return bass.IndirectOffsetOnAxis(ap=c, axis=0)

        @block.gpsimd
        def _(pool):
            def hold(s, v):
                pool.wait_ge(s, v)
                pool.sem_inc(s_hold, 1)

            pool.memset(ident[:, :], 1.0)
            pool.memset(ltri[:, :], 1.0)
            pool.memset(ones[:, :], 1.0).then_inc(s_pool_chain, 1)
            pool.wait_ge(s_pool_chain, 1)
            pool.affine_select(out=ident[:, :], in_=ident[:, :], compare_op=ALU.is_equal, fill=0.0, base=0,
                               pattern=[[-1, P]], channel_multiplier=1)
            pool.affine_select(out=ltri[:, :], in_=ltri[:, :], compare_op=ALU.is_gt, fill=0.0, base=0,
                               pattern=[[-1, P]], channel_multiplier=1)
            pool.iota(iota_f[:, :], pattern=[[1, max(TF, P)]], base=0, channel_multiplier=0,
                      allow_small_or_imprecise_dtypes=True)
            pool.iota(iota_p[:, :], pattern=[[0, 1]], base=0, channel_multiplier=1,
                      allow_small_or_imprecise_dtypes=True)
            pool.iota(trash[:, :], pattern=[[0, 1]], base=N, channel_multiplier=1,
                      allow_small_or_imprecise_dtypes=True).then_inc(s_pool_const, 1)

            def gather(s, buf, width, table_ap, idx, us=range(U)):
                for u in us:
                    pool.indirect_dma_start(out=buf[:, u, 0:width], out_offset=None, in_=table_ap,
                                            in_offset=at(idx[:, u:u + 1])).then_inc(s, 16)

            def scatter(ph, g, table_ap, width, idx):
                hold(ph["ysb"], ph.due("ysb", g + 1))
                hold(ph["oidx"], ph.due("oidx", g + 1))
                for u in range(U):
                    pool.indirect_dma_start(out=table_ap, out_offset=at(idx[:, u:u + 1]), in_=y[:, u, 0:width],
                                            in_offset=None, compute_op=ALU.add).then_inc(ph["scat"], 16)
                    hold(ph["scat"], ph.due("scat", 16 * U * g + 16 * (u + 1)))
                pool.sem_inc(ph["yfree"], 1)

            def may_gather(ph, g):
                hold(ph["taken"], ph.due("taken", g + 1))
                hold(ph["idx"], ph.due("idx", g + 1))

            with pool.Fori(0, G) as g:
                hold(p0["taken"], p0.due("taken", g + 1))
                hold(p0["idx"], p0.due("idx", g + 1))
                gather(p0["gathered_s"], gA, C, x, ibS)
                gather(p0["gathered_d"], gB, C, x, ibD)
            pool.wait_ge(sm["hmax"], sm.due("hmax", 1))
            pool.partition_all_reduce(hall[:, :], hmax[:, :], P, bass.bass_isa.ReduceOp.max).then_inc(sm["allmax"], 1)
            pool.wait_ge(sm["hsum"], sm.due("hsum", 1))
            pool.partition_all_reduce(hall[:, :], hsum[:, :], P, bass.bass_isa.ReduceOp.add).then_inc(sm["allsum"], 1)
            pool.sem_inc(l0["yfree"], 1)
            hold(s_zero[0], 16 * (TF // ZR))
            with pool.Fori(0, G) as g:
                scatter(l0, g, S0, C, ibO)
            def gather1(us=range(U)):
                gather(l1["gathered_s"], gA, C, S0, ibS, us)
                gather(l1["gathered_d"], gB, C, S0, ibD, us)

            def gather2(us=range(U)):
                gather(l2["gathered_s"], gA, C, S1, ibS, us)

            def gather3(us=range(U)):
                gather(l3["gathered_s"], gA, AW, S2, ibS, us)

            for ph, zero, rows_in, target, width in ((l1, s_zero[1], gather1, S1, C), (l2, s_zero[2], gather2, S2, AW),
                                                     (l3, s_zero[3], gather3, S3, C)):
                pool.sem_inc(ph["yfree"], 1)
                hold(zero, 16 * (TF // ZR))
                for g in range(2):
                    may_gather(ph, g)
                    rows_in()
                with pool.Fori(0, G - 2) as g:
                    may_gather(ph, g + 2)
                    rows_in()
                    scatter(ph, g, target, width, ibO)
                for g in (G - 2, G - 1):
                    scatter(ph, g, target, width, ibO)

            def attend(n):
                pool.wait_ge(d_in[n.residue % 4], loads_due(n))
                pool.tensor_tensor(B("x1", n), B("x", n), B("s0", n), ALU.add).then_inc(dd["pchain"], 1)
                pool.wait_ge(dd["pchain"], n.number + 1)
                pool.tensor_tensor(B("x1", n), B("x1", n), over_rows(bo_b[:, :]), ALU.add).then_inc(dd["x1a"], 1)

            def pool_slot(g, now):
                if (n := g(-1)) is not None:
                    if n.from_number(8):
                        pool.wait_ge(dd["xn4"], n.number - 7)
                        pool.sem_inc(s_hold, 1)
                        pool.wait_ge(dd["comb4"], n.number - 7)
                        pool.sem_inc(s_hold, 1)
                    attend(n)
                if (n := g(LD)) is not None:
                    pool.wait_ge(dd["comb"], n.number + 1)
                    pool.sem_inc(s_hold, 1)
                    pool.wait_ge(d_in3[n.residue], n.turn * 16 + 16)
                    pool.tensor_tensor(B("s3", n), B("s3", n), over_cols(rr8[:, 2 * n.residue + 1, :], C), ALU.mult)\
                        .then_inc(dd["pchain4"], 1)
                    if n.from_number(4):
                        pool.wait_ge(d_out[n.residue % 4], n.quarter * 16)
                        pool.sem_inc(s_hold, 1)
                    pool.wait_ge(dd["pchain4"], n.number + 1)
                    pool.tensor_tensor(B("o", n), B("s3", n), B("x1", n), ALU.add).then_inc(dd["comb4"], 1)
                if (n := g(LC)) is not None:
                    pool.wait_ge(dd["n3"], n.number + 1)
                    pool.tensor_tensor(B("n3", n), B("n3", n), over_rows(gamma_b[:, :]), ALU.mult)\
                        .then_inc(dd["pchain2"], 1)
                    pool.wait_ge(dd["pchain2"], n.number + 1)
                    pool.tensor_tensor(B("n3", n), B("n3", n), over_rows(beta_b[:, :]), ALU.add)\
                        .then_inc(dd["pchain3"], 1)
                    pool.wait_ge(dd["pchain3"], n.number + 1)
                    pool.tensor_tensor(B("x1", n), B("x1", n), B("n3", n), ALU.add).then_inc(dd["x3"], 1)

            attend(Group(0, 0, 0, 0))
            slots(pool, pool_slot, NG - 1 + LD, 2)

        @block.scalar
        def _(act):
            def relu(o, i, bias=0.0):
                return act.activation(o, i, ACT.Relu, bias=bias)

            def cp(o, i):
                return act.activation(o, i, ACT.Copy)

            def root(o, i):
                return act.activation(o, i, ACT.Sqrt, bias=eps[:, 0:1])

            def sd_step(ph, want, done, g, o, i):
                act.wait_ge(ph[want], ph.due(want, g + 1))
                root(o, i).then_inc(ph[done], 1)

            act.wait_ge(s_loaded, NLOAD)
            act.wait_ge(s_vec_const, 2)
            def act_p0(b, a):
                def copies(us):
                    for u in us:
                        act.wait_ge(p0["kvq"], p0.due("kvq", U * b + u + 1))
                        cp(RV[:, ds(U * b + u, 1), :].rearrange("p a c -> p (a c)"), pb[:, 2 + u % 2, C:2 * C])
                        if u >= 2:
                            act.wait_ge(p0["prod"], p0.due("prod", U * b + u - 1))
                        cp(qsb[:, u % 2, :], pb[:, 2 + u % 2, KV:KV + QW]).then_inc(p0["copied"], 1)

                if b is not None:
                    copies(range(1))
                if a is not None:
                    sd_step(p0, "var", "sd", a, sd[:, :], mv[:, :, 1])
                if b is not None:
                    copies(range(1, U))
                if a is not None:
                    act.wait_ge(p0["xT"], p0.due("xT", a + 1))
                    relu(hTA[:, :, :], bank(0))
                    relu(hTB[:, :, :], bank(1)).then_inc(p0["hT"], 1)

            skewed(act, act_p0)
            act.wait_ge(sm["shifted"], sm.due("shifted", 1))
            act.activation(scores[:, :, :], scores[:, :, :], ACT.Exp).then_inc(sm["exp"], 1)

            def copy_sums(ph, g, mid, src_bank, dst):
                act.wait_ge(ph[mid], ph.due(mid, g + 1))
                cp(dst, bank(src_bank)).then_inc(ph[mid + "s"], 1)

            def put_y(ph, g, b):
                act.wait_ge(ph["y"], ph.due("y", g + 1))
                act.wait_ge(ph["yfree"], ph.due("yfree", g + 1))
                cp(y[:, :, 0:C], bank(b)).then_inc(ph["ysb"], 1)

            with act.Fori(0, G) as g:
                copy_sums(l0, g, "mT", 0, hTA[:, :, :])
                put_y(l0, g, 1)
            act.wait_ge(wx["shifted"], wx.due("shifted", 1))
            act.activation(wexp[:, :], segmax[:, :], ACT.Exp).then_inc(wx["exp"], 1)
            def act_l1(b, a):
                if b is not None:
                    copy_sums(l1, b, "mT", 7, dgB[:, :, :])
                if a is not None:
                    sd_step(l1, "var", "sd", a, sd[:, :], mv[:, :, 1])
                    act.wait_ge(l1["xT"], l1.due("xT", a + 1))
                    relu(hTA[:, :, :], bank(0))
                    relu(hTB[:, :, :], bank(1)).then_inc(l1["hT"], 1)
                    act.wait_ge(l1["hid"], l1.due("hid", a + 1))
                    relu(hTB[:, :, :], bank(2), be1c[:, 0:1]).then_inc(l1["hids"], 1)
                    cp(RV[:, ds(U * a, U), :], bank(3))
                    copy_sums(l1, a, "en", 6, oh[:, :, :])
                if b is not None:
                    put_y(l1, b, 5)

            skewed(act, act_l1)

            def act_l2(b, a):
                if b is not None:
                    sd_step(l2, "var", "sd", b, sd[:, 0:U], mv[:, 0:U, 1])
                if a is not None:
                    act.wait_ge(l2["uT"], l2.due("uT", a + 1))
                    relu(hTA[:, :, :], bank(0), bn1c[:, 0:1]).then_inc(l2["uTs"], 1)
                if b is not None:
                    act.wait_ge(l2["y"], l2.due("y", b + 1))
                    act.wait_ge(l2["yfree"], l2.due("yfree", b + 1))
                    for k in range(2):
                        last = cp(y[:, 2 * k:2 * k + 2, :],
                                  pb[:, 2 + k, 0:2 * AW].rearrange("p (u c) -> p u c", u=2))
                    last.then_inc(l2["ysb"], 1)

            skewed(act, act_l2)

            def act_l3(b, a):
                if b is not None:
                    sd_step(l3, "var", "sd", b, sd[:, 0:U], mv[:, 0:U, 1])
                if a is not None:
                    act.wait_ge(l3["sq"], l3.due("sq", a + 1))
                    act.activation(nr[:, :], sq[:, :], ACT.Sqrt).then_inc(l3["norm"], 1)
                    copy_sums(l3, a, "cT", 0, hTA[:, :, :])
                    act.wait_ge(l3["hid"], l3.due("hid", a + 1))
                    relu(hTB[:, :, :], bank(1), b1c[:, 0:1]).then_inc(l3["hids"], 1)
                if b is not None:
                    sd_step(l3, "var2", "sd2", b, sd2[:, :], mv2[:, :, 1])
                    copy_sums(l3, b, "mT", 5, oh[:, :, :])
                    put_y(l3, b, 6)

            skewed(act, act_l3)

            def act_slot(g, now):
                if (n := g(LB)) is not None:
                    act.wait_ge(d_in[n.residue % 4], loads_due(n))
                    for u in range(U):
                        ins = act.activation(B("squares", n)[:, u, :], B("s2", n)[:, u, 0:C], ACT.Square,
                                             accum_out=sq4[n.residue % 2][:, u:u + 1])
                    ins.then_inc(dd["sq"], 1)
                    act.wait_ge(dd["sq"], n.number + 1)
                    act.activation(nr4[n.residue % 2][:, :], sq4[n.residue % 2][:, :], ACT.Sqrt).then_inc(dd["norm"], 1)
                par = now.residue % 2
                m = mv16[par]
                act.wait_ge(dd["var"], now.number + 1)
                root(sd16[par][:, :], m[:, 1, :]).then_inc(dd["sd"], 1)
                act.wait_ge(dd["rs"], now.number + 1)
                if (n := g(LB)) is not None:
                    for u in range(U):
                        t = U + u
                        ins = act.activation(B("h2", n)[:, u, :], B("x1", n)[:, u, :], ACT.Relu,
                                             scale=m[:, 2, t:t + 1], bias=m[:, 3, t:t + 1])
                    ins.then_inc(dd["h2"], 1)
                if (n := g(0)) is not None:
                    act.wait_ge(dd["t1"], n.number + 1)
                    relu(B("hT1", n), bank(0)).then_inc(dd["h1"], 1)
                if (n := g(LB + 1)) is not None:
                    act.wait_ge(dd["hid2"], n.number + 1)
                    relu(B("u2", n), bank(4), b1c[:, 0:1]).then_inc(dd["u2"], 1)
                if (n := g(LC)) is not None:
                    for u in range(U):
                        t = 2 * U + u
                        ins = act.activation(B("n3", n)[:, u, :], bank(5)[:, u, :], ACT.Identity,
                                             scale=m[:, 2, t:t + 1], bias=m[:, 3, t:t + 1])
                    ins.then_inc(dd["n3"], 1)
                if (n := g(LD)) is not None:
                    act.wait_ge(dd["t4"], n.number + 1)
                    relu(B("hT4", n), bank(6)).then_inc(dd["h4"], 1)
                if (n := g(0)) is not None:
                    act.wait_ge(dd["hid1"], n.number + 1)
                    relu(B("u1", n), bank(1), bn1c[:, 0:1]).then_inc(dd["u1"], 1)
                if (n := g(LB)) is not None:
                    act.wait_ge(dd["cT"], n.number + 1)
                    cp(B("hT2", n), bank(3)).then_inc(dd["cTs"], 1)

            slots(act, act_slot, NG - 1 + LF)

        @block.tensor
        def _(pe):
            def transposes(b, tiles, done):
                for u in range(U):
                    last = pe.transpose(bank(b)[:, u, :], tiles[:, u, 0:P], ident[:, :])
                last.then_inc(done, 1)

            def bcast(b, dg):
                return pe.matmul(pb[:, b, :], ones[:, :], dg[:, :, :], start=True, stop=True)

            def stationary(b, w, rhs):
                return pe.matmul(pb[:, b, :], w, rhs, start=True, stop=True)

            def bias_rows(b, at_):
                pe.matmul(pb[:, b, :], ones16[0:3, :], parts3[:, at_:at_ + C].unsqueeze(1).broadcast_to([3, U, C]),
                          start=True, stop=False, skip_group_check=True)

            def per_tile(b, lhs, rhs, bias=None):
                if bias is not None:
                    bias_rows(b, bias)
                for u in range(U):
                    last = pe.matmul(bank(b)[:, u, :], lhs[:, u, 0:P], rhs[:, u, :] if len(rhs.shape) == 3 else rhs,
                                     start=bias is None, stop=True, skip_group_check=True)
                return last

            pe.wait_ge(s_loaded, NLOAD)
            pe.wait_ge(s_pool_const, 1)
            pe.wait_ge(s_vec_const, 2)

            def kvq(g, u):
                b = 2 + u % 2
                if u >= 2:
                    pe.wait_ge(p0["copied"], p0.due("copied", U * g + u - 1))
                    pe.wait_ge(p0["prod"], p0.due("prod", U * g + u - 1))
                pe.matmul(pb[:, b, 0:KV + QW], ones16[0:3, :], parts3[:, 0:KV + QW], start=True, stop=False,
                          skip_group_check=True)
                pe.matmul(pb[:, b, 0:KV], hTB[:, u, :], wkv[:, :], start=False, stop=True, skip_group_check=True)
                pe.matmul(pb[:, b, KV:KV + QW], hTA[:, u, :], wq[:, :], start=False, stop=True,
                          skip_group_check=True).then_inc(p0["kvq"], 1)

            def tab(g, u):
                b = 6 + u % 2
                pe.wait_ge(p0["oh"], p0.due("oh", U * g + u + 1))
                if u >= 2:
                    pe.wait_ge(p0["tabmax"], p0.due("tabmax", U * g + u - 1))
                o = pb[:, b, 0:TF]
                pe.matmul(o, ones16[0:1, :], far_row[0:1, :], start=True, stop=False)
                pe.matmul(o, oh16[:, u, :], ohb[:, u % 2, :], start=False, stop=False)
                pe.matmul(o, oh[:, u, :], ohv[:, u % 2, :], start=False, stop=True).then_inc(p0["tab"], 1)

            def pe_p0(b, a):
                if b is not None:
                    pe.wait_ge(p0["diag"], p0.due("diag", b + 1))
                    bcast(4, dgA)
                    bcast(5, dgB).then_inc(p0["bcast"], 1)
                    pe.wait_ge(p0["hT"], p0.due("hT", b + 1))
                    for u in range(U):
                        kvq(b, u)
                if a is not None:
                    pe.wait_ge(p0["xn"], p0.due("xn", a + 1))
                    for k, t in ((0, wA), (1, wB)):
                        for u in range(U):
                            last = pe.transpose(bank(k)[:, u, :], t[:, u, :], ident[:, :])
                    last.then_inc(p0["xT"], 1)
                if b is not None:
                    for u in range(U):
                        tab(b, u)

            skewed(pe, pe_p0)

            def sums(ph, g, out_bank, rhs):
                pe.wait_ge(ph["mTs"], ph.due("mTs", g + 1))
                per_tile(out_bank, hTA, rhs).then_inc(ph["y"], 1)

            with pe.Fori(0, G) as g:
                pe.wait_ge(l0["diag"], l0.due("diag", g + 1))
                bcast(4, dgA)
                bcast(5, dgB).then_inc(l0["bcast"], 1)
                pe.wait_ge(l0["sel"], l0.due("sel", g + 1))
                for u in range(U):
                    if u >= 2:
                        pe.wait_ge(l0["looked"], l0.due("looked", U * g + u - 1))
                    pe.matmul(pb[:, 6 + u % 2, 0:TF], oh[:, u, :], table[:, :], start=True, stop=True)\
                      .then_inc(l0["look"], 1)
                pe.wait_ge(l0["msgs"], l0.due("msgs", g + 1))
                per_tile(0, wA, sel).then_inc(l0["mT"], 1)
                sums(l0, g, 1, wo[:, :])

            def select(ph, g, b):
                pe.wait_ge(ph["diag"], ph.due("diag", g + 1))
                bcast(b, dgA).then_inc(ph["bcast"], 1)

            def sums_of(ph, g, out_bank, lhs, rhs):
                pe.wait_ge(ph["mTs"], ph.due("mTs", g + 1))
                pe.wait_ge(ph["ysb"], ph.due("ysb", g))
                per_tile(out_bank, lhs, rhs).then_inc(ph["y"], 1)

            def pe_l1(b, a):
                if b is not None:
                    select(l1, b, 4)
                    pe.wait_ge(l1["ens"], l1.due("ens", b + 1))
                    pe.wait_ge(l1["sel"], l1.due("sel", b + 1))
                    per_tile(7, oh, sel).then_inc(l1["mT"], 1)
                if a is not None:
                    pe.wait_ge(l1["xn"], l1.due("xn", a + 1))
                    for k, t in ((0, wA), (1, wB)):
                        for u in range(U):
                            last = pe.transpose(bank(k)[:, u, :], t[:, u, :], ident[:, :])
                    last.then_inc(l1["xT"], 1)
                if b is not None:
                    sums_of(l1, b, 5, dgB, wn1[:, 1, :])
                if a is not None:
                    pe.wait_ge(l1["hT"], l1.due("hT", a + 1))
                    pe.matmul(pb[:, 2, :], we1[:, 0, :], hTA[:, :, :], start=True, stop=False)
                    pe.matmul(pb[:, 2, :], we1[:, 1, :], hTB[:, :, :], start=False, stop=True)
                    per_tile(3, hTA, wn1[:, 0, :]).then_inc(l1["hid"], 1)
                    pe.wait_ge(l1["hids"], l1.due("hids", a + 1))
                    per_tile(6, hTB, we2[:, :], b_e2).then_inc(l1["en"], 1)

            skewed(pe, pe_l1)

            def pe_l2(b, a):
                if b is not None:
                    select(l2, b, 4)
                if a is not None:
                    pe.wait_ge(l2["u"], l2.due("u", a + 1))
                    transposes(0, wA, l2["uT"])
                    pe.wait_ge(l2["uTs"], l2.due("uTs", a + 1))
                    per_tile(1, hTA, wn2[:, :], b_n2).then_inc(l2["x2"], 1)
                if b is not None:
                    pe.wait_ge(l2["sel"], l2.due("sel", b + 1))
                    pe.wait_ge(l2["msgs"], l2.due("msgs", b + 1))
                    pe.wait_ge(l2["ysb"], l2.due("ysb", b))
                    for u in range(U):
                        last = pe.matmul(pb[:, 2 + u // 2, AW * (u % 2):AW * (u % 2) + AW], sel[:, u, :], msg[:, u, :],
                                         start=True, stop=True, skip_group_check=True)
                    last.then_inc(l2["y"], 1)

            skewed(pe, pe_l2)

            def pe_l3(b, a):
                if b is not None:
                    select(l3, b, 4)
                if a is not None:
                    pe.wait_ge(l3["comb"], l3.due("comb", a + 1))
                    transposes(0, wA, l3["cT"])
                    pe.wait_ge(l3["cTs"], l3.due("cTs", a + 1))
                    stationary(1, w1[:, :], hTA[:, :, :]).then_inc(l3["hid"], 1)
                    pe.wait_ge(l3["hids"], l3.due("hids", a + 1))
                    per_tile(2, hTB, w2[:, :], b_2).then_inc(l3["h2"], 1)
                if b is not None:
                    pe.wait_ge(l3["sel"], l3.due("sel", b + 1))
                    pe.wait_ge(l3["h3"], l3.due("h3", b + 1))
                    per_tile(5, wB, sel).then_inc(l3["mT"], 1)
                    sums_of(l3, b, 6, oh, wout[:, 1, :])

            skewed(pe, pe_l3)

            def tr(b, tiles):
                for u in range(U):
                    last = pe.transpose(bank(b)[:, u, :], tiles[:, u, :], ident[:, :])
                return last

            def pe_slot(g, now):
                if (n := g(LD + 1)) is not None:
                    pe.wait_ge(dd["h4"], n.number + 1)
                    if n.from_number(1):
                        pe.wait_ge(dd["osb"], n.number)
                    per_tile(7, B("hT4", n), wout[:, 0, :], b_out3).then_inc(dd["o4"], 1)
                if (n := g(LB + 1)) is not None:
                    pe.wait_ge(dd["cTs"], n.number + 1)
                    stationary(4, w1[:, :], B("hT2", n)).then_inc(dd["hid2"], 1)
                if (n := g(1)) is not None:
                    pe.wait_ge(dd["u1"], n.number + 1)
                    if n.from_number(1):
                        pe.wait_ge(dd["x2"], n.number)
                    bias_rows(2, b_n2)
                    for u in range(U):
                        pe.matmul(bank(2)[:, u, :], B("hT1", n)[:, u, :], ident[:, :], start=False, stop=False,
                                  skip_group_check=True)
                        last = pe.matmul(bank(2)[:, u, :], B("u1", n)[:, u, :], wn2[:, :], start=False, stop=True,
                                         skip_group_check=True)
                    last.then_inc(dd["m1"], 1)
                if (n := g(0)) is not None:
                    pe.wait_ge(dd["xn1"], n.number + 1)
                    tr(0, B("xn1", n)).then_inc(dd["t1"], 1)
                if (n := g(LD)) is not None:
                    pe.wait_ge(dd["xn4"], n.number + 1)
                    tr(6, B("xn4", n)).then_inc(dd["t4"], 1)
                if (n := g(0)) is not None:
                    pe.wait_ge(dd["h1"], n.number + 1)
                    pe.wait_ge(d_in[n.residue % 4], loads_due(n))
                    pe.matmul(pb[:, 1, :], wn1[:, 0, :], B("hT1", n), start=True, stop=False, skip_group_check=True)
                    for u in range(U):
                        last = pe.matmul(bank(1)[:, u, :], B("s1", n)[:, u, :], ident[:, :], start=False,
                                         stop=True, skip_group_check=True)
                    last.then_inc(dd["hid1"], 1)
                if (n := g(LB + 1)) is not None:
                    pe.wait_ge(dd["u2"], n.number + 1)
                    if n.from_number(1):
                        pe.wait_ge(dd["n3"], n.number)
                    per_tile(5, B("u2", n), w2[:, :], b_2).then_inc(dd["h2p"], 1)
                if (n := g(LB)) is not None:
                    pe.wait_ge(dd["comb"], n.number + 1)
                    tr(3, B("h2", n)).then_inc(dd["cT"], 1)

            slots(pe, pe_slot, NG + LD)

        @block.vector
        def _(v):
            tt, ts, stt = v.tensor_tensor, v.tensor_scalar, v.scalar_tensor_tensor

            def stats(chain, tiles, st_, mv_, ph, want, n):
                for t in range(n):
                    ins = v.bn_stats(st_[:, t, :], tiles[t])
                chain(ins)
                f = lambda j: st_[:, 0:n, j]
                tt(mv_[:, 0:n, 2], f(1), f(4), ALU.add)
                tt(mv_[:, 0:n, 3], f(1), f(4), ALU.subtract)
                chain(tt(mv_[:, 0:n, 4], f(2), f(5), ALU.add))
                ts(mv_[:, 0:n, 0], mv_[:, 0:n, 2], 0.5, None, ALU.mult)
                chain(stt(out=mv_[:, 0:n, 5], in0=mv_[:, 0:n, 3], scalar=0.25, in1=mv_[:, 0:n, 3],
                          op0=ALU.mult, op1=ALU.mult))
                stt(out=mv_[:, 0:n, 1], in0=mv_[:, 0:n, 4], scalar=1.0 / C, in1=mv_[:, 0:n, 5],
                    op0=ALU.mult, op1=ALU.add).then_inc(ph[want], 1)

            def normalize(chain, ph, done, g, outs, tiles, mv_, sd_, rs_, n):
                v.wait_ge(ph[done], ph.due(done, g + 1))
                chain(v.reciprocal(rs_[:, 0:n], sd_[:, 0:n]))
                for t in range(n):
                    ins = v.tensor_scalar(outs[t], tiles[t], mv_[:, t, 0:1], rs_[:, t:t + 1], ALU.subtract, ALU.mult)
                return ins


            v.memset(srcI[:, :], 0)
            v.memset(dstI[:, :], 0)
            v.memset(ew[:, :], 0.0)
            v.memset(rest[0], 0.0)
            v.memset(zeros[:, :], 0.0).then_inc(s_vec_const, 1)
            v.memset(ones16[:, :], 1.0)
            v.memset(far_row[:, :], -ABSENT)
            v.memset(table[:, :], -ABSENT)
            v.memset(eps[:, :], LN_EPS)
            setup = Chain(v, sem("vec_setup"), 21)
            setup.step(0)
            v.wait_ge(s_loaded, NLOAD)
            v.wait_ge(s_pool_const, 1)
            setup(ts(not_edge[:, :], iota_p[:, :], float(EP), None, ALU.is_ge))
            setup(tt(rr[:, 0:1], not_edge[:, :], trash[:, :], ALU.mult))
            setup(ts(keyS[:, :], srcI[:, 0:CH], rr[:, 0:1], None, ALU.add))
            setup(ts(keyD[:, :], dstI[:, 0:CH], rr[:, 0:1], None, ALU.add))
            setup(v.tensor_copy(keyI, keyD[:, :]))
            setup(ts(pI, keyI, P - 1, None, ALU.bitwise_and))
            setup(ts(fI, keyI, 7, None, ALU.arith_shift_right))
            setup(v.tensor_copy(keyp[:, :], pI))
            setup(v.tensor_copy(keyf[:, :], fI))
            setup(ts(wkv[:, 2 * C:KV], wdb[:, :], 1.0 / C, None, ALU.mult))
            setup(ts(wq[:, C:QW], wdb[:, :], -1.0 / C, None, ALU.mult))
            v.tensor_copy(ibS[:, :], srcI[:, 0:U])
            setup(v.tensor_copy(ibD[:, :], dstI[:, 0:U]))
            for k in range(3):
                ins = ts(part_of[:, k:k + 1], iota_p[:, :], float(k), None, ALU.is_equal)
            value, first, second = rest
            for t in (first, second):
                setup(v.tensor_copy(parts3[:, :], value))
                setup(v.tensor_copy(t, parts3[:, :]))
                setup(tt(value, value, t, ALU.subtract))
            setup(ts(first, first, part_of[0:3, 0:1], None, ALU.mult))
            setup(stt(out=first, in0=second, scalar=part_of[0:3, 1:2], in1=first, op0=ALU.mult, op1=ALU.add))
            setup(stt(out=parts3[:, :], in0=value, scalar=part_of[0:3, 2:3], in1=first, op0=ALU.mult, op1=ALU.add))
            setup.end()
            v.sem_inc(s_vec_const, 1)
            v.sem_inc(p0["taken"], 1)
            v.sem_inc(p0["idx"], 1)

            def cols(t, g):
                return t[:, ds(U * g, U)]

            def diag(dg, keys):
                return tt(dg[:, :, :], ident[:, :].unsqueeze(1).broadcast_to([P, U, P]), over_cols(keys), ALU.mult)

            def next_idx(ph, g, both_ends):
                ins = v.tensor_copy(ibS[:, :], srcI[:, ds(U * g + U, U)])
                if both_ends:
                    ins = v.tensor_copy(ibD[:, :], dstI[:, ds(U * g + U, U)])
                ins.then_inc(ph["idx"], 1)

            def each(t, g):
                return [t[:, ds(U * g + u, 1), :].rearrange("p a c -> p (a c)") for u in range(U)]

            def part(t):
                return [t[:, u, 0:C] for u in range(U)]

            c = Chain(v, p0["chain"], 6)
            ca = Chain(v, p0["chain_a"], 5)

            def table_max(g, u):
                v.wait_ge(p0["tab"], p0.due("tab", U * g + u + 1))
                if u > 0:
                    v.wait_ge(p0["tabmax"], p0.due("tabmax", U * g + u))
                tt(table[:, :], pb[:, 6 + u % 2, 0:TF], table[:, :], ALU.max).then_inc(p0["tabmax"], 1)

            def table_parts(g, u):
                cc = ds(U * g + u, 1)
                ts(ohv[:, u % 2, :], iota_f[:, 0:TF], keyf[:, cc], ml[:, u:u + 1], ALU.is_equal, ALU.mult)
                ts(ohb[:, u % 2, :], iota_f[:, 0:TF], keyf[:, cc], ABSENT, ALU.is_equal, ALU.mult)\
                    .then_inc(p0["oh"], 1)

            def products(g, u):
                b = 2 + u % 2
                v.wait_ge(p0["copied"], p0.due("copied", U * g + u + 1))
                tt(y[:, u, 0:C], pb[:, b, 0:C], qsb[:, u % 2, 0:C], ALU.mult)
                stt(out=sct[:, u, :], in0=pb[:, b, 2 * C:KV], scalar=ew[:, ds(U * g + u, 1)],
                    in1=qsb[:, u % 2, C:QW], op0=ALU.add, op1=ALU.add).then_inc(p0["prod"], 1)

            def dve_p0(b, a):
                if b is not None:
                    c.step(b)
                    diag(dgA, cols(keyD, b))
                    diag(dgB, cols(ew, b)).then_inc(p0["diag"], 1)
                if a is not None:
                    ca.step(a)
                    v.wait_ge(p0["gathered_s"], p0.due("gathered_s", 16 * U * a + 16 * U))
                    v.wait_ge(p0["gathered_d"], p0.due("gathered_d", 16 * U * a + 16 * U))
                    next_idx(p0, a, True)
                    v.tensor_copy(RS[:, ds(U * a, U), :], gA[:, :, 0:C])
                    ca(v.tensor_copy(RD[:, ds(U * a, U), :], gB[:, :, 0:C]))
                    v.sem_inc(p0["taken"], 1)
                    tiles = each(RS, a) + each(RD, a)
                    stats(ca, tiles, st, mv, p0, "var", 2 * U)
                if b is not None:
                    v.wait_ge(p0["bcast"], p0.due("bcast", b + 1))
                    c(tt(sel[:, :, :], bank(4), over_cols(cols(keyD, b)), ALU.not_equal))
                    stt(out=dgB[:, :, 0:C], in0=sel[:, :, :], scalar=-FAR, in1=bank(5), op0=ALU.mult, op1=ALU.add)
                    c(stt(out=dgA[:, :, :], in0=sel[:, :, :], scalar=0.0,
                          in1=ltri[:, :].unsqueeze(1).broadcast_to([P, U, P]), op0=ALU.is_equal, op1=ALU.mult))
                    products(b, 0)
                    products(b, 1)
                if a is not None:
                    normalize(ca, p0, "sd", a, part(wA) + part(wB), tiles, mv, sd, rs, 2 * U).then_inc(p0["xn"], 1)
                    ca.end()
                if b is not None:
                    products(b, 2)
                    v.tensor_reduce(out=ml[:, :], in_=dgB[:, :, 0:C], axis=AX.X, op=ALU.max)
                    c(v.tensor_reduce(out=rk[:, :], in_=dgA[:, :, :], axis=AX.X, op=ALU.add))
                    products(b, 3)
                    v.tensor_copy(cols(rankD, b), rk[:, :])
                    c(ts(fr[:, :], rk[:, :], 0.0, None, ALU.is_equal))
                    for u in range(U):
                        ins = ts(oh[:, u, :], iota_f[:, 0:P], keyp[:, ds(U * b + u, 1)], fr[:, u:u + 1],
                                 ALU.is_equal, ALU.mult)
                    c(ins)
                    v.tensor_copy(oh16[:, :, :], oh[:, :, :])
                    table_parts(b, 0)
                    table_parts(b, 1)
                    for u in range(U):
                        table_max(b, u)
                        if u + 2 < U:
                            table_parts(b, u + 2)
                    v.wait_ge(p0["prod"], p0.due("prod", U * b + U))
                    c(v.tensor_reduce(out=red[:, :, :], in_=y[:, :, 0:C].rearrange("p u (h d) -> p u h d", d=HD),
                                      axis=AX.X, op=ALU.add))
                    stt(out=scores[:, ds(U * b, U), :], in0=red[:, :, :], scalar=SCALE, in1=sct[:, :, :],
                        op0=ALU.mult, op1=ALU.add)
                    v.wait_ge(p0["tabmax"], p0.due("tabmax", U * b + U))
                    c.end()

            skewed(v, dve_p0)
            c = Chain(v, sm["chain"], 12)
            c.step(0)

            def indices(rank, key, t):
                c(ts(rank, rank, 1.0, None, ALU.min))
                c(ts(t, key, -1.0, trash[:, 0:1], ALU.mult, ALU.add))
                c(tt(t, t, rank, ALU.mult))
                c(tt(t, t, key, ALU.add))

            indices(rankD[:, :], keyD[:, :], tmpc[:, :])
            c(v.tensor_copy(idxD[:, :], tmpc[:, :]))
            c(ts(rr[:, 0:1], not_edge[:, :], -FAR, None, ALU.mult))
            c(ts(scores[:, :, :], scores[:, :, :], rr[:, 0:1], None, ALU.add))
            v.tensor_reduce(out=hmax[:, :], in_=scores[:, :, :].rearrange("p c h -> p h c"), axis=AX.X, op=ALU.max)\
                .then_inc(sm["hmax"], 1)
            over_edges = lambda t: t[:, :].unsqueeze(1).broadcast_to([P, CH, H])
            v.wait_ge(sm["allmax"], sm.due("allmax", 1))
            tt(scores[:, :, :], scores[:, :, :], over_edges(hall), ALU.subtract).then_inc(sm["shifted"], 1)
            v.wait_ge(sm["exp"], sm.due("exp", 1))
            v.tensor_reduce(out=hsum[:, :], in_=scores[:, :, :].rearrange("p c h -> p h c"), axis=AX.X, op=ALU.add)\
                .then_inc(sm["hsum"], 1)
            v.wait_ge(sm["allsum"], sm.due("allsum", 1))
            c(v.reciprocal(hrec[:, :], hall[:, :]))
            c(tt(scores[:, :, :], scores[:, :, :], over_edges(hrec), ALU.mult))

            c = Chain(v, l0["chain"], 6)
            with v.Fori(0, G) as g:
                c.step(g)
                diag(dgA, cols(keyS, g))
                diag(dgB, cols(keyp, g)).then_inc(l0["diag"], 1)
                v.wait_ge(l0["bcast"], l0.due("bcast", g + 1))
                tt(wA[:, :, :].rearrange("p u (h d) -> p (u h) d", d=HD),
                   RV[:, ds(U * g, U), :].rearrange("p u (h d) -> p (u h) d", d=HD),
                   scores[:, ds(U * g, U), :].rearrange("p u h -> p (u h)").unsqueeze(2).broadcast_to([P, U * H, HD]),
                   ALU.mult).then_inc(l0["msgs"], 1)
                ts(oh[:, :, :], bank(5), iota_p[:, 0:1], None, ALU.is_equal)
                ins = tt(sel[:, :, :], bank(4), over_cols(cols(keyS, g)), ALU.is_equal)
                ins.then_inc(l0["sel"], 1)
                v.wait_ge(l0["sel"], l0.due("sel", g + 1))
                c(tt(dgA[:, :, :], sel[:, :, :], ltri[:, :].unsqueeze(1).broadcast_to([P, U, P]), ALU.mult))
                c(v.tensor_reduce(out=rk[:, :], in_=dgA[:, :, :], axis=AX.X, op=ALU.add))
                for u in range(U):
                    v.wait_ge(l0["look"], l0.due("look", U * g + u + 1))
                    stt(out=ohv[:, u % 2, :], in0=iota_f[:, 0:TF], scalar=keyf[:, ds(U * g + u, 1)],
                        in1=pb[:, 6 + u % 2, 0:TF], op0=ALU.is_equal, op1=ALU.mult, accum_out=ml[:, u:u + 1])\
                        .then_inc(l0["looked"], 1)
                v.wait_ge(l0["looked"], l0.due("looked", U * g + U))
                v.tensor_copy(cols(segmax, g), ml[:, :])
                indices(rk[:, :], cols(keyS, g), fr[:, :])
                v.wait_ge(l0["yfree"], l0.due("yfree", g + 1))
                v.tensor_copy(ibO[:, :], fr[:, :]).then_inc(l0["oidx"], 1)
                c.end()
            c = Chain(v, wx["chain"], 1)
            c.step(0)
            tt(segmax[:, :], ew[:, :], segmax[:, :], ALU.subtract).then_inc(wx["shifted"], 1)
            v.wait_ge(wx["exp"], wx.due("exp", 1))

            def first_idx(before, ph, both_ends):
                v.wait_ge(before["yfree"], before.due("yfree", G + 1))
                ins = v.tensor_copy(ibS[:, :], srcI[:, 0:U])
                if both_ends:
                    ins = v.tensor_copy(ibD[:, :], dstI[:, 0:U])
                c(ins)
                v.sem_inc(ph["taken"], 1)
                v.sem_inc(ph["idx"], 1)

            def out_idx(ph, g):
                v.wait_ge(ph["yfree"], ph.due("yfree", g + 1))
                v.tensor_copy(ibO[:, :], cols(idxD, g)).then_inc(ph["oidx"], 1)

            def select(ph, g):
                v.wait_ge(ph["bcast"], ph.due("bcast", g + 1))
                tt(sel[:, :, :], bank(4), over_cols(cols(keyD, g)), ALU.is_equal).then_inc(ph["sel"], 1)

            first_idx(l0, l1, True)
            c = Chain(v, l1["chain"], 7)

            def dve_l1(b, a):
                if b is not None:
                    diag(dgA, cols(keyD, b)).then_inc(l1["diag"], 1)
                if a is not None:
                    c.step(a)
                    S, D = RS[:, ds(U * a, U), :], RD[:, ds(U * a, U), :]
                    v.wait_ge(l1["gathered_s"], l1.due("gathered_s", 16 * U * a + 16 * U))
                    v.wait_ge(l1["gathered_d"], l1.due("gathered_d", 16 * U * a + 16 * U))
                    next_idx(l1, a, True)
                    tt(S, S, gA[:, :, 0:C], ALU.add)
                    c(tt(D, D, gB[:, :, 0:C], ALU.add))
                    v.sem_inc(l1["taken"], 1)
                if b is not None:
                    select(l1, b)
                if a is not None:
                    tt(S, S, over_rows(bo_b[:, :]), ALU.add)
                    c(tt(D, D, over_rows(bo_b[:, :]), ALU.add))
                    tiles = each(RS, a) + each(RD, a)
                    v.sem_inc(s_vhold, 1)
                    stats(c, tiles, st, mv, l1, "var", 2 * U)
                    normalize(c, l1, "sd", a, part(wA) + part(wB), tiles, mv, sd, rs, 2 * U).then_inc(l1["xn"], 1)
                    v.wait_ge(l1["xn"], l1.due("xn", a + 1))
                    c(stt(out=S, in0=wA[:, :, :], scalar=0.0, in1=S, op0=ALU.max, op1=ALU.add))
                    c.end()
                if b is not None:
                    out_idx(l1, b)

            skewed(v, dve_l1)
            c = Chain(v, wx["chain2"], 1)
            c.step(0)
            first_idx(l1, l2, False)
            v.memset(msg[:, :, :], 1.0)
            c = Chain(v, l2["chain"], 7)

            def dve_l2(b, a):
                if b is not None:
                    c.step(b)
                    S = RS[:, ds(U * b, U), :]
                    diag(dgA, cols(keyD, b)).then_inc(l2["diag"], 1)
                    v.wait_ge(l2["x2"], l2.due("x2", b + 1))
                    c(tt(S, bank(1), S, ALU.add))
                    v.sem_inc(s_vhold, 1)
                    stats(c, each(RS, b), st, mv, l2, "var", U)
                if a is not None:
                    v.wait_ge(l2["gathered_s"], l2.due("gathered_s", 16 * U * a + 16 * U))
                    next_idx(l2, a, False)
                    tt(wA[:, :, :], RV[:, ds(U * a, U), :], gA[:, :, 0:C], ALU.add).then_inc(l2["u"], 1)
                    v.wait_ge(l2["u"], l2.due("u", a + 1))
                    v.sem_inc(l2["taken"], 1)
                if b is not None:
                    c(normalize(c, l2, "sd", b, part(wB), each(RS, b), mv, sd, rs, U))
                    c(ts(RD[:, ds(U * b, U), :], wB[:, :, :], 0.0, None, ALU.max))
                    v.wait_ge(l2["y"], l2.due("y", b))
                    select(l2, b)
                    tt(msg[:, :, 0:C], RD[:, ds(U * b, U), :], over_cols(cols(wexp, b), C), ALU.mult)
                    v.tensor_copy(msg[:, :, C:C + 1].rearrange("p u a -> p (u a)"), cols(wexp, b))\
                        .then_inc(l2["msgs"], 1)
                    out_idx(l2, b)
                    c.end()

            skewed(v, dve_l2)
            c = Chain(v, wx["chain3"], 1)
            c.step(0)
            first_idx(l2, l3, False)
            c = Chain(v, l3["chain"], 13)
            ca = Chain(v, l3["chain_a"], 4)

            def dve_l3(b, a):
                if b is not None:
                    c.step(b)
                    S = RS[:, ds(U * b, U), :]
                    diag(dgA, cols(keyD, b)).then_inc(l3["diag"], 1)
                    v.wait_ge(l3["h2"], l3.due("h2", b + 1))
                    stats(c, part(bank(2)), st, mv, l3, "var", U)
                if a is not None:
                    ca.step(a)
                    v.wait_ge(l3["gathered_s"], l3.due("gathered_s", 16 * U * a + 16 * U))
                    next_idx(l3, a, False)
                    ca(tt(dgB[:, :, 0:C], gA[:, :, 0:C], gA[:, :, 0:C], ALU.mult))
                    v.tensor_reduce(out=sq[:, :], in_=dgB[:, :, 0:C], axis=AX.X, op=ALU.add).then_inc(l3["sq"], 1)
                    den = gA[:, :, C:C + 1].rearrange("p u a -> p (u a)")
                    ca(ts(dn[:, :], den, 0.5, PROJ_EPS, ALU.max, ALU.mult))
                if b is not None:
                    v.wait_ge(l3["mT"], l3.due("mT", b))
                    c(normalize(c, l3, "sd", b, part(wB), part(bank(2)), mv, sd, rs, U))
                if a is not None:
                    v.wait_ge(l3["norm"], l3.due("norm", a + 1))
                    ca(tt(dn[:, :], nr[:, :], dn[:, :], ALU.add))
                    ca(v.reciprocal(rr[:, :], dn[:, :]))
                    h2 = each(RD, a)
                    for u in range(U):
                        ins = stt(out=wA[:, u, :], in0=gA[:, u, 0:C], scalar=rr[:, u:u + 1], in1=h2[u],
                                  op0=ALU.mult, op1=ALU.add)
                    ins.then_inc(l3["comb"], 1)
                    ca.end()
                if b is not None:
                    c(tt(wB[:, :, :], wB[:, :, :], over_rows(gamma_b[:, :]), ALU.mult))
                if a is not None:
                    v.wait_ge(l3["comb"], l3.due("comb", a + 1))
                    v.sem_inc(l3["taken"], 1)
                if b is not None:
                    c(tt(wB[:, :, :], wB[:, :, :], over_rows(beta_b[:, :]), ALU.add))
                    c(tt(S, S, wB[:, :, :], ALU.add))
                    v.sem_inc(s_vhold, 1)
                    stats(c, each(RS, b), st2, mv2, l3, "var2", U)
                    select(l3, b)
                    c(normalize(c, l3, "sd2", b, part(wB), each(RS, b), mv2, sd2, rs2, U))
                    ts(wB[:, :, :], wB[:, :, :], 0.0, None, ALU.max).then_inc(l3["h3"], 1)
                    out_idx(l3, b)
                    c.end()

            skewed(v, dve_l3)

            v.wait_ge(l3["yfree"], l3.due("yfree", G + 1))
            for k in range(2):
                v.memset(st16[k], 1.0)
            v.memset(dn4, 1.0).then_inc(dd["set"], 1)
            v.wait_ge(dd["set"], 1)

            def bn(g, tile0, tiles):
                for u in range(U):
                    ins = v.bn_stats(st16[g][:, tile0 + u, :], tiles[:, u, 0:C])
                return ins

            def dve_slot(g, now):
                par = now.residue % 2
                count = 0

                def c(ins=None):
                    nonlocal count
                    if ins is None:
                        v.sem_inc(dd["chain"], 1)
                    else:
                        ins.then_inc(dd["chain"], 1)
                        v.wait_ge(dd["chain"], now.number * 5 + (count + 1))
                    count += 1

                n0, nb, nc_, nd, nf = g(0), g(LB), g(LC), g(LD), g(LF)
                ins = None
                if n0 is not None:
                    v.wait_ge(dd["x1a"], n0.number + 1)
                    ins = bn(par, 0, B("x1", n0))
                if nb is not None:
                    v.wait_ge(dd["m1"], nb.number + 1)
                    tt(B("x1", nb), bank(2), B("x1", nb), ALU.add).then_inc(dd["x2"], 1)
                    v.wait_ge(dd["x2"], nb.number + 1)
                    ins = bn(par, U, B("x1", nb))
                if nd is not None:
                    v.wait_ge(dd["x3"], nd.number + 1)
                    ins = bn(par, 3 * U, B("x1", nd))
                if nc_ is not None:
                    v.wait_ge(dd["h2p"], nc_.number + 1)
                    ins = bn(par, 2 * U, bank(5))
                c(ins)
                m, f = mv16[par], lambda j: st16[par][:, :, j]
                tt(m[:, 4, :], f(1), f(4), ALU.add)
                tt(m[:, 5, :], f(1), f(4), ALU.subtract)
                c(tt(m[:, 6, :], f(2), f(5), ALU.add))
                ts(m[:, 0, :], m[:, 4, :], 0.5, None, ALU.mult)
                c(stt(out=m[:, 5, :], in0=m[:, 5, :], scalar=0.25, in1=m[:, 5, :], op0=ALU.mult, op1=ALU.mult))
                stt(out=m[:, 1, :], in0=m[:, 6, :], scalar=1.0 / C, in1=m[:, 5, :], op0=ALU.mult, op1=ALU.add)\
                    .then_inc(dd["var"], 1)
                if nb is not None:
                    den = B("s2", nb)[:, :, C:C + 1].rearrange("p u a -> p (u a)")
                    ts(dn4[:, 0, :], den, 0.5, PROJ_EPS, ALU.max, ALU.mult)
                    cnt = B("s2", nb)[:, :, C + 1:C + 2].rearrange("p u a -> p (u a)")
                    ts(dn4[:, 1, :], cnt, 1.0, None, ALU.max)
                if nf is not None:
                    v.wait_ge(dd["o4"], nf.number + 1)
                    v.wait_ge(dd["comb4"], nf.number + 1)
                    tt(B("o", nf), bank(7), B("o", nf), ALU.add).then_inc(dd["osb"], 1)
                v.wait_ge(dd["sd"], now.number + 1)
                c(v.reciprocal(m[:, 2, :], sd16[par][:, :]))
                if nb is not None:
                    v.wait_ge(dd["norm"], nb.number + 1)
                    tt(dn4[:, 0, :], nr4[nb.residue % 2][:, :], dn4[:, 0, :], ALU.add)
                stt(out=m[:, 3, :], in0=m[:, 0, :], scalar=-1.0, in1=m[:, 2, :], op0=ALU.mult, op1=ALU.mult)\
                    .then_inc(dd["rs"], 1)

                def norm(o, i, tile0):
                    for u in range(U):
                        t = tile0 + u
                        ins = ts(o[:, u, :], i[:, u, :], m[:, 0, t:t + 1], m[:, 2, t:t + 1], ALU.subtract, ALU.mult)
                    return ins

                if n0 is not None:
                    norm(B("xn1", n0), B("x1", n0), 0).then_inc(dd["xn1"], 1)
                if nd is not None:
                    norm(B("xn4", nd), B("x1", nd), 3 * U).then_inc(dd["xn4"], 1)
                v.wait_ge(dd["rs"], now.number + 1)
                if nb is not None:
                    k = nb.residue
                    c(v.reciprocal(rr8[:, 2 * k:2 * k + 2, :], dn4[:, :, :]))
                else:
                    c()
                if nb is not None:
                    v.wait_ge(dd["h2"], nb.number + 1)
                    for u in range(U):
                        ins = stt(out=B("h2", nb)[:, u, :], in0=B("s2", nb)[:, u, 0:C], scalar=rr8[:, 2 * k, u:u + 1],
                                  in1=B("h2", nb)[:, u, :], op0=ALU.mult, op1=ALU.add)
                    ins.then_inc(dd["comb"], 1)
                assert count == 5

            slots(v, dve_slot, NG - 1 + LF, 2)


_ORDER = ['x', 'src', 'dst', 'edge_weight', 'WqT', 'bq', 'WkT', 'bk', 'WvT', 'bv', 'Wd', 'bd', 'WoT', 'bo',
          'We1', 'be1', 'We2', 'be2', 'Wn1', 'bn1', 'Wn2', 'bn2', 'W1', 'b1', 'W2', 'b2', 'gamma', 'beta',
          'WoutT', 'b_out']
_FROM = {'WqT': ('L0_gnn_Wq', True), 'bq': ('L0_gnn_bq', False), 'WkT': ('L0_gnn_Wk', True),
         'bk': ('L0_gnn_bk', False), 'WvT': ('L0_gnn_Wv', True), 'bv': ('L0_gnn_bv', False),
         'Wd': ('L0_gnn_Wd', False), 'bd': ('L0_gnn_bd', False), 'WoT': ('L0_gnn_Wo', True),
         'bo': ('L0_gnn_bo', False), 'WoutT': ('L3_gnn_W_out', True), 'b_out': ('L3_gnn_b_out', False)}
_FROM.update({n: (f'L1_gnn_{n}', False) for n in ('We1', 'be1', 'We2', 'be2', 'Wn1', 'bn1', 'Wn2', 'bn2')})
_FROM.update({n: (f'L2_gnn_{n}', False) for n in ('W1', 'b1', 'W2', 'b2', 'gamma', 'beta')})


def kernel(**inputs):
    import numpy as _np
    import concourse.bacc as _bacc
    from concourse import mybir as _mybir
    from concourse.bass_utils import run_bass_kernel_spmd as _run

    nc = _bacc.Bacc("TRN2", target_bir_lowering=False, num_devices=1)
    arrays, args = {}, []
    for name in _ORDER:
        key, transposed = _FROM.get(name, (name, False))
        a = _np.asarray(inputs[key])
        a = _np.ascontiguousarray(a.T if transposed else a)
        arrays[f"in_{name}"] = a
        args.append(nc.dram_tensor(f"in_{name}", a.shape, _mybir.dt.from_np(a.dtype), kind="ExternalInput").ap())
    shape = tuple(arrays["in_x"].shape)
    out = nc.dram_tensor("out_x", shape, _mybir.dt.float32, kind="ExternalOutput").ap()
    build_gnn(nc, *args, out)
    r = _run(nc, [arrays], core_ids=[0])
    return r.results[0]["out_x"]
```
